# Optimizing a Trainium2 kernel written in Bass

```python
import numpy as np
import jax
import jax.numpy as jnp

def _softmax(x, axis=-1):
    return jax.nn.softmax(x, axis=axis)

def _gelu(x):
    return jax.nn.gelu(x, approximate=True)

def _silu(x):
    return jax.nn.silu(x)

def _sigmoid(x):
    return jax.nn.sigmoid(x)

def _layernorm(x, axis=-1, eps=1e-05):
    m = jnp.mean(x, axis=axis, keepdims=True)
    v = jnp.var(x, axis=axis, keepdims=True)
    return (x - m) / jnp.sqrt(v + eps)

def _scatter_add(tgt, idx, src, axis=0):
    return tgt.at[idx].add(src)

def _segment_sum(src, seg, n):
    return jax.ops.segment_sum(src, seg, n)
kernel_name = 'mk_adaln_d1_jaxref_r8_af735a'

def setup_inputs(seed: int=0):
    np.random.seed(seed)
    _w = jnp.asarray

    def _L0_attn_setup():
        import jax, jax.numpy as jnp
        import numpy as np
        from functools import partial
        LN_EPS = 1000000.0
        FEAT_EPS = 1e-06

        def _layernorm(x, gamma, beta):
            mu = jnp.mean(x, axis=-1, keepdims=True)
            var = jnp.var(x, axis=-1, keepdims=True)
            return gamma * (x - mu) / jnp.sqrt(var + LN_EPS) + beta

        def _phi(x, omega):
            m = omega.shape[0]
            proj = jnp.einsum('bhsd,md->bhsm', x, omega)
            z = proj - 0.5 * jnp.sum(x * x, axis=-1, keepdims=True)
            z = z - jnp.max(z, axis=-1, keepdims=True)
            return jnp.exp(z) / jnp.sqrt(jnp.asarray(m, x.dtype)) + FEAT_EPS

        def _forward(batch, Wq, Wk, Wv, Wo, omega, W1, b1, W2, b2, gamma, beta):
            B, S, D = batch.shape
            M, dh = omega.shape
            H = D // dh
            scale = dh ** (-0.25)

            def heads(W):
                return (batch @ W).reshape(B, S, H, dh).transpose(0, 2, 1, 3)
            q = heads(Wq) * scale
            k = heads(Wk) * scale
            v = heads(Wv)
            qp = _phi(q, omega)
            kp = _phi(k, omega)
            qs = qp.transpose(2, 0, 1, 3)
            ks = kp.transpose(2, 0, 1, 3)
            vs = v.transpose(2, 0, 1, 3)

            def step(carry, qkv):
                S_kv, s_k = carry
                qt, kt, vt = qkv
                S_kv = S_kv + kt[..., :, None] * vt[..., None, :]
                s_k = s_k + kt
                num = jnp.einsum('bhm,bhmd->bhd', qt, S_kv)
                den = jnp.einsum('bhm,bhm->bh', qt, s_k)
                return ((S_kv, s_k), num / (den[..., None] + FEAT_EPS))
            carry0 = (jnp.zeros((B, H, M, dh), batch.dtype), jnp.zeros((B, H, M), batch.dtype))
            _, outs = jax.lax.scan(step, carry0, (qs, ks, vs))
            attn = outs.transpose(1, 0, 2, 3).reshape(B, S, D) @ Wo
            h = _layernorm(batch + attn, gamma, beta)
            out = jnp.maximum(h @ W1 + b1, 0.0) @ W2 + b2
            return out
        key = jax.random.key(seed)
        ks = jax.random.split(key, 8)
        B, S, D, H, dh, M, DFF = (4, 128, 128, 16, 64, 128, 512)
        w = 0.02
        return {'batch': jax.random.normal(ks[0], (B, S, D), jnp.float32), 'Wq': jax.random.normal(ks[1], (D, D), jnp.float32) * w, 'Wk': jax.random.normal(ks[2], (D, D), jnp.float32) * w, 'Wv': jax.random.normal(ks[3], (D, D), jnp.float32) * w, 'Wo': jax.random.normal(ks[4], (D, D), jnp.float32) * w, 'omega': jax.random.normal(ks[5], (M, dh), jnp.float32), 'W1': jax.random.normal(ks[6], (D, DFF), jnp.float32) * w, 'b1': jnp.zeros((DFF,), jnp.float32), 'W2': jax.random.normal(ks[7], (DFF, D), jnp.float32) * w, 'b2': jnp.zeros((D,), jnp.float32), 'gamma': jnp.ones((D,), jnp.float32), 'beta': jnp.zeros((D,), jnp.float32)}
    _L0_attn_in = _L0_attn_setup()

    def _L0_ffn_setup():
        import jax, jax.numpy as jnp
        import numpy as np
        B, S, H = (2, 256, 128)
        E_ROUTED = 8
        TOP_K = 2
        I = 256
        key = jax.random.key(seed)
        ks = jax.random.split(key, 9)
        s = 0.02
        return {'x': jax.random.normal(ks[0], (B, S, H), dtype=jnp.float32), 'shared_gate': jax.random.normal(ks[1], (I, H), dtype=jnp.float32) * s, 'shared_up': jax.random.normal(ks[2], (I, H), dtype=jnp.float32) * s, 'shared_down': jax.random.normal(ks[3], (H, I), dtype=jnp.float32) * s, 'gate_w': jax.random.normal(ks[4], (E_ROUTED, H, I), dtype=jnp.float32) * s, 'up_w': jax.random.normal(ks[5], (E_ROUTED, H, I), dtype=jnp.float32) * s, 'down_w': jax.random.normal(ks[6], (E_ROUTED, I, H), dtype=jnp.float32) * s, 'router_w': jax.random.normal(ks[7], (E_ROUTED, H), dtype=jnp.float32) * s, 'routing_bias': jnp.zeros((E_ROUTED,), dtype=jnp.float32)}
    _L0_ffn_in = _L0_ffn_setup()
    _L0_c = _w((lambda *s: np.random.randn(*s).astype(np.float32) * 0.05)(2, 128))
    _L0_wmod = _w((lambda *s: np.random.randn(*s).astype(np.float32) * 0.05)(128, 6 * 128) * 128 ** (-0.5))
    _d = {'L0_attn_batch': _L0_attn_in['batch'], 'L0_attn_Wq': _L0_attn_in['Wq'], 'L0_attn_Wk': _L0_attn_in['Wk'], 'L0_attn_Wv': _L0_attn_in['Wv'], 'L0_attn_Wo': _L0_attn_in['Wo'], 'L0_attn_omega': _L0_attn_in['omega'], 'L0_attn_W1': _L0_attn_in['W1'], 'L0_attn_b1': _L0_attn_in['b1'], 'L0_attn_W2': _L0_attn_in['W2'], 'L0_attn_b2': _L0_attn_in['b2'], 'L0_attn_gamma': _L0_attn_in['gamma'], 'L0_attn_beta': _L0_attn_in['beta'], 'L0_ffn_shared_gate': _L0_ffn_in['shared_gate'], 'L0_ffn_shared_up': _L0_ffn_in['shared_up'], 'L0_ffn_shared_down': _L0_ffn_in['shared_down'], 'L0_ffn_gate_w': _L0_ffn_in['gate_w'], 'L0_ffn_up_w': _L0_ffn_in['up_w'], 'L0_ffn_down_w': _L0_ffn_in['down_w'], 'L0_ffn_router_w': _L0_ffn_in['router_w'], 'L0_ffn_routing_bias': _L0_ffn_in['routing_bias'], 'L0_c': _L0_c, 'L0_wmod': _L0_wmod}
    _x0 = _d['L0_attn_batch']
    _d['L0_attn_batch'] = jax.random.normal(jax.random.fold_in(jax.random.key(seed), 1), (2, 1024, 128), dtype=_x0.dtype)
    del _x0
    return _d

def reference(L0_attn_batch, L0_attn_Wq, L0_attn_Wk, L0_attn_Wv, L0_attn_Wo, L0_attn_omega, L0_attn_W1, L0_attn_b1, L0_attn_W2, L0_attn_b2, L0_attn_gamma, L0_attn_beta, L0_ffn_shared_gate, L0_ffn_shared_up, L0_ffn_shared_down, L0_ffn_gate_w, L0_ffn_up_w, L0_ffn_down_w, L0_ffn_router_w, L0_ffn_routing_bias, L0_c, L0_wmod):

    def _L0_attn_ref(batch, Wq, Wk, Wv, Wo, omega, W1, b1, W2, b2, gamma, beta):
        import jax, jax.numpy as jnp
        import numpy as np
        from functools import partial
        LN_EPS = 1000000.0
        FEAT_EPS = 1e-06

        def _layernorm(x, gamma, beta):
            mu = jnp.mean(x, axis=-1, keepdims=True)
            var = jnp.var(x, axis=-1, keepdims=True)
            return gamma * (x - mu) / jnp.sqrt(var + LN_EPS) + beta

        def _phi(x, omega):
            m = omega.shape[0]
            proj = jnp.einsum('bhsd,md->bhsm', x, omega)
            z = proj - 0.5 * jnp.sum(x * x, axis=-1, keepdims=True)
            z = z - jnp.max(z, axis=-1, keepdims=True)
            return jnp.exp(z) / jnp.sqrt(jnp.asarray(m, x.dtype)) + FEAT_EPS

        def _forward(batch, Wq, Wk, Wv, Wo, omega, W1, b1, W2, b2, gamma, beta):
            B, S, D = batch.shape
            M, dh = omega.shape
            H = D // dh
            scale = dh ** (-0.25)

            def heads(W):
                return (batch @ W).reshape(B, S, H, dh).transpose(0, 2, 1, 3)
            q = heads(Wq) * scale
            k = heads(Wk) * scale
            v = heads(Wv)
            qp = _phi(q, omega)
            kp = _phi(k, omega)
            qs = qp.transpose(2, 0, 1, 3)
            ks = kp.transpose(2, 0, 1, 3)
            vs = v.transpose(2, 0, 1, 3)

            def step(carry, qkv):
                S_kv, s_k = carry
                qt, kt, vt = qkv
                S_kv = S_kv + kt[..., :, None] * vt[..., None, :]
                s_k = s_k + kt
                num = jnp.einsum('bhm,bhmd->bhd', qt, S_kv)
                den = jnp.einsum('bhm,bhm->bh', qt, s_k)
                return ((S_kv, s_k), num / (den[..., None] + FEAT_EPS))
            carry0 = (jnp.zeros((B, H, M, dh), batch.dtype), jnp.zeros((B, H, M), batch.dtype))
            _, outs = jax.lax.scan(step, carry0, (qs, ks, vs))
            attn = outs.transpose(1, 0, 2, 3).reshape(B, S, D) @ Wo
            h = _layernorm(batch + attn, gamma, beta)
            out = jnp.maximum(h @ W1 + b1, 0.0) @ W2 + b2
            return out
        return _forward(batch, Wq, Wk, Wv, Wo, omega, W1, b1, W2, b2, gamma, beta)

    def _L0_ffn_ref(x, shared_gate, shared_up, shared_down, gate_w, up_w, down_w, router_w, routing_bias):
        import jax, jax.numpy as jnp
        import numpy as np
        B, S, H = (2, 256, 128)
        E_ROUTED = 8
        TOP_K = 2
        I = 256
        b, s, h = x.shape
        shared = jnp.einsum('bsi,hi->bsh', jax.nn.silu(jnp.einsum('bsh,ih->bsi', x, shared_gate)) * jnp.einsum('bsh,ih->bsi', x, shared_up), shared_down)
        logits = jnp.einsum('bsh,eh->bse', x, router_w) + routing_bias
        probs = jax.nn.sigmoid(logits)
        scores, indices = jax.lax.top_k(probs, TOP_K)
        scores = scores / jnp.sum(scores, axis=-1, keepdims=True)
        t = b * s
        xf = x.reshape(t, h)
        idx = indices.reshape(t, TOP_K)
        sc = scores.reshape(t, TOP_K)
        w = jnp.zeros((t, E_ROUTED), dtype=x.dtype)
        w = w.at[jnp.arange(t)[:, None], idx].add(sc)
        g = jax.nn.silu(jnp.einsum('th,ehi->tei', xf, gate_w))
        u = jnp.einsum('th,ehi->tei', xf, up_w)
        combined = jnp.einsum('tei,eih,te->th', g * u, down_w, w)
        return shared + combined.reshape(b, s, h)
    x = L0_attn_batch
    mod = (_silu(L0_c) @ L0_wmod).reshape(L0_c.shape[0], 6, 1, -1)
    sa, ca, ga, sb, cb, gb = (mod[:, 0], mod[:, 1], mod[:, 2], mod[:, 3], mod[:, 4], mod[:, 5])
    ga = (2 * (ga >= 0) - 1) * jnp.maximum(jnp.abs(ga), 0.25)
    gb = (2 * (gb >= 0) - 1) * jnp.maximum(jnp.abs(gb), 0.25)
    h = _layernorm(x, axis=-1) * (1 + ca) + sa
    x = x + ga * _L0_attn_ref(h, L0_attn_Wq, L0_attn_Wk, L0_attn_Wv, L0_attn_Wo, L0_attn_omega, L0_attn_W1, L0_attn_b1, L0_attn_W2, L0_attn_b2, L0_attn_gamma, L0_attn_beta)
    h = _layernorm(x, axis=-1) * (1 + cb) + sb
    x = x + gb * _L0_ffn_ref(h, L0_ffn_shared_gate, L0_ffn_shared_up, L0_ffn_shared_down, L0_ffn_gate_w, L0_ffn_up_w, L0_ffn_down_w, L0_ffn_router_w, L0_ffn_routing_bias)
    return x

_drawn_inputs = setup_inputs


def setup_inputs(seed=0):
    import zlib

    import numpy as np

    out = dict(_drawn_inputs(seed))
    spreads = {'L0_attn_b1': (0.0, 0.8),
     'L0_attn_b2': (0.0, 0.306),
     'L0_attn_gamma': (1.0, 0.6),
     'L0_attn_beta': (0.0, 0.8),
     'L0_ffn_routing_bias': (0.0, 0.8)}
    factors = {'L0_attn_Wq': 24.268,
     'L0_attn_Wk': 23.377,
     'L0_attn_Wv': 30.612,
     'L0_attn_Wo': 27.362,
     'L0_attn_omega': 22.756,
     'L0_attn_W1': 8.0,
     'L0_attn_W2': 8.0,
     'L0_ffn_shared_gate': 8.0,
     'L0_ffn_shared_up': 8.0,
     'L0_ffn_shared_down': 8.0,
     'L0_ffn_gate_w': 8.0,
     'L0_ffn_up_w': 8.0,
     'L0_ffn_down_w': 8.0,
     'L0_ffn_router_w': 8.0}
    for name, (base, spread) in spreads.items():
        noise = np.random.default_rng([zlib.crc32(name.encode()), seed]).standard_normal(out[name].shape)
        drawn = base * np.exp(spread * noise) if base else spread * noise
        out[name] = jnp.asarray(drawn.astype(out[name].dtype))
    for name, factor in factors.items():
        out[name] = (out[name] * factor).astype(out[name].dtype)
    return out
```

```python
from contextlib import ExitStack

import concourse.bass as bass
from concourse import mybir

P = 128
F32 = mybir.dt.float32
I32 = mybir.dt.int32
ALU = mybir.AluOpType
ACT = mybir.ActivationFunctionType
AX = mybir.AxisListType

LN_EPS = 1e-5
ATTN_LN_EPS = 1e6
FEAT_EPS = 1e-6


def adaln_block(nc, x, wq, wk, wv, wo, omega, w1, b1, w2, b2, gamma, beta,
                sh_gate, sh_up, sh_down, gate_w, up_w, down_w, router_w, routing_bias,
                c, wmod, out):
    B, S, D = x.shape
    M, DH = omega.shape
    H = D // DH
    HB = DFF_BLOCKS = w1.shape[1] // P
    E, _, I = gate_w.shape
    IB = I // P
    C = S // P
    TG = 4
    G = C // TG
    NV = DH + 1
    INV_SQRT_M = float(M) ** -0.5
    QK_SCALE = float(DH) ** -0.25
    assert D == P and M == P and B == 2 and H == 2 and IB == 2

    with ExitStack() as ctx:
        def sb(name, shape, dt=F32):
            return ctx.enter_context(nc.sbuf_tensor(name, shape, dt))

        def sem(name):
            return ctx.enter_context(nc.semaphore(name))

        ident = sb("ident", [P, P])
        causal = sb("causal", [P, H, P])
        x_all = sb("x_all", [P, B, C, P])
        xn_all = sb("xn_all", [P, B, C, P])
        h_all = sb("h_all", [P, B, C, P])
        stats = sb("stats", [P, B, C, 6])
        stats3 = sb("stats3", [P, B, TG, 6])
        mean = sb("mean", [P, B, C])
        var = sb("var", [P, B, C])
        rstd = sb("rstd", [P, B, C])
        lt = [sb(f"lt{i}", [P, B, C]) for i in range(3)]
        l3 = [sb(f"l3{i}", [P, B, TG]) for i in range(6)]
        vec_rows = sb("vec_rows", [5 + HB + E, P])
        vecT = sb("vecT", [P, 5 + HB + E])
        rbias = sb("rbias", [P, E])
        silu_c = sb("silu_c", [P, B])
        silu_bc = sb("silu_bc", [P, B, P])
        wmod_sb = sb("wmod_sb", [P, 6 * P])
        mod = sb("mod", [P, B, 6, P])
        ga_col = sb("ga_col", [P, B])
        ga_abs = sb("ga_abs", [P, B])
        gab2 = sb("gab2", [P, B])
        gsign = sb("gsign", [P, B, P])
        wq_sb, wk_sb, wv_sb, wo_sb = (sb(n, [P, P]) for n in ("wq_sb", "wk_sb", "wv_sb", "wo_sb"))
        om2 = sb("om2", [P, 2, DH])
        wqT, wkT, om2T = (sb(n, [P, P]) for n in ("wqT", "wkT", "om2T"))
        wproj = sb("wproj", [P, 2 * H, M])
        w1_sb = sb("w1_sb", [P, HB, P])
        w2_sb = sb("w2_sb", [P, HB, P])
        shg_sb = sb("shg_sb", [P, IB, P])
        shu_sb = sb("shu_sb", [P, IB, P])
        shd_sb = sb("shd_sb", [P, IB, P])
        shgT = sb("shgT", [P, I])
        shuT = sb("shuT", [P, I])
        shdT = sb("shdT", [P, IB, P])
        gate_sb = sb("gate_sb", [P, E, I])
        up_sb = sb("up_sb", [P, E, I])
        down_sb = sb("down_sb", [P, E, IB, P])
        hmul = [sb(f"hmul{b}", [P, P]) for b in range(B)]
        hst = [sb(f"hst{b}", [P, P]) for b in range(B)]
        hT = [sb(f"hT{b}", [P, P]) for b in range(B)]
        negmax = [sb(f"negmax{b}", [P, 2 * H]) for b in range(B)]
        feat = [sb(f"feat{b}", [P, 2 * H, M]) for b in range(B)]
        featT = [sb(f"featT{b}", [P, 2 * H, P]) for b in range(B)]
        kfeat = [sb(f"kfeat{b}", [P, H, M]) for b in range(B)]
        vext = [sb(f"vext{b}", [P, H, NV]) for b in range(B)]
        att = [sb(f"att{b}", [P, H, P]) for b in range(B)]
        state = [sb(f"state{b}", [P, H, NV]) for b in range(B)]
        den = [sb(f"den{b}", [P, H]) for b in range(B)]
        rden = [sb(f"rden{b}", [P, H]) for b in range(B)]
        o_n = [sb(f"o_n{b}", [P, H, DH]) for b in range(B)]
        oT = [sb(f"oT{b}", [P, P]) for b in range(B)]
        yn = [sb(f"yn{b}", [P, TG, P]) for b in range(B)]
        h2T = [sb(f"h2T{b}", [P, TG * P]) for b in range(B)]
        hid = [sb(f"hid{b}", [P, HB, TG * P]) for b in range(B)]
        o2T = [sb(f"o2T{b}", [P, TG * P]) for b in range(B)]
        h3 = [sb(f"h3{b}", [P, TG, P]) for b in range(B)]
        h3T = [sb(f"h3T{b}", [P, TG * P]) for b in range(B)]
        logit = [sb(f"logit{b}", [P, TG, E]) for b in range(B)]
        prob = [sb(f"prob{b}", [P, TG, E]) for b in range(B)]
        rank = sb("rank", [P, TG, E])
        r1, r2, r3 = (sb(n, [P, TG, E]) for n in ("r1", "r2", "r3"))
        top1, top2, tk, tsum, tinv = (sb(n, [P, TG]) for n in ("top1", "top2", "tk", "tsum", "tinv"))
        wgt = [sb(f"wgt{b}", [P, TG, E]) for b in range(B)]
        sil = [sb(f"sil{i}", [P, TG * P]) for i in range(2)]
        act = [sb(f"act{i}", [P, IB, TG * P]) for i in range(2)]
        acc = [sb(f"acc{b}", [P, TG, P]) for b in range(B)]

        bank = [ctx.enter_context(nc.psum_tensor(f"bank{i}", [P, 512], F32)) for i in range(8)]
        bA, bB, bC, bD = ([bank[4 * b + k] for b in range(B)] for k in range(4))

        x_in = [sem(f"x_in{b}") for b in range(B)]
        vec_in, attn_in, mod_in, ffn_in, moe_in = map(sem, ("vec_in", "attn_in", "mod_in", "ffn_in", "moe_in"))
        consts = sem("consts")
        pe_setup = sem("pe_setup")
        setup_used = sem("setup_used")
        silu_done = sem("silu_done")
        silu_bc_done = sem("silu_bc_done")
        mod_ready = sem("mod_ready")
        xn_ready = sem("xn_ready")
        dv = sem("dv")
        pl = sem("pl")
        h_staged = sem("h_staged")
        hT_tr, hT_ready = sem("hT_tr"), sem("hT_ready")
        proj_done, max_ready, feat_ready = sem("proj_done"), sem("max_ready"), sem("feat_ready")
        featT_tr, featT_ready, kfeat_ready = sem("featT_tr"), sem("featT_ready"), sem("kfeat_ready")
        v_done, vext_ready = sem("v_done"), sem("vext_ready")
        att_done, att_ready = sem("att_done"), sem("att_ready")
        o_done, st_done, on_ready = sem("o_done"), sem("st_done"), sem("on_ready")
        oT_tr, oT_ready, wo_done, y_ready = sem("oT_tr"), sem("oT_ready"), sem("wo_done"), sem("y_ready")
        den_ready, rden_ready = sem("den_ready"), sem("rden_ready")
        dv2 = sem("dv2")
        yn_ready, h2T_tr, h2T_ready = sem("yn_ready"), sem("h2T_tr"), sem("h2T_ready")
        w1_done, hid_a, hid_v = sem("w1_done"), sem("hid_a"), sem("hid_v")
        w2_done, o2T_ready, o2_tr, x1_ready = sem("w2_done"), sem("o2T_ready"), sem("o2_tr"), sem("x1_ready")
        x1n_ready, h3_mul, h3_ready, h3T_tr, h3T_ready = (sem(n) for n in ("x1n_ready", "h3_mul", "h3_ready", "h3T_tr", "h3T_ready"))
        logit_done, logit_ready, prob_ready = sem("logit_done"), sem("logit_ready"), sem("prob_ready")
        g_done, u_done, sil_ready, act_ready = sem("g_done"), sem("u_done"), sem("sil_ready"), sem("act_ready")
        yexp_done, acc_ready = sem("yexp_done"), sem("acc_ready")
        fin_ready, stored = sem("fin_ready"), sem("stored")
        dv3 = sem("dv3")

        block = ctx.enter_context(nc.Block())
        NSETUP = 4

        @block.sync
        def _(sp):
            sp.dma_start(vec_rows[0:2, :], c).then_inc(vec_in, 16)
            sp.dma_start(vec_rows[2:3, :], gamma.rearrange("(a n) -> a n", a=1)).then_inc(vec_in, 16)
            sp.dma_start(vec_rows[3:4, :], beta.rearrange("(a n) -> a n", a=1)).then_inc(vec_in, 16)
            sp.dma_start(vec_rows[4:5, :], b2.rearrange("(a n) -> a n", a=1)).then_inc(vec_in, 16)
            sp.dma_start(vec_rows[5:5 + HB, :], b1.rearrange("(a n) -> a n", n=P)).then_inc(vec_in, 16)
            sp.dma_start(vec_rows[5 + HB:5 + HB + E, :], router_w).then_inc(vec_in, 16)
            for b in range(B):
                sp.dma_start(x_all[:, b, :, :], x[b].rearrange("(c p) d -> p c d", p=P)).then_inc(x_in[b], 16)
            sp.dma_start(w1_sb[:, :, :], w1.rearrange("d (j n) -> d j n", n=P)).then_inc(ffn_in, 16)
            sp.dma_start(w2_sb[:, :, :], w2.rearrange("(j p) n -> p j n", p=P)).then_inc(ffn_in, 16)
            sp.dma_start(gate_sb[:, :, :], gate_w.rearrange("e h i -> h e i")).then_inc(moe_in, 16)
            sp.dma_start(up_sb[:, :, :], up_w.rearrange("e h i -> h e i")).then_inc(moe_in, 16)
            sp.dma_start(down_sb[:, :, :, :], down_w.rearrange("e (j p) n -> p e j n", p=P)).then_inc(moe_in, 16)
            with sp.Fori(0, G) as k:
                for b in range(B):
                    sp.wait_ge(fin_ready, k * B + b + 1)
                    sp.dma_start(out[b].rearrange("(c p) d -> p c d", p=P)[:, bass.ds(k * TG, TG), :],
                                 h_all[:, b, bass.ds(k * TG, TG), :]).then_inc(stored, 16)
            sp.wait_ge(stored, 16 * B * G)

        @block.gpsimd
        def _(pool):
            nc.gpsimd.memset(ident[:, :], 0.0).then_inc(pl, 1)
            nc.gpsimd.memset(causal[:, :, :], 1.0).then_inc(pl, 1)
            nc.gpsimd.iota(rank[:, :, :], pattern=[[0, TG], [-1, E]], base=E, channel_multiplier=0,
                           allow_small_or_imprecise_dtypes=True).then_inc(pl, 1)
            pool.wait_ge(pl, 3)
            nc.gpsimd.affine_select(out=ident[:, :], in_=ident[:, :], compare_op=ALU.not_equal, fill=1.0,
                                    base=0, pattern=[[-1, P]], channel_multiplier=1).then_inc(consts, 1)
            nc.gpsimd.affine_select(out=causal[:, :, :], in_=causal[:, :, :], compare_op=ALU.is_ge, fill=0.0,
                                    base=0, pattern=[[0, H], [1, P]], channel_multiplier=-1).then_inc(consts, 1)

            def stage(ci, first=False):
                for b in range(B):
                    nc.gpsimd.tensor_tensor(hmul[b][:, :], xn_all[:, b, bass.ds(ci, 1), :], mod[:, b, 1, :],
                                            ALU.mult).then_inc(pl, 1)
                    pool.wait_ge(pl, ci * 2 * B + 2 * b + 4)
                    nc.gpsimd.tensor_tensor(h_all[:, b, bass.ds(ci, 1), :], hmul[b][:, :], mod[:, b, 0, :],
                                            ALU.add).then_inc(pl, 1)
                    if not first:
                        pool.wait_ge(hT_tr, ci * B + b - B + 1)
                    nc.gpsimd.tensor_tensor(hst[b][:, :], hmul[b][:, :], mod[:, b, 0, :],
                                            ALU.add).then_inc(h_staged, 1)

            pool.wait_ge(xn_ready, 1)
            pool.wait_ge(mod_ready, 1)
            stage(0, first=True)
            with pool.Fori(1, C) as ci:
                stage(ci)
            with pool.Fori(0, G) as k:
                for b in range(B):
                    pool.wait_ge(x1n_ready, k * B + b + 1)
                    nc.gpsimd.tensor_tensor(h3[b][:, :, :], yn[b][:, :, :],
                                            mod[:, b, 4, :].unsqueeze(1).to_broadcast([P, TG, P]),
                                            ALU.mult).then_inc(h3_mul, 1)
                    pool.wait_ge(h3_mul, k * B + b + 1)
                    nc.gpsimd.tensor_tensor(h3[b][:, :, :], h3[b][:, :, :],
                                            mod[:, b, 3, :].unsqueeze(1).to_broadcast([P, TG, P]),
                                            ALU.add).then_inc(h3_ready, 1)

        @block.scalar
        def _(act_e):
            act_e.dma_start(wmod_sb[:, :], wmod).then_inc(mod_in, 16)
            act_e.dma_start(wq_sb[:, :], wq).then_inc(attn_in, 16)
            act_e.dma_start(wk_sb[:, :], wk).then_inc(attn_in, 16)
            act_e.dma_start(om2[:, 0, :], omega).then_inc(attn_in, 16)
            act_e.dma_start(om2[:, 1, :], omega).then_inc(attn_in, 16)
            act_e.dma_start(wv_sb[:, :], wv).then_inc(attn_in, 16)
            act_e.dma_start(wo_sb[:, :], wo).then_inc(attn_in, 16)
            act_e.dma_start(shg_sb[:, :, :], sh_gate.rearrange("(j p) h -> p j h", p=P)).then_inc(attn_in, 16)
            act_e.dma_start(shu_sb[:, :, :], sh_up.rearrange("(j p) h -> p j h", p=P)).then_inc(attn_in, 16)
            act_e.dma_start(shd_sb[:, :, :], sh_down.rearrange("h (j p) -> h j p", p=P)).then_inc(attn_in, 16)
            act_e.dma_start(rbias[:, :], routing_bias.partition_broadcast(P)).then_inc(attn_in, 16)
            act_e.wait_ge(setup_used, 1)
            nc.scalar.activation(silu_c[:, :], vecT[:, 0:B], ACT.Silu).then_inc(silu_done, 1)

            def front_hT(ci):
                for b in range(B):
                    act_e.wait_ge(hT_tr, ci * B + b + 1)
                    nc.scalar.copy(hT[b][:, :], bA[b][:, 0:P]).then_inc(hT_ready, 1)

            def front_exp(ci):
                for b in range(B):
                    act_e.wait_ge(max_ready, ci * B + b + 1)
                    for j in range(2 * H):
                        a = nc.scalar.activation(feat[b][:, j, :], bB[b][:, j * M:(j + 1) * M], ACT.Exp,
                                                 bias=negmax[b][:, j:j + 1])
                    a.then_inc(feat_ready, 1)

            def front_v(ci):
                for b in range(B):
                    act_e.wait_ge(v_done, ci * B + b + 1)
                    nc.scalar.copy(vext[b][:, :, 0:DH],
                                   bD[b][:, 2 * P:3 * P].rearrange("p (h d) -> p h d", h=H)).then_inc(vext_ready, 1)

            def back(ci):
                for b in range(B):
                    act_e.wait_ge(oT_tr, ci * B + b + 1)
                    nc.scalar.copy(oT[b][:, :], bC[b][:, 2 * P:3 * P]).then_inc(oT_ready, 1)

            front_hT(0)
            front_exp(0)
            front_v(0)
            with act_e.Fori(0, C - 1) as ci:
                front_hT(ci + 1)
                front_exp(ci + 1)
                front_v(ci + 1)
                back(ci)
            back(C - 1)

            with act_e.Fori(0, G) as k:
                for b in range(B):
                    act_e.wait_ge(h2T_tr, k * B + b + 1)
                    nc.scalar.activation(h2T[b][:, :], bA[b][:, :], ACT.Identity, bias=vecT[:, 3:4],
                                         scale=vecT[:, 2:3]).then_inc(h2T_ready, 1)
                    for j in range(0, HB, 2):
                        act_e.wait_ge(w1_done, (k * B + b) * HB + j + 1)
                        nc.scalar.activation(hid[b][:, j, :], [bB, bC, bD, bB][j][b][:, :], ACT.Relu,
                                             bias=vecT[:, 5 + j:6 + j]).then_inc(hid_a, 1)
                for b in range(B):
                    act_e.wait_ge(w2_done, k * B + b + 1)
                    nc.scalar.activation(o2T[b][:, :], bA[b][:, :], ACT.Identity, bias=gab2[:, b:b + 1],
                                         scale=ga_col[:, b:b + 1]).then_inc(o2T_ready, 1)
                for b in range(B):
                    act_e.wait_ge(h3T_tr, k * B + b + 1)
                    nc.scalar.copy(h3T[b][:, :], bC[b][:, :]).then_inc(h3T_ready, 1)
                for b in range(B):
                    act_e.wait_ge(logit_ready, k * B + b + 1)
                    nc.scalar.activation(prob[b][:, :, :], logit[b][:, :, :], ACT.Sigmoid).then_inc(prob_ready, 1)
                n = 0
                for b in range(B):
                    for e in range(E + 1):
                        for j in range(IB):
                            act_e.wait_ge(g_done, k * (B * (E + 1) * IB) + n + 1)
                            if n >= 2:
                                act_e.wait_ge(act_ready, k * (B * (E + 1) * IB) + n - 1)
                            nc.scalar.activation(sil[n % 2][:, :], bank[2 * (n % 2)][:, :],
                                                 ACT.Silu).then_inc(sil_ready, 1)
                            n += 1

        @block.vector
        def _(dve):
            V = nc.vector
            count = [0]

            def link(ins):
                ins.then_inc(dv, 1)
                count[0] += 1
                dve.wait_ge(dv, count[0])

            def moments(st, mn, vr, chain, u, v_, w):
                V.tensor_tensor(mn, st[:, :, :, 1], st[:, :, :, 4], ALU.add)
                V.tensor_tensor(u, st[:, :, :, 1], st[:, :, :, 4], ALU.subtract)
                chain(V.tensor_tensor(v_, st[:, :, :, 2], st[:, :, :, 5], ALU.add))
                V.tensor_scalar(mn, mn, 0.5, None, ALU.mult)
                chain(V.scalar_tensor_tensor(w, u, 0.25, u, ALU.mult, ALU.mult))
                chain(V.scalar_tensor_tensor(vr, v_, 1.0 / P, w, ALU.mult, ALU.add))

            def rsqrt(r, v_, eps, chain, u, w, t):
                chain(V.tensor_scalar(w, v_, eps, None, ALU.add))
                chain(V.tensor_scalar(u.bitcast(I32), w.bitcast(I32), 1, None, ALU.logical_shift_right))
                chain(V.tensor_scalar(r.bitcast(I32), u.bitcast(I32), -1.0, float(0x5F3759DF), ALU.mult, ALU.add))
                for _ in range(4):
                    chain(V.tensor_tensor(u, r, r, ALU.mult))
                    chain(V.scalar_tensor_tensor(t, u, -0.5, w, ALU.mult, ALU.mult))
                    chain(V.scalar_tensor_tensor(r, t, 1.5, r, ALU.add, ALU.mult))

            L = lambda t: t[:, :, :]
            V.memset(vext[0][:, :, DH:NV], 1.0)
            V.memset(vext[1][:, :, DH:NV], 1.0)
            V.memset(state[0][:, :, :], 0.0)
            V.memset(state[1][:, :, :], 0.0).then_inc(y_ready, 2)
            for b in range(B):
                dve.wait_ge(x_in[b], 16)
                for ci in range(C):
                    V.bn_stats(stats[:, b, ci, :], x_all[:, b, ci, :]).then_inc(dv, 1)
                    count[0] += 1
            dve.wait_ge(dv, count[0])
            dve.wait_ge(pe_setup, 1)
            V.tensor_copy(vecT[:, :], bank[0][:, 0:5 + HB + E]).then_inc(setup_used, 1)
            moments(stats, L(mean), L(var), link, L(lt[0]), L(lt[1]), L(lt[2]))
            rsqrt(L(rstd), L(var), LN_EPS, link, L(lt[0]), L(lt[1]), L(lt[2]))
            for b in range(B):
                for ci in range(C):
                    last = V.tensor_scalar(xn_all[:, b, ci, :], x_all[:, b, ci, :], mean[:, b, ci:ci + 1],
                                           rstd[:, b, ci:ci + 1], ALU.subtract, ALU.mult)
            last.then_inc(xn_ready, 1)
            dve.wait_ge(silu_done, 1)
            for b in range(B):
                last = V.tensor_copy(silu_bc[:, b, :], silu_c[:, b:b + 1].to_broadcast([P, P]))
            last.then_inc(silu_bc_done, 1)
            dve.wait_ge(pe_setup, 2)
            V.tensor_copy(wqT[:, :], bank[1][:, 0:P])
            V.tensor_copy(wkT[:, :], bank[1][:, P:2 * P])
            V.tensor_copy(om2T[:, :], bank[1][:, 2 * P:3 * P]).then_inc(setup_used, 1)
            V.tensor_copy(shgT[:, :], bank[2][:, 0:I])
            V.tensor_copy(shuT[:, :], bank[2][:, I:2 * I])
            V.tensor_copy(shdT[:, :, :], bank[3][:, 0:I])
            dve.wait_ge(pe_setup, 3)
            for h in range(H):
                last = V.tensor_scalar(wproj[:, h:2 * H:H, :], bank[4 + 2 * h][:, 0:2 * M].rearrange(
                    "p (j m) -> p j m", m=M), QK_SCALE, None, ALU.mult)
            last.then_inc(setup_used, 1)
            dve.wait_ge(pe_setup, 4)
            V.tensor_copy(mod[:, 0, 0:4, :], bank[0][:, :])
            V.tensor_copy(mod[:, 0, 4:6, :], bank[1][:, 0:2 * P])
            V.tensor_copy(mod[:, 1, 0:4, :], bank[2][:, :])
            link(V.tensor_copy(mod[:, 1, 4:6, :], bank[3][:, 0:2 * P]))
            link(V.tensor_copy(ga_col[:, :], bank[5][:, 0:B]))
            V.tensor_scalar(mod[:, :, 1, :], mod[:, :, 1, :], 1.0, None, ALU.add)
            V.tensor_scalar(mod[:, :, 4, :], mod[:, :, 4, :], 1.0, None, ALU.add)
            link(V.scalar_tensor_tensor(ga_abs[:, :], ga_col[:, :], -1.0, ga_col[:, :], ALU.mult, ALU.max))
            V.tensor_scalar(ga_abs[:, :], ga_abs[:, :], 0.25, None, ALU.max)
            V.tensor_scalar(gsign[:, :, :], mod[:, :, 5, :], 0.0, 2.0, ALU.is_ge, ALU.mult)
            link(V.tensor_scalar(ga_col[:, :], ga_col[:, :], 0.0, 2.0, ALU.is_ge, ALU.mult))
            link(V.scalar_tensor_tensor(mod[:, :, 5, :], mod[:, :, 5, :], -1.0, mod[:, :, 5, :], ALU.mult, ALU.max))
            link(V.tensor_scalar(mod[:, :, 5, :], mod[:, :, 5, :], 0.25, None, ALU.max))
            V.scalar_tensor_tensor(ga_col[:, :], ga_col[:, :], -1.0, ga_abs[:, :], ALU.add, ALU.mult)
            link(V.scalar_tensor_tensor(mod[:, :, 5, :], gsign[:, :, :], -1.0, mod[:, :, 5, :], ALU.add, ALU.mult))
            V.tensor_scalar(gab2[:, :], ga_col[:, :], vecT[:, 4:5], None, ALU.mult).then_inc(mod_ready, 1)

            def front_max(ci):
                for b in range(B):
                    dve.wait_ge(proj_done, ci * B + b + 1)
                    V.tensor_reduce(negmax[b][:, :], bB[b][:, :].rearrange("p (j m) -> p j m", m=M), AX.X,
                                    ALU.max, negate=True).then_inc(max_ready, 1)

            def back_feat(ci):
                for b in range(B):
                    dve.wait_ge(featT_tr, ci * B + b + 1)
                    V.tensor_scalar(featT[b][:, :, :], bC[b][:, :], INV_SQRT_M, FEAT_EPS, ALU.mult,
                                    ALU.add).then_inc(featT_ready, 1)
                    V.tensor_scalar(kfeat[b][:, :, :], feat[b][:, H:2 * H, :], INV_SQRT_M, FEAT_EPS, ALU.mult,
                                    ALU.add).then_inc(kfeat_ready, 1)

            def back_mask(ci):
                for b in range(B):
                    dve.wait_ge(att_done, ci * B + b + 1)
                    V.tensor_tensor(att[b][:, :, :], bD[b][:, 0:H * P], causal[:, :, :], ALU.mult)\
                        .then_inc(att_ready, 1)

            def back_out(ci):
                for b in range(B):
                    o = bA[b][:, 2 * P:2 * P + H * NV].rearrange("p (h n) -> p h n", h=H)
                    dve.wait_ge(o_done, ci * B + b + 1)
                    V.tensor_scalar(den[b][:, :], o[:, :, DH], FEAT_EPS, None, ALU.add).then_inc(den_ready, 1)
                    dve.wait_ge(den_ready, ci * B + b + 1)
                    V.reciprocal(rden[b][:, :], den[b][:, :]).then_inc(rden_ready, 1)
                    dve.wait_ge(st_done, ci * B + b + 1)
                    V.tensor_tensor(state[b][:, :, :], bC[b][:, 0:H * NV], state[b][:, :, :], ALU.add)
                    dve.wait_ge(rden_ready, ci * B + b + 1)
                    V.tensor_tensor(o_n[b][:, :, :], o[:, :, 0:DH],
                                    rden[b][:, :].unsqueeze(2).to_broadcast([P, H, DH]), ALU.mult)\
                        .then_inc(on_ready, 1)
                for b in range(B):
                    dve.wait_ge(wo_done, ci * B + b + 1)
                    V.tensor_tensor(h_all[:, b, bass.ds(ci, 1), :], bC[b][:, 3 * P:4 * P],
                                    h_all[:, b, bass.ds(ci, 1), :], ALU.add).then_inc(y_ready, 1)
                dve.wait_ge(y_ready, ci * B + B + 2)
                V.memset(tk[0:1, 0:1], 0.0)
                for b in range(B):
                    V.bn_stats(stats[:, b, bass.ds(ci, 1), :], h_all[:, b, bass.ds(ci, 1), :]).then_inc(dv2, 1)

            front_max(0)
            with dve.Fori(0, C - 1) as ci:
                back_feat(ci)
                back_mask(ci)
                front_max(ci + 1)
                back_out(ci)
            back_feat(C - 1)
            back_mask(C - 1)
            back_out(C - 1)
            dve.wait_ge(dv2, B * C)
            moments(stats, L(mean), L(var), link, L(lt[0]), L(lt[1]), L(lt[2]))
            rsqrt(L(rstd), L(var), ATTN_LN_EPS, link, L(lt[0]), L(lt[1]), L(lt[2]))

            dve.wait_ge(consts, 2)
            with dve.Fori(0, G) as k:
                turn = [0]
                CHAIN = 56

                def link3(ins):
                    ins.then_inc(dv3, 1)
                    turn[0] += 1
                    dve.wait_ge(dv3, k * CHAIN + turn[0])

                for b in range(B):
                    for j in range(TG):
                        last = V.tensor_scalar(yn[b][:, j, :], h_all[:, b, bass.ds(k * TG + j, 1), :],
                                               mean[:, b, bass.ds(k * TG + j, 1)],
                                               rstd[:, b, bass.ds(k * TG + j, 1)], ALU.subtract, ALU.mult)
                    last.then_inc(yn_ready, 1)
                for b in range(B):
                    for j in range(1, HB, 2):
                        dve.wait_ge(w1_done, (k * B + b) * HB + j + 1)
                        V.tensor_scalar(hid[b][:, j, :], [bB, bC, bD, bB][j][b][:, :], vecT[:, 5 + j:6 + j], 0.0,
                                        ALU.add, ALU.max).then_inc(hid_v, 1)
                for b in range(B):
                    xs = x_all[:, b, bass.ds(k * TG, TG), :]
                    dve.wait_ge(o2_tr, k * B + b + 1)
                    link3(V.tensor_tensor(xs, bB[b][:, :].rearrange("p (t d) -> p t d", d=P), xs, ALU.add))
                    V.memset(tk[0:1, 0:1], 0.0)
                    for j in range(TG):
                        last = V.bn_stats(stats3[:, b, j, :], x_all[:, b, bass.ds(k * TG + j, 1), :])
                    link3(last)
                s3 = stats3[:, :, :, :]
                moments(s3, L(l3[0]), L(l3[1]), link3, L(l3[2]), L(l3[4]), L(l3[3]))
                rsqrt(L(l3[2]), L(l3[1]), LN_EPS, link3, L(l3[3]), L(l3[4]), L(l3[5]))
                for b in range(B):
                    dve.wait_ge(h2T_tr, k * B + b + 1)
                    for j in range(TG):
                        last = V.tensor_scalar(yn[b][:, j, :], x_all[:, b, bass.ds(k * TG + j, 1), :],
                                               l3[0][:, b, j:j + 1], l3[2][:, b, j:j + 1],
                                               ALU.subtract, ALU.mult)
                    last.then_inc(x1n_ready, 1)
                for b in range(B):
                    dve.wait_ge(logit_done, k * B + b + 1)
                    V.tensor_tensor(logit[b][:, :, :], bD[b][:, 0:TG * E].rearrange("p (t e) -> p t e", e=E),
                                    rbias[:, :].unsqueeze(1).to_broadcast([P, TG, E]), ALU.add)\
                        .then_inc(logit_ready, 1)
                for b in range(B):
                    dve.wait_ge(prob_ready, k * B + b + 1)
                    pr = prob[b][:, :, :]

                    def bc(t):
                        return t[:, :].unsqueeze(2).to_broadcast([P, TG, E])

                    def first_of(p_ap, top, onehot):
                        link3(V.tensor_reduce(top[:, :], p_ap, AX.X, ALU.max))
                        link3(V.tensor_tensor(r3[:, :, :], p_ap, bc(top), ALU.is_equal))
                        link3(V.tensor_tensor(r3[:, :, :], r3[:, :, :], rank[:, :, :], ALU.mult))
                        link3(V.tensor_reduce(tk[:, :], r3[:, :, :], AX.X, ALU.max))
                        link3(V.tensor_tensor(onehot, r3[:, :, :], bc(tk), ALU.is_equal))

                    first_of(pr, top1, r1[:, :, :])
                    link3(V.scalar_tensor_tensor(r2[:, :, :], r1[:, :, :], -2.0, pr, ALU.mult, ALU.add))
                    first_of(r2[:, :, :], top2, r2[:, :, :])
                    link3(V.tensor_tensor(tsum[:, :], top1[:, :], top2[:, :], ALU.add))
                    link3(V.tensor_tensor(r1[:, :, :], r1[:, :, :], r2[:, :, :], ALU.add))
                    link3(V.reciprocal(tinv[:, :], tsum[:, :]))
                    link3(V.tensor_tensor(r1[:, :, :], r1[:, :, :], pr, ALU.mult))
                    link3(V.tensor_tensor(wgt[b][:, :, :], r1[:, :, :], bc(tinv), ALU.mult))
                def accumulate(b, e):
                    m = b * (E + 1) + e
                    y = bank[4 + m % 2]
                    dve.wait_ge(yexp_done, k * B * (E + 1) + m + 1)
                    if e == 0:
                        V.tensor_copy(acc[b][:, :, :], y[:, :]).then_inc(acc_ready, 1)
                        dve.wait_ge(acc_ready, k * B * (E + 1) + m + 1)
                        return
                    for t in range(TG):
                        last = V.scalar_tensor_tensor(acc[b][:, t, :], y[:, t * P:(t + 1) * P],
                                                    wgt[b][:, t, e - 1:e], acc[b][:, t, :], ALU.mult, ALU.add)
                    last.then_inc(acc_ready, 1)
                    dve.wait_ge(acc_ready, k * B * (E + 1) + m + 1)

                n = 0
                for b in range(B):
                    for e in range(E + 1):
                        for j in range(IB):
                            dve.wait_ge(sil_ready, k * (B * (E + 1) * IB) + n + 1)
                            dve.wait_ge(u_done, k * (B * (E + 1) * IB) + n + 1)
                            V.tensor_tensor(act[(b * (E + 1) + e) % 2][:, j, :], bank[2 * (n % 2) + 1][:, :],
                                            sil[n % 2][:, :], ALU.mult).then_inc(act_ready, 1)
                            n += 1
                        if e >= 1:
                            accumulate(b, e - 1)
                    accumulate(b, E)
                    link3(V.tensor_tensor(acc[b][:, :, :], acc[b][:, :, :],
                                          mod[:, b, 5, :].unsqueeze(1).to_broadcast([P, TG, P]), ALU.mult))
                    V.tensor_tensor(h_all[:, b, bass.ds(k * TG, TG), :], acc[b][:, :, :],
                                    x_all[:, b, bass.ds(k * TG, TG), :], ALU.add).then_inc(fin_ready, 1)
                assert turn[0] == CHAIN, turn[0]

        @block.tensor
        def _(pe):
            def mm(o, lhsT, rhs, start=True, stop=True):
                return nc.tensor.matmul(o, lhsT, rhs, start=start, stop=stop)

            pe.wait_ge(consts, 1)
            pe.wait_ge(vec_in, 16 * 6)
            nv = 5 + HB + E
            nc.tensor.transpose(bank[0][:, 0:nv], vec_rows[:, :], ident[0:nv, 0:nv]).then_inc(pe_setup, 1)
            pe.wait_ge(attn_in, 16 * 10)
            nc.tensor.transpose(bank[1][:, 0:P], wq_sb[:, :], ident[:, :])
            nc.tensor.transpose(bank[1][:, P:2 * P], wk_sb[:, :], ident[:, :])
            for j in range(IB):
                nc.tensor.transpose(bank[2][:, j * P:(j + 1) * P], shg_sb[:, j, :], ident[:, :])
                nc.tensor.transpose(bank[2][:, I + j * P:I + (j + 1) * P], shu_sb[:, j, :], ident[:, :])
                nc.tensor.transpose(bank[3][:, j * P:(j + 1) * P], shd_sb[:, j, :], ident[:, :])
            nc.tensor.transpose(bank[1][:, 2 * P:3 * P], om2[:, :, :].rearrange("p a d -> p (a d)"),
                                ident[:, :]).then_inc(pe_setup, 1)
            pe.wait_ge(setup_used, 2)
            for i, (w, h) in enumerate([(wqT, 0), (wqT, 1), (wkT, 0), (wkT, 1)]):
                last = mm(bank[4 + 2 * h][:, (i // H) * M:(i // H + 1) * M], w[h * DH:(h + 1) * DH, :], om2T[h * DH:(h + 1) * DH, :])
            last.then_inc(pe_setup, 1)
            pe.wait_ge(mod_in, 16)
            pe.wait_ge(silu_bc_done, 1)
            pe.wait_ge(setup_used, 3)
            for b in range(B):
                mm(bank[2 * b][:, :], silu_bc[:, b, :], wmod_sb[:, 0:512])
                mm(bank[2 * b + 1][:, 0:256], silu_bc[:, b, :], wmod_sb[:, 512:768])
            mm(bank[5][:, 0:B], wmod_sb[:, 2 * P:3 * P], silu_c[:, :]).then_inc(pe_setup, 1)
            pe.wait_ge(mod_ready, 1)

            def front_tr(ci):
                for b in range(B):
                    pe.wait_ge(h_staged, ci * B + b + 1)
                    nc.tensor.transpose(bA[b][:, 0:P], hst[b][:, :], ident[:, :]).then_inc(hT_tr, 1)

            def front_proj(ci):
                for b in range(B):
                    pe.wait_ge(hT_ready, ci * B + b + 1)
                    mm(bB[b][:, :], hT[b][:, :], wproj[:, :, :]).then_inc(proj_done, 1)

            def front_v(ci):
                for b in range(B):
                    mm(bD[b][:, 2 * P:3 * P], hT[b][:, :], wv_sb[:, :]).then_inc(v_done, 1)

            def back_featT(ci):
                for b in range(B):
                    pe.wait_ge(feat_ready, ci * B + b + 1)
                    pe.wait_ge(y_ready, ci * B + b + 1)
                    for j in range(2 * H):
                        last = nc.tensor.transpose(bC[b][:, j * P:(j + 1) * P], feat[b][:, j, :], ident[:, :])
                    last.then_inc(featT_tr, 1)

            def back_att(ci):
                for b in range(B):
                    pe.wait_ge(featT_ready, ci * B + b + 1)
                    pe.wait_ge(vext_ready, ci * B + b + 1)
                    for h in range(H):
                        last = mm(bD[b][:, h * P:(h + 1) * P], featT[b][:, H + h, :], featT[b][:, h, :])
                    last.then_inc(att_done, 1)

            def back_o(ci):
                for b in range(B):
                    pe.wait_ge(att_ready, ci * B + b + 1)
                    pe.wait_ge(kfeat_ready, ci * B + b + 1)
                    for h in range(H):
                        o = bA[b][:, 2 * P + h * NV:2 * P + (h + 1) * NV]
                        mm(o, featT[b][:, h, :], state[b][:, h, :], stop=False)
                        last = mm(o, att[b][:, h, :], vext[b][:, h, :], start=False)
                    last.then_inc(o_done, 1)
                    for h in range(H):
                        last = mm(bC[b][:, h * NV:(h + 1) * NV], kfeat[b][:, h, :], vext[b][:, h, :])
                    last.then_inc(st_done, 1)

            def back_wo(ci):
                for b in range(B):
                    pe.wait_ge(on_ready, ci * B + b + 1)
                    nc.tensor.transpose(bC[b][:, 2 * P:3 * P], o_n[b][:, :, :].rearrange("p h d -> p (h d)"),
                                        ident[:, :]).then_inc(oT_tr, 1)
                for b in range(B):
                    pe.wait_ge(oT_ready, ci * B + b + 1)
                    mm(bC[b][:, 3 * P:4 * P], oT[b][:, :], wo_sb[:, :]).then_inc(wo_done, 1)

            front_tr(0)
            front_proj(0)
            front_v(0)
            with pe.Fori(0, C - 1) as ci:
                back_featT(ci)
                front_tr(ci + 1)
                back_att(ci)
                front_proj(ci + 1)
                back_o(ci)
                front_v(ci + 1)
                back_wo(ci)
            back_featT(C - 1)
            back_att(C - 1)
            back_o(C - 1)
            back_wo(C - 1)

            pe.wait_ge(ffn_in, 32)
            pe.wait_ge(moe_in, 48)
            NU = B * (E + 1) * IB
            with pe.Fori(0, G) as k:
                for b in range(B):
                    pe.wait_ge(yn_ready, k * B + b + 1)
                    for j in range(TG):
                        last = nc.tensor.transpose(bA[b][:, j * P:(j + 1) * P], yn[b][:, j, :], ident[:, :])
                    last.then_inc(h2T_tr, 1)
                for b in range(B):
                    pe.wait_ge(h2T_ready, k * B + b + 1)
                    for j in range(HB):
                        if j == 3:
                            pe.wait_ge(hid_a, (k * B + b) * (HB // 2) + 1)
                        mm([bB, bC, bD, bB][j][b][:, :], w1_sb[:, j, :], h2T[b][:, :]).then_inc(w1_done, 1)
                for b in range(B):
                    pe.wait_ge(hid_a, (k * B + b + 1) * (HB // 2))
                    pe.wait_ge(hid_v, (k * B + b + 1) * (HB // 2))
                    for j in range(HB):
                        last = mm(bA[b][:, :], w2_sb[:, j, :], hid[b][:, j, :], start=j == 0, stop=j == HB - 1)
                    last.then_inc(w2_done, 1)
                for b in range(B):
                    pe.wait_ge(o2T_ready, k * B + b + 1)
                    for j in range(TG):
                        last = nc.tensor.transpose(bB[b][:, j * P:(j + 1) * P], o2T[b][:, j * P:(j + 1) * P],
                                                   ident[:, :])
                    last.then_inc(o2_tr, 1)
                for b in range(B):
                    pe.wait_ge(h3_ready, k * B + b + 1)
                    for j in range(TG):
                        last = nc.tensor.transpose(bC[b][:, j * P:(j + 1) * P], h3[b][:, j, :], ident[:, :])
                    last.then_inc(h3T_tr, 1)
                for b in range(B):
                    pe.wait_ge(h3T_ready, k * B + b + 1)
                    for j in range(TG):
                        last = mm(bD[b][:, j * E:(j + 1) * E], h3T[b][:, j * P:(j + 1) * P],
                                  vecT[:, 5 + HB:5 + HB + E])
                    last.then_inc(logit_done, 1)
                for b in range(B):
                    pe.wait_ge(logit_ready, k * B + b + 1)
                n = 0

                def down(b, e):
                    m = b * (E + 1) + e
                    pe.wait_ge(act_ready, k * NU + (m + 1) * IB)
                    if m >= 2:
                        pe.wait_ge(acc_ready, k * B * (E + 1) + m - 1)
                    for t in range(TG):
                        for j in range(IB):
                            w = shdT[:, j, :] if e == 0 else down_sb[:, e - 1, j, :]
                            last = mm(bank[4 + m % 2][:, t * P:(t + 1) * P], act[m % 2][:, j, t * P:(t + 1) * P],
                                      w, start=j == 0, stop=j == IB - 1)
                    last.then_inc(yexp_done, 1)

                for b in range(B):
                    for e in range(E + 1):
                        for j in range(IB):
                            if n >= 2:
                                pe.wait_ge(act_ready, k * NU + n - 1)
                            g, u = (shgT[:, j * P:(j + 1) * P], shuT[:, j * P:(j + 1) * P]) if e == 0 else \
                                (gate_sb[:, e - 1, j * P:(j + 1) * P], up_sb[:, e - 1, j * P:(j + 1) * P])
                            mm(bank[2 * (n % 2)][:, :], g, h3T[b][:, :]).then_inc(g_done, 1)
                            mm(bank[2 * (n % 2) + 1][:, :], u, h3T[b][:, :]).then_inc(u_done, 1)
                            n += 1
                        if (b, e) != (0, 0):
                            m = b * (E + 1) + e - 1
                            down(m // (E + 1), m % (E + 1))
                down(B - 1, E)
                pe.wait_ge(fin_ready, (k + 1) * B)


_INS = ["L0_attn_batch", "L0_attn_Wq", "L0_attn_Wk", "L0_attn_Wv", "L0_attn_Wo", "L0_attn_omega", "L0_attn_W1",
        "L0_attn_b1", "L0_attn_W2", "L0_attn_b2", "L0_attn_gamma", "L0_attn_beta", "L0_ffn_shared_gate",
        "L0_ffn_shared_up", "L0_ffn_shared_down", "L0_ffn_gate_w", "L0_ffn_up_w", "L0_ffn_down_w",
        "L0_ffn_router_w", "L0_ffn_routing_bias", "L0_c", "L0_wmod"]


def kernel(**inputs):
    import numpy as _np
    import concourse.bacc as _bacc
    from concourse import mybir as _mybir
    from concourse.bass_utils import run_bass_kernel_spmd as _run

    nc = _bacc.Bacc("TRN2", target_bir_lowering=False, num_devices=1)
    arrays, args = {}, []
    for name in _INS:
        a = _np.ascontiguousarray(inputs[name])
        arrays[f"in_{name}"] = a
        args.append(nc.dram_tensor(f"in_{name}", a.shape, _mybir.dt.from_np(a.dtype), kind="ExternalInput").ap())
    out = nc.dram_tensor("out", inputs["L0_attn_batch"].shape, _mybir.dt.float32, kind="ExternalOutput").ap()
    adaln_block(nc, *args, out)
    r = _run(nc, [arrays], core_ids=[0])
    return r.results[0]["out"]
```

```python
from contextlib import ExitStack

import concourse.bass as bass
from concourse import mybir

P = 128
F32 = mybir.dt.float32
F32R = mybir.dt.float32r
BF16 = mybir.dt.bfloat16
I32 = mybir.dt.int32
ALU = mybir.AluOpType
ACT = mybir.ActivationFunctionType
AX = mybir.AxisListType

LN_EPS = 1e-5
ATTN_LN_EPS = 1e6
FEAT_EPS = 1e-6


def adaln_block(nc, xdisp, ydisp, x, wq, wk, wv, wo, omega, w1, b1, w2, b2, gamma, beta,
                sh_gate, sh_up, sh_down, gate_w, up_w, down_w, router_w, routing_bias,
                c, wmod, out):
    B, S, D = x.shape
    M, DH = omega.shape
    H = D // DH
    HB = DFF_BLOCKS = w1.shape[1] // P
    E, _, I = gate_w.shape
    IB = I // P
    C = S // P
    TG = 4
    G = C // TG
    NV = DH + 1
    INV_SQRT_M = float(M) ** -0.5
    QK_SCALE = float(DH) ** -0.25
    U = G * B
    TT = B * TG
    T = B * S
    RB = T // P + 1
    NT = (2 * T + E * (P - 1)) // P
    NU = NT - 2 * T // P + 1
    YB = ydisp.shape[0] // P
    YN = 2 * C
    NBUF = 3
    BW = YB
    assert BW ** NBUF <= 1 << 24 and E ** (2 * NBUF) <= 1 << 24
    assert YB >= E * RB + NU and YB % YN == 0
    assert NT % NBUF == 0 and E * (T // P) == P
    assert D == P and M == P and B == 2 and H == 2 and IB == 2

    with ExitStack() as ctx:
        def sb(name, shape, dt=F32):
            return ctx.enter_context(nc.sbuf_tensor(name, shape, dt))

        def sem(name):
            return ctx.enter_context(nc.semaphore(name))

        ident = sb("ident", [P, P])
        causal = sb("causal", [P, H, P])
        x_all = sb("x_all", [P, B, C, P])
        xn_all = sb("xn_all", [P, B, C, P])
        h_all = sb("h_all", [P, B, C, P])
        stats = sb("stats", [P, B, C, 6])
        stats3 = sb("stats3", [P, B, TG, 6])
        mean = sb("mean", [P, B, C])
        var = sb("var", [P, B, C])
        rstd = sb("rstd", [P, B, C])
        lt = [sb(f"lt{i}", [P, B, C]) for i in range(3)]
        l3 = [sb(f"l3{i}", [P, B, TG]) for i in range(6)]
        vec_rows = sb("vec_rows", [5 + HB + E, P])
        vecT = sb("vecT", [P, 5 + HB + E])
        rbias = sb("rbias", [P, E])
        silu_c = sb("silu_c", [P, B])
        silu_bc = sb("silu_bc", [P, B, P])
        mod = sb("mod", [P, B, 6, P])
        ga_col = sb("ga_col", [P, B])
        ga_abs = sb("ga_abs", [P, B])
        gab2 = sb("gab2", [P, B])
        gsign = silu_bc
        wq_sb, wk_sb, wv_sb, wo_sb = (sb(n, [P, P]) for n in ("wq_sb", "wk_sb", "wv_sb", "wo_sb"))
        om2 = sb("om2", [P, 2, DH])
        wqT, wkT, om2T = (sb(n, [P, P]) for n in ("wqT", "wkT", "om2T"))
        wproj = sb("wproj", [P, 2 * H, M])
        w1_sb = sb("w1_sb", [P, HB, P])
        w2_sb = sb("w2_sb", [P, HB, P])
        shg_sb = sb("shg_sb", [P, IB, P])
        shu_sb = sb("shu_sb", [P, IB, P])
        shd_sb = sb("shd_sb", [P, IB, P])
        shgT = sb("shgT", [P, I])
        shuT = sb("shuT", [P, I])
        shdT = sb("shdT", [P, IB, P])
        gate_sb = sb("gate_sb", [P, E, I])
        up_sb = sb("up_sb", [P, E, I])
        down_sb = sb("down_sb", [P, E, IB, P])
        hmul = [sb(f"hmul{b}", [P, P]) for b in range(B)]
        hst = [sb(f"hst{b}", [P, P]) for b in range(B)]
        hT = [sb(f"hT{b}", [P, P]) for b in range(B)]
        negmax = [sb(f"negmax{b}", [P, 2 * H]) for b in range(B)]
        feat = [sb(f"feat{b}", [P, 2 * H, M]) for b in range(B)]
        featT = [sb(f"featT{b}", [P, 2 * H, P]) for b in range(B)]
        kfeat = [sb(f"kfeat{b}", [P, H, M]) for b in range(B)]
        vext = [sb(f"vext{b}", [P, H, NV]) for b in range(B)]
        att = [sb(f"att{b}", [P, H, P]) for b in range(B)]
        state = [sb(f"state{b}", [P, H, NV]) for b in range(B)]
        den = [sb(f"den{b}", [P, H]) for b in range(B)]
        rden = [sb(f"rden{b}", [P, H]) for b in range(B)]
        o_n = [sb(f"o_n{b}", [P, H, DH]) for b in range(B)]
        oT = [sb(f"oT{b}", [P, P]) for b in range(B)]
        yn = [sb(f"yn{b}", [P, TG, P]) for b in range(B)]
        h2T = [sb(f"h2T{b}", [P, TG * P]) for b in range(B)]
        hid = [sb(f"hid{b}", [P, HB, TG * P]) for b in range(B)]
        wmod_sb = hid[0][:, 0:2, :].rearrange("p j n -> p (j n)")[:, 0:6 * P]
        blank = hid[1][:, :, :].rearrange("p j n -> p (j n)")
        o2T = [sb(f"o2T{b}", [P, TG * P]) for b in range(B)]
        x1n = [sb(f"x1n{b}", [P, TG, P]) for b in range(B)]
        h3 = [[sb(f"h3{k}{b}", [P, TG, P]) for b in range(B)] for k in range(G)]
        h3T = [[sb(f"h3T{k}{b}", [P, TG * P]) for b in range(B)] for k in range(G)]
        logit = sb("logit", [P, TT, E])
        prob = sb("prob", [P, TT, E])
        prob2 = sb("prob2", [P, TT, E])
        first8 = sb("first8", [P, TT, E])
        hit = sb("hit", [P, TT, E])
        pick = [sb(f"pick{i}", [P, TT, E]) for i in range(2)]
        top = [sb(f"top{i}", [P, TT]) for i in range(2)]
        hitmax = sb("hitmax", [P, TT])
        topsum = sb("topsum", [P, TT])
        topinv = sb("topinv", [P, TT])
        wts = sb("wts", [P, G, 2, TT])
        sel = sb("sel", [P, TT + 1, E], BF16)
        slotf = sb("slotf", [P, TT, E])
        slotp = sb("slotp", [P, TT, E])
        rowf = sb("rowf", [P, 2, TT])
        rows = sb("rows", [P, G, 2, TT], I32)
        cnt = sb("cnt", [P, E])
        cbase = sb("cbase", [P, E])
        cum = sb("cum", [P, G * TT, E])
        cumi = sb("cumi", [P, G * TT, E], I32)
        tri = sb("tri", [P, P], BF16)
        ones = sb("ones", [P, P], BF16)
        cand = sb("cand", [P, 1], I32)
        cki = sb("cki", [P, 1], I32)
        cf, ck, ce, cvalid, cpos = (sb(n, [P, 1]) for n in ("cf", "ck", "ce", "cvalid", "cpos"))
        iota_e = sb("iota_e", [P, E])
        iota_n = sb("iota_n", [P, NT])
        emask = sb("emask", [P, E])
        ntiles = sb("ntiles", [P, E])
        ntq = sb("ntq", [P, E])
        ntc = sb("ntc", [P, 1])
        cvals = sb("cvals", [P, 2], BF16)
        cv16 = sb("cv16", [P, 1], BF16)
        onehot = sb("onehot", [P, NT], BF16)
        tile_e = sb("tile_e", [1, NT // NBUF], I32)
        tile_row = sb("tile_row", [1, NT // NBUF], I32)
        out_row = sb("out_row", [1, NT // NBUF], I32)
        packed = [sb(f"packed{i}", [1, NT // NBUF]) for i in range(3)]
        tile_blk = sb("tile_blk", [1, NT])
        spare = sb("spare", [1, NT])
        ntail = sb("ntail", [1, NT])
        pad_row = sb("pad_row", [1, E], I32)
        rounds = sb("rounds", [1, G * TT])
        reqm = sb("reqm", [1, G * TT, E])
        reqf = sb("reqf", [1, G * TT])
        req = sb("req", [1, G * TT], I32)
        zeros = sb("zeros", [P, P])
        act = [hid[b][:, 0:IB, :] for b in range(B)]
        sil = [hid[b][:, IB, :] for b in range(B)]
        wgu = [sb(f"wgu_{n}", [P, E, 2 * I], F32R) for n in ("hi", "lo")]
        wdn = [sb(f"wdn_{n}", [P, E, IB * P], F32R) for n in ("hi", "lo")]
        xt = [kfeat[m // 2][:, m % 2, :] for m in range(NBUF)]
        xT = [[sb(f"xT_{n}{m}", [P, P], F32R) for n in ("hi", "lo")] for m in range(NBUF)]
        silt = [feat[m // 2][:, 2 * (m % 2):2 * (m % 2) + 2, :].rearrange("p a n -> p (a n)") for m in range(NBUF)]
        actt = [featT[m // 2][:, 2 * (m % 2):2 * (m % 2) + 2, :].rearrange("p a n -> p (a n)") for m in range(NBUF)]
        aT = [[sb(f"aT_{n}{m}", [P, IB, P], F32R) for n in ("hi", "lo")] for m in range(NBUF)]
        yt = [att[m // 2][:, m % 2, :] for m in range(NBUF)]
        got = [xn_all[:, :, :, :].rearrange("p b c d -> p (b c) d"),
               gate_sb[:, :, :].rearrange("p e (a d) -> p (e a) d", d=P)]
        comb = yn[0]

        bank = [ctx.enter_context(nc.psum_tensor(f"bank{i}", [P, 512], F32)) for i in range(8)]
        bA, bB, bC, bD = ([bank[4 * b + k] for b in range(B)] for k in range(4))

        x_in = [sem(f"x_in{b}") for b in range(B)]
        vec_in, attn_in, mod_in, ffn_in, moe_in = map(sem, ("vec_in", "attn_in", "mod_in", "ffn_in", "moe_in"))
        consts = sem("consts")
        pe_setup = sem("pe_setup")
        setup_used = sem("setup_used")
        silu_done = sem("silu_done")
        silu_bc_done = sem("silu_bc_done")
        mod_ready = sem("mod_ready")
        xn_ready = sem("xn_ready")
        dv = sem("dv")
        pl = sem("pl")
        h_staged = sem("h_staged")
        hT_tr, hT_ready = sem("hT_tr"), sem("hT_ready")
        proj_done, max_ready, feat_ready = sem("proj_done"), sem("max_ready"), sem("feat_ready")
        featT_tr, featT_ready, kfeat_ready = sem("featT_tr"), sem("featT_ready"), sem("kfeat_ready")
        v_done, vext_ready = sem("v_done"), sem("vext_ready")
        att_done, att_ready = sem("att_done"), sem("att_ready")
        o_done, st_done, on_ready = sem("o_done"), sem("st_done"), sem("on_ready")
        oT_tr, oT_ready, wo_done, y_ready = sem("oT_tr"), sem("oT_ready"), sem("wo_done"), sem("y_ready")
        den_ready, rden_ready = sem("den_ready"), sem("rden_ready")
        dv2 = sem("dv2")
        dvc = sem("dvc")
        yn_ready, h2T_tr, h2T_ready = sem("yn_ready"), sem("h2T_tr"), sem("h2T_ready")
        w1_done, hid_a, hid_v = sem("w1_done"), sem("hid_a"), sem("hid_v")
        w2_done, o2T_ready, o2_tr, x1_ready = sem("w2_done"), sem("o2T_ready"), sem("o2_tr"), sem("x1_ready")
        x1n_ready, h3_mul, h3_ready, h3T_tr, h3T_ready = (sem(n) for n in ("x1n_ready", "h3_mul", "h3_ready", "h3T_tr", "h3T_ready"))
        logit_done, logit_ready, prob_ready = sem("logit_done"), sem("logit_ready"), sem("prob_ready")
        sel_ready, rank_done, rows_ready = sem("sel_ready"), sem("rank_done"), sem("rows_ready")
        cv_ready, cpos_done, onehot_ready, tab_done, tab_ready = (sem(n) for n in ("cv_ready", "cpos_done", "onehot_ready", "tab_done", "tab_ready"))
        blank_ready, blanked = sem("blank_ready"), sem("blanked")
        scattered, padded, zeros_ready, req_ready = sem("scattered"), sem("padded"), sem("zeros_ready"), sem("req_ready")
        wsplit = sem("wsplit")
        g_done, sil_ready, act_ready = sem("g_done"), sem("sil_ready"), sem("act_ready")
        ysh_done, base_ready = sem("ysh_done"), sem("base_ready")
        xt_in = [sem(f"xt_in{m}") for m in range(NBUF)]
        xT_tr, xhi_ready, xlo_ready = sem("xT_tr"), sem("xhi_ready"), sem("xlo_ready")
        gu_done, silt_ready, actt_ready = sem("gu_done"), sem("silt_ready"), sem("actt_ready")
        aT_tr, ahi_ready, alo_ready = sem("aT_tr"), sem("ahi_ready"), sem("alo_ready")
        yt_done, yt_ready = sem("yt_done"), sem("yt_ready")
        yt_out = [sem(f"yt_out{m}") for m in range(NBUF)]
        landed = sem("landed")
        gathered = [sem(f"gathered{i}") for i in range(G * TT)]
        fin_ready, stored = sem("fin_ready"), sem("stored")

        block = ctx.enter_context(nc.Block())
        RK = 64
        SC = 192
        XB = [6, 7, 6]

        def pipeline(eng, s0, s1, s2, s3):
            s0(0, 0, 0)
            s0(1, 1, 0), s1(0, 0)
            s0(2, 2, 0), s1(1, 1), s2(0, 0)
            with eng.Fori(0, NT // NBUF - 1) as i:
                for m in range(NBUF):
                    n = i * NBUF + m
                    s0(n + 3, m, i + 1)
                    s1(n + 2, (m + 2) % NBUF)
                    s2(n + 1, (m + 1) % NBUF)
                    s3(n, m, i)
            n = NT - NBUF
            s1(n + 2, 2), s2(n + 1, 1), s3(n, 0, n // NBUF)
            s2(n + 2, 2), s3(n + 1, 1, n // NBUF)
            s3(n + 2, 2, n // NBUF)

        @block.sync
        def _(sp):
            sp.dma_start(vec_rows[0:2, :], c).then_inc(vec_in, 16)
            sp.dma_start(vec_rows[2:3, :], gamma.rearrange("(a n) -> a n", a=1)).then_inc(vec_in, 16)
            sp.dma_start(vec_rows[3:4, :], beta.rearrange("(a n) -> a n", a=1)).then_inc(vec_in, 16)
            sp.dma_start(vec_rows[4:5, :], b2.rearrange("(a n) -> a n", a=1)).then_inc(vec_in, 16)
            sp.dma_start(vec_rows[5:5 + HB, :], b1.rearrange("(a n) -> a n", n=P)).then_inc(vec_in, 16)
            sp.dma_start(vec_rows[5 + HB:5 + HB + E, :], router_w).then_inc(vec_in, 16)
            for b in range(B):
                sp.dma_start(x_all[:, b, :, :], x[b].rearrange("(c p) d -> p c d", p=P)).then_inc(x_in[b], 16)
            sp.dma_start(w1_sb[:, :, :], w1.rearrange("d (j n) -> d j n", n=P)).then_inc(ffn_in, 16)
            sp.dma_start(w2_sb[:, :, :], w2.rearrange("(j p) n -> p j n", p=P)).then_inc(ffn_in, 16)
            sp.dma_start(gate_sb[:, :, :], gate_w.rearrange("e h i -> h e i")).then_inc(moe_in, 16)
            sp.dma_start(up_sb[:, :, :], up_w.rearrange("e h i -> h e i")).then_inc(moe_in, 16)
            sp.dma_start(down_sb[:, :, :, :], down_w.rearrange("e (j p) n -> p e j n", p=P)).then_inc(moe_in, 16)
            sp.wait_ge(blank_ready, 1)
            for r0 in range(0, YB, YN):
                sp.dma_start(ydisp[r0 * P:(r0 + YN) * P, :].rearrange("(p r) d -> p (r d)", p=P),
                             blank).then_inc(blanked, 16)
            sp.wait_ge(zeros_ready, 1)
            sp.dma_start(xdisp[E * RB * P:(E * RB + 1) * P, :], zeros[:, :]).then_inc(padded, 16)
            sp.wait_ge(tab_ready, 1)
            with sp.Fori(0, E) as e:
                r = sp.value_load(pad_row[0:1, bass.ds(e, 1)], min_val=0, max_val=E * RB * P - P)
                sp.dma_start(xdisp[bass.ds(r, P), :], zeros[:, :]).then_inc(padded, 16)

            def tile_rows(table, i):
                w = sp.value_load(table[0:1, bass.ds(i, 1)], min_val=0, max_val=BW ** NBUF - 1)
                return [(w // BW ** j) % BW * P for j in range(NBUF)]

            def load(row, m):
                sp.dma_start(xt[m], xdisp[bass.ds(row, P), :]).then_inc(xt_in[m], 16)

            def store(j, m, row):
                sp.wait_ge(yt_ready, j + 2)
                sp.dma_start(ydisp[bass.ds(row, P), :], yt[m]).then_inc(yt_out[m], 16)

            for m in range(NBUF):
                sp.sem_inc(yt_out[m], 16)
            sp.sem_inc(yt_ready, 1)
            sp.wait_ge(scattered, 16 * 2 * G * TT)
            sp.wait_ge(padded, 16 * (E + 1))
            sp.wait_ge(blanked, 16 * YB // YN)
            first = tile_rows(tile_row, 0)
            for m in range(NBUF):
                load(first[m], m)
            second = tile_rows(tile_row, 1)
            for m in range(NBUF):
                sp.wait_ge(xT_tr, m + 1)
                load(second[m], m)

            def results(i, m, row):
                store(i * NBUF + m, m, row)
                last = (m - 1) % NBUF
                sp.wait_ge(yt_out[last], i * 16 + (32 if m else 16))
                sp.sem_inc(landed, 1)

            with sp.Fori(0, NT // NBUF - 2) as i:
                ahead = tile_rows(tile_row, i + 2)
                now = tile_rows(out_row, i)
                for m in range(NBUF):
                    sp.wait_ge(xT_tr, (i + 1) * NBUF + m + 1)
                    load(ahead[m], m)
                    results(i, m, now[m])
            for i in range(NT // NBUF - 2, NT // NBUF):
                now = tile_rows(out_row, i)
                for m in range(NBUF):
                    results(i, m, now[m])
            sp.wait_ge(yt_out[NBUF - 1], 16 * (NT // NBUF + 1))
            sp.sem_inc(landed, 1)
            for u in range(U):
                k, b = divmod(u, B)
                sp.wait_ge(fin_ready, u + 1)
                sp.dma_start(out[b].rearrange("(c p) d -> p c d", p=P)[:, k * TG:(k + 1) * TG, :],
                             h_all[:, b, k * TG:(k + 1) * TG, :]).then_inc(stored, 16)
            sp.wait_ge(stored, 16 * U)

        @block.gpsimd
        def _(pool):
            nc.gpsimd.memset(blank, 0.0).then_inc(blank_ready, 1)
            nc.gpsimd.memset(ident[:, :], 0.0).then_inc(pl, 1)
            nc.gpsimd.memset(causal[:, :, :], 1.0).then_inc(pl, 1)
            nc.gpsimd.memset(tri[:, :], 1.0).then_inc(pl, 1)
            pool.wait_ge(pl, 3)
            nc.gpsimd.affine_select(out=ident[:, :], in_=ident[:, :], compare_op=ALU.not_equal, fill=1.0,
                                    base=0, pattern=[[-1, P]], channel_multiplier=1).then_inc(consts, 1)
            nc.gpsimd.affine_select(out=causal[:, :, :], in_=causal[:, :, :], compare_op=ALU.is_ge, fill=0.0,
                                    base=0, pattern=[[0, H], [1, P]], channel_multiplier=-1).then_inc(consts, 1)

            nc.gpsimd.affine_select(out=tri[:, :], in_=tri[:, :], compare_op=ALU.is_gt, fill=0.0,
                                    base=0, pattern=[[1, P]], channel_multiplier=-1)
            nc.gpsimd.iota(first8[:, :, :], pattern=[[0, TT], [-1, E]], base=E, channel_multiplier=0,
                           allow_small_or_imprecise_dtypes=True)
            nc.gpsimd.iota(iota_e[:, :], pattern=[[1, E]], base=0, channel_multiplier=0,
                           allow_small_or_imprecise_dtypes=True)
            nc.gpsimd.iota(iota_n[:, :], pattern=[[1, NT]], base=0, channel_multiplier=0,
                           allow_small_or_imprecise_dtypes=True)
            nc.gpsimd.iota(cbase[:, :], pattern=[[RB * P, E]], base=0, channel_multiplier=0,
                           allow_small_or_imprecise_dtypes=True)
            nc.gpsimd.iota(cand[:, :], pattern=[[0, 1]], base=0, channel_multiplier=1)
            nc.gpsimd.memset(ones[:, :], 1.0)
            nc.gpsimd.memset(sel[:, :, :], 0.0)
            nc.gpsimd.memset(cnt[:, :], 0.0)
            nc.gpsimd.memset(zeros[:, :], 0.0).then_inc(zeros_ready, 1)

            def stage(ci, first=False):
                for b in range(B):
                    nc.gpsimd.tensor_tensor(hmul[b][:, :], xn_all[:, b, bass.ds(ci, 1), :], mod[:, b, 1, :],
                                            ALU.mult).then_inc(pl, 1)
                    pool.wait_ge(pl, ci * 2 * B + 2 * b + 4)
                    nc.gpsimd.tensor_tensor(h_all[:, b, bass.ds(ci, 1), :], hmul[b][:, :], mod[:, b, 0, :],
                                            ALU.add).then_inc(pl, 1)
                    if not first:
                        pool.wait_ge(hT_tr, ci * B + b - B + 1)
                    nc.gpsimd.tensor_tensor(hst[b][:, :], hmul[b][:, :], mod[:, b, 0, :],
                                            ALU.add).then_inc(h_staged, 1)

            pool.wait_ge(xn_ready, 1)
            pool.wait_ge(mod_ready, 1)
            stage(0, first=True)
            with pool.Fori(1, C) as ci:
                stage(ci)
            pool.wait_ge(moe_in, 48)
            with pool.Fori(0, E) as e:
                parts = [(wgu, 0, I, gate_sb[:, bass.ds(e, 1), :]), (wgu, I, 2 * I, up_sb[:, bass.ds(e, 1), :]),
                         (wdn, 0, IB * P, down_sb[:, bass.ds(e, 1), :, :])]
                for w, lo, hi, src in parts:
                    nc.gpsimd.tensor_copy(w[0][:, bass.ds(e, 1), lo:hi], src).then_inc(wsplit, 1)
                pool.wait_ge(wsplit, e * 6 + 3)
                for w, lo, hi, src in parts:
                    nc.gpsimd.tensor_tensor(w[1][:, bass.ds(e, 1), lo:hi], src,
                                            w[0][:, bass.ds(e, 1), lo:hi].bitcast(F32),
                                            ALU.subtract).then_inc(wsplit, 1)
            for k in range(G):
                for b in range(B):
                    pool.wait_ge(x1n_ready, k * B + b + 1)
                    nc.gpsimd.tensor_tensor(h3[k][b][:, :, :], x1n[b][:, :, :],
                                            mod[:, b, 4, :].unsqueeze(1).to_broadcast([P, TG, P]),
                                            ALU.mult).then_inc(h3_mul, 1)
                    pool.wait_ge(h3_mul, k * B + b + 1)
                    nc.gpsimd.tensor_tensor(h3[k][b][:, :, :], h3[k][b][:, :, :],
                                            mod[:, b, 3, :].unsqueeze(1).to_broadcast([P, TG, P]),
                                            ALU.add).then_inc(h3_ready, 1)
                pool.wait_ge(h3_ready, (k + 1) * B)
                pool.wait_ge(rows_ready, k + 1)
                for t in range(TT):
                    for i in range(2):
                        nc.gpsimd.indirect_dma_start(
                            out=xdisp, out_offset=bass.IndirectOffsetOnAxis(ap=rows[:, k, i, t:t + 1], axis=0),
                            in_=h3[k][t // TG][:, t % TG, :], in_offset=None).then_inc(scattered, 16)
            pool.wait_ge(req_ready, 1)
            for q in range(G * TT):
                n = pool.value_load(req[0:1, q:q + 1], min_val=1, max_val=NT + 1)
                pool.wait_ge(landed, n)
                pool.sem_inc(pl, 1)
                for i in range(2):
                    nc.gpsimd.indirect_dma_start(
                        out=got[i][:, q, :], out_offset=None, in_=ydisp,
                        in_offset=bass.IndirectOffsetOnAxis(ap=rows[:, q // TT, i, q % TT:q % TT + 1], axis=0))\
                        .then_inc(gathered[q], 16)

        @block.scalar
        def _(act_e):
            act_e.dma_start(wmod_sb, wmod).then_inc(mod_in, 16)
            act_e.dma_start(wq_sb[:, :], wq).then_inc(attn_in, 16)
            act_e.dma_start(wk_sb[:, :], wk).then_inc(attn_in, 16)
            act_e.dma_start(om2[:, 0, :], omega).then_inc(attn_in, 16)
            act_e.dma_start(om2[:, 1, :], omega).then_inc(attn_in, 16)
            act_e.dma_start(wv_sb[:, :], wv).then_inc(attn_in, 16)
            act_e.dma_start(wo_sb[:, :], wo).then_inc(attn_in, 16)
            act_e.dma_start(shg_sb[:, :, :], sh_gate.rearrange("(j p) h -> p j h", p=P)).then_inc(attn_in, 16)
            act_e.dma_start(shu_sb[:, :, :], sh_up.rearrange("(j p) h -> p j h", p=P)).then_inc(attn_in, 16)
            act_e.dma_start(shd_sb[:, :, :], sh_down.rearrange("h (j p) -> h j p", p=P)).then_inc(attn_in, 16)
            act_e.dma_start(rbias[:, :], routing_bias.partition_broadcast(P)).then_inc(attn_in, 16)
            act_e.wait_ge(setup_used, 1)
            nc.scalar.activation(silu_c[:, :], vecT[:, 0:B], ACT.Silu).then_inc(silu_done, 1)

            def front_hT(ci):
                for b in range(B):
                    act_e.wait_ge(hT_tr, ci * B + b + 1)
                    nc.scalar.copy(hT[b][:, :], bA[b][:, 0:P]).then_inc(hT_ready, 1)

            def front_exp(ci):
                for b in range(B):
                    act_e.wait_ge(max_ready, ci * B + b + 1)
                    for j in range(2 * H):
                        a = nc.scalar.activation(feat[b][:, j, :], bB[b][:, j * M:(j + 1) * M], ACT.Exp,
                                                 bias=negmax[b][:, j:j + 1])
                    a.then_inc(feat_ready, 1)

            def front_v(ci):
                for b in range(B):
                    act_e.wait_ge(v_done, ci * B + b + 1)
                    nc.scalar.copy(vext[b][:, :, 0:DH],
                                   bD[b][:, 2 * P:3 * P].rearrange("p (h d) -> p h d", h=H)).then_inc(vext_ready, 1)

            def back(ci):
                for b in range(B):
                    act_e.wait_ge(oT_tr, ci * B + b + 1)
                    nc.scalar.copy(oT[b][:, :], bB[b][:, 0:P]).then_inc(oT_ready, 1)

            def front(ci):
                front_hT(ci)
                front_exp(ci)
                front_v(ci)

            front(0)
            front(1)
            with act_e.Fori(1, C - 1) as ci:
                back(ci - 1)
                front(ci + 1)
            back(C - 2)
            back(C - 1)

            def h2T_copy(k, b):
                act_e.wait_ge(h2T_tr, k * B + b + 1)
                nc.scalar.activation(h2T[b][:, :], bA[b][:, :], ACT.Identity, bias=vecT[:, 3:4],
                                     scale=vecT[:, 2:3]).then_inc(h2T_ready, 1)

            def relu(k, b):
                if k == 0 and b == 1:
                    act_e.wait_ge(blanked, 16 * YB // YN)
                for j in range(0, HB, 2):
                    act_e.wait_ge(w1_done, (k * B + b) * HB + j + 1)
                    nc.scalar.activation(hid[b][:, j, :], [bB, bC, bD, bB][j][b][:, :], ACT.Relu,
                                         bias=vecT[:, 5 + j:6 + j]).then_inc(hid_a, 1)

            def o2T_copy(k, b):
                act_e.wait_ge(w2_done, k * B + b + 1)
                nc.scalar.activation(o2T[b][:, :], bA[b][:, :], ACT.Identity, bias=gab2[:, b:b + 1],
                                     scale=ga_col[:, b:b + 1]).then_inc(o2T_ready, 1)

            def h3T_copy(k, b):
                act_e.wait_ge(h3T_tr, k * B + b + 1)
                nc.scalar.copy(h3T[k][b][:, :], bC[b][:, :]).then_inc(h3T_ready, 1)

            def sigmoid(k):
                act_e.wait_ge(logit_ready, k + 1)
                nc.scalar.activation(prob[:, :, :], logit[:, :, :], ACT.Sigmoid).then_inc(prob_ready, 1)

            def shared_silu(k):
                for j in range(IB):
                    for b in range(B):
                        n = (k * IB + j) * B + b
                        act_e.wait_ge(g_done, n + 1)
                        if n >= B:
                            act_e.wait_ge(act_ready, n - B + 1)
                        nc.scalar.activation(sil[b], bA[b][:, :], ACT.Silu).then_inc(sil_ready, 1)

            for k in range(G):
                for step in (h2T_copy, relu, o2T_copy):
                    if k and step is o2T_copy:
                        for b in range(B):
                            h3T_copy(k - 1, b)
                        sigmoid(k - 1)
                    for b in range(B):
                        step(k, b)
            shared_silu(0)
            for b in range(B):
                h3T_copy(G - 1, b)
            sigmoid(G - 1)
            shared_silu(1)

            def xhi(n, m, turn):
                act_e.wait_ge(xT_tr, n + 1)
                nc.scalar.copy(xT[m][0][:, :], bank[XB[m]][:, 0:P]).then_inc(xhi_ready, 1)

            def silu(n, m):
                act_e.wait_ge(gu_done, n + 1)
                nc.scalar.activation(silt[m], bank[m][:, 0:I], ACT.Silu).then_inc(silt_ready, 1)

            def ahi(n, m):
                act_e.wait_ge(aT_tr, n + 1)
                nc.scalar.copy(aT[m][0][:, :, :], bank[3 + m][:, 0:IB * P]).then_inc(ahi_ready, 1)

            def yout(n, m, turn):
                act_e.wait_ge(yt_done, n + 1)
                act_e.wait_ge(yt_out[m], turn * 16 + 16)
                nc.scalar.copy(yt[m], bank[3 + m][:, IB * P:(IB + 1) * P]).then_inc(yt_ready, 1)

            pipeline(act_e, xhi, silu, ahi, yout)

        @block.vector
        def _(dve):
            V = nc.vector
            count = [0]

            def link(ins):
                ins.then_inc(dv, 1)
                count[0] += 1
                dve.wait_ge(dv, count[0])

            def moments(st, mn, vr, chain, u, v_, w):
                V.tensor_tensor(mn, st[:, :, :, 1], st[:, :, :, 4], ALU.add)
                V.tensor_tensor(u, st[:, :, :, 1], st[:, :, :, 4], ALU.subtract)
                chain(V.tensor_tensor(v_, st[:, :, :, 2], st[:, :, :, 5], ALU.add))
                V.tensor_scalar(mn, mn, 0.5, None, ALU.mult)
                chain(V.scalar_tensor_tensor(w, u, 0.25, u, ALU.mult, ALU.mult))
                chain(V.scalar_tensor_tensor(vr, v_, 1.0 / P, w, ALU.mult, ALU.add))

            def rsqrt(r, v_, eps, chain, u, w, t):
                chain(V.tensor_scalar(w, v_, eps, None, ALU.add))
                chain(V.tensor_scalar(u.bitcast(I32), w.bitcast(I32), 1, None, ALU.logical_shift_right))
                chain(V.tensor_scalar(r.bitcast(I32), u.bitcast(I32), -1.0, float(0x5F3759DF), ALU.mult, ALU.add))
                for _ in range(4):
                    chain(V.tensor_tensor(u, r, r, ALU.mult))
                    chain(V.scalar_tensor_tensor(t, u, -0.5, w, ALU.mult, ALU.mult))
                    chain(V.scalar_tensor_tensor(r, t, 1.5, r, ALU.add, ALU.mult))

            L = lambda t: t[:, :, :]
            V.memset(vext[0][:, :, DH:NV], 1.0)
            V.memset(vext[1][:, :, DH:NV], 1.0)
            V.memset(state[0][:, :, :], 0.0)
            V.memset(state[1][:, :, :], 0.0)
            for b in range(B):
                dve.wait_ge(x_in[b], 16)
                for ci in range(C):
                    V.bn_stats(stats[:, b, ci, :], x_all[:, b, ci, :]).then_inc(dv, 1)
                    count[0] += 1
            dve.wait_ge(dv, count[0])
            dve.wait_ge(pe_setup, 1)
            V.tensor_copy(vecT[:, :], bank[0][:, 0:5 + HB + E]).then_inc(setup_used, 1)
            moments(stats, L(mean), L(var), link, L(lt[0]), L(lt[1]), L(lt[2]))
            rsqrt(L(rstd), L(var), LN_EPS, link, L(lt[0]), L(lt[1]), L(lt[2]))
            for b in range(B):
                for ci in range(C):
                    last = V.tensor_scalar(xn_all[:, b, ci, :], x_all[:, b, ci, :], mean[:, b, ci:ci + 1],
                                           rstd[:, b, ci:ci + 1], ALU.subtract, ALU.mult)
            last.then_inc(xn_ready, 1)
            dve.wait_ge(silu_done, 1)
            for b in range(B):
                last = V.tensor_copy(silu_bc[:, b, :], silu_c[:, b:b + 1].to_broadcast([P, P]))
            last.then_inc(silu_bc_done, 1)
            dve.wait_ge(pe_setup, 2)
            V.tensor_copy(wqT[:, :], bank[1][:, 0:P])
            V.tensor_copy(wkT[:, :], bank[1][:, P:2 * P])
            V.tensor_copy(om2T[:, :], bank[1][:, 2 * P:3 * P]).then_inc(setup_used, 1)
            V.tensor_copy(shgT[:, :], bank[2][:, 0:I])
            V.tensor_copy(shuT[:, :], bank[2][:, I:2 * I])
            V.tensor_copy(shdT[:, :, :], bank[3][:, 0:I])
            dve.wait_ge(pe_setup, 3)
            for h in range(H):
                last = V.tensor_scalar(wproj[:, h:2 * H:H, :], bank[4 + 2 * h][:, 0:2 * M].rearrange(
                    "p (j m) -> p j m", m=M), QK_SCALE, None, ALU.mult)
            last.then_inc(setup_used, 1)
            dve.wait_ge(pe_setup, 4)
            V.tensor_copy(mod[:, 0, 0:4, :], bank[0][:, :])
            V.tensor_copy(mod[:, 0, 4:6, :], bank[1][:, 0:2 * P])
            V.tensor_copy(mod[:, 1, 0:4, :], bank[2][:, :])
            link(V.tensor_copy(mod[:, 1, 4:6, :], bank[3][:, 0:2 * P]))
            link(V.tensor_copy(ga_col[:, :], bank[5][:, 0:B]))
            V.tensor_scalar(mod[:, :, 1, :], mod[:, :, 1, :], 1.0, None, ALU.add)
            V.tensor_scalar(mod[:, :, 4, :], mod[:, :, 4, :], 1.0, None, ALU.add)
            link(V.scalar_tensor_tensor(ga_abs[:, :], ga_col[:, :], -1.0, ga_col[:, :], ALU.mult, ALU.max))
            V.tensor_scalar(ga_abs[:, :], ga_abs[:, :], 0.25, None, ALU.max)
            V.tensor_scalar(gsign[:, :, :], mod[:, :, 5, :], 0.0, 2.0, ALU.is_ge, ALU.mult)
            link(V.tensor_scalar(ga_col[:, :], ga_col[:, :], 0.0, 2.0, ALU.is_ge, ALU.mult))
            link(V.scalar_tensor_tensor(mod[:, :, 5, :], mod[:, :, 5, :], -1.0, mod[:, :, 5, :], ALU.mult, ALU.max))
            link(V.tensor_scalar(mod[:, :, 5, :], mod[:, :, 5, :], 0.25, None, ALU.max))
            V.scalar_tensor_tensor(ga_col[:, :], ga_col[:, :], -1.0, ga_abs[:, :], ALU.add, ALU.mult)
            link(V.scalar_tensor_tensor(mod[:, :, 5, :], gsign[:, :, :], -1.0, mod[:, :, 5, :], ALU.add, ALU.mult))
            V.tensor_scalar(gab2[:, :], ga_col[:, :], vecT[:, 4:5], None, ALU.mult).then_inc(mod_ready, 1)

            def front_max(ci):
                for b in range(B):
                    dve.wait_ge(proj_done, ci * B + b + 1)
                    V.tensor_reduce(negmax[b][:, :], bB[b][:, :].rearrange("p (j m) -> p j m", m=M), AX.X,
                                    ALU.max, negate=True).then_inc(max_ready, 1)

            def back_feat(ci):
                for b in range(B):
                    dve.wait_ge(featT_tr, ci * B + b + 1)
                    V.tensor_scalar(featT[b][:, :, :], bC[b][:, :], INV_SQRT_M, FEAT_EPS, ALU.mult,
                                    ALU.add).then_inc(featT_ready, 1)
                    V.tensor_scalar(kfeat[b][:, :, :], feat[b][:, H:2 * H, :], INV_SQRT_M, FEAT_EPS, ALU.mult,
                                    ALU.add).then_inc(kfeat_ready, 1)

            def back_mask(ci):
                for b in range(B):
                    dve.wait_ge(att_done, ci * B + b + 1)
                    V.tensor_tensor(att[b][:, :, :], bD[b][:, 0:H * P], causal[:, :, :], ALU.mult)\
                        .then_inc(att_ready, 1)

            def back_out(ci):
                for b in range(B):
                    o = bA[b][:, 2 * P:2 * P + H * NV].rearrange("p (h n) -> p h n", h=H)
                    dve.wait_ge(o_done, ci * B + b + 1)
                    V.tensor_scalar(den[b][:, :], o[:, :, DH], FEAT_EPS, None, ALU.add).then_inc(den_ready, 1)
                    dve.wait_ge(den_ready, ci * B + b + 1)
                    V.reciprocal(rden[b][:, :], den[b][:, :]).then_inc(rden_ready, 1)
                    dve.wait_ge(st_done, ci * B + b + 1)
                    V.tensor_tensor(state[b][:, :, :], bC[b][:, 0:H * NV], state[b][:, :, :], ALU.add)
                    dve.wait_ge(rden_ready, ci * B + b + 1)
                    V.tensor_tensor(o_n[b][:, :, :], o[:, :, 0:DH],
                                    rden[b][:, :].unsqueeze(2).to_broadcast([P, H, DH]), ALU.mult)\
                        .then_inc(on_ready, 1)
            def back_y(ci):
                for b in range(B):
                    dve.wait_ge(wo_done, ci * B + b + 1)
                    V.tensor_tensor(h_all[:, b, bass.ds(ci, 1), :], bB[b][:, P:2 * P],
                                    h_all[:, b, bass.ds(ci, 1), :], ALU.add).then_inc(y_ready, 1)

            def back_stats(ci):
                dve.wait_ge(y_ready, (ci + 1) * B)
                V.memset(lt[0][0:1, 0, 0:1], 0.0)
                for b in range(B):
                    V.bn_stats(stats[:, b, bass.ds(ci, 1), :], h_all[:, b, bass.ds(ci, 1), :]).then_inc(dv2, 1)

            front_max(0)
            back_feat(0)
            back_mask(0)
            front_max(1)
            back_out(0)
            with dve.Fori(1, C - 1) as ci:
                back_feat(ci)
                back_y(ci - 1)
                back_mask(ci)
                back_stats(ci - 1)
                front_max(ci + 1)
                back_out(ci)
            back_feat(C - 1)
            back_y(C - 2)
            back_mask(C - 1)
            back_stats(C - 2)
            back_out(C - 1)
            back_y(C - 1)
            back_stats(C - 1)
            dve.wait_ge(dv2, B * C)
            moments(stats, L(mean), L(var), link, L(lt[0]), L(lt[1]), L(lt[2]))
            rsqrt(L(rstd), L(var), ATTN_LN_EPS, link, L(lt[0]), L(lt[1]), L(lt[2]))

            count2 = [0]

            def chain(ins):
                ins.then_inc(dvc, 1)
                count2[0] += 1
                dve.wait_ge(dvc, count2[0])

            def normalise2(k):
                for b in range(B):
                    if k:
                        dve.wait_ge(h2T_tr, (k - 1) * B + b + 1)
                    for j in range(TG):
                        c_ = k * TG + j
                        last = V.tensor_scalar(yn[b][:, j, :], h_all[:, b, c_, :], mean[:, b, c_:c_ + 1],
                                               rstd[:, b, c_:c_ + 1], ALU.subtract, ALU.mult)
                    last.then_inc(yn_ready, 1)

            def relu(k):
                for b in range(B):
                    if k == 0 and b == 1:
                        dve.wait_ge(blanked, 16 * YB // YN)
                    for j in range(1, HB, 2):
                        dve.wait_ge(w1_done, (k * B + b) * HB + j + 1)
                        V.tensor_scalar(hid[b][:, j, :], [bB, bC, bD, bB][j][b][:, :], vecT[:, 5 + j:6 + j], 0.0,
                                        ALU.add, ALU.max).then_inc(hid_v, 1)

            def residual1(k):
                for b in range(B):
                    xs = x_all[:, b, k * TG:(k + 1) * TG, :]
                    dve.wait_ge(o2_tr, k * B + b + 1)
                    V.tensor_tensor(xs, bB[b][:, :].rearrange("p (t d) -> p t d", d=P), xs, ALU.add)\
                        .then_inc(x1_ready, 1)
                for b in range(B):
                    dve.wait_ge(x1_ready, k * B + b + 1)
                    for j in range(TG):
                        last = V.bn_stats(stats3[:, b, j, :], x_all[:, b, k * TG + j, :])
                chain(last)
                moments(stats3, L(l3[0]), L(l3[1]), chain, L(l3[2]), L(l3[4]), L(l3[3]))
                rsqrt(L(l3[2]), L(l3[1]), LN_EPS, chain, L(l3[3]), L(l3[4]), L(l3[5]))
                for b in range(B):
                    if k:
                        dve.wait_ge(h3_ready, (k - 1) * B + b + 1)
                    for j in range(TG):
                        last = V.tensor_scalar(x1n[b][:, j, :], x_all[:, b, k * TG + j, :],
                                               l3[0][:, b, j:j + 1], l3[2][:, b, j:j + 1],
                                               ALU.subtract, ALU.mult)
                    last.then_inc(x1n_ready, 1)

            def tiles(t):
                return t[:, :].unsqueeze(2).to_broadcast([P, TT, E])

            def experts(t):
                return t[:, :].unsqueeze(1).to_broadcast([P, TT, E])

            def first_of(p_ap, top_, onehot_):
                chain(V.tensor_reduce(top_[:, :], p_ap, AX.X, ALU.max))
                chain(V.tensor_tensor(L(hit), p_ap, tiles(top_), ALU.is_equal))
                chain(V.tensor_tensor(L(hit), L(hit), L(first8), ALU.mult))
                chain(V.tensor_reduce(hitmax[:, :], L(hit), AX.X, ALU.max))
                chain(V.tensor_tensor(L(onehot_), L(hit), tiles(hitmax), ALU.is_equal))

            def logits(k):
                for b in range(B):
                    dve.wait_ge(logit_done, k * B + b + 1)
                    last = V.tensor_tensor(logit[:, b * TG:(b + 1) * TG, :],
                                           bD[b][:, 0:TG * E].rearrange("p (t e) -> p t e", e=E),
                                           rbias[:, :].unsqueeze(1).to_broadcast([P, TG, E]), ALU.add)
                last.then_inc(logit_ready, 1)

            def choose(k):
                dve.wait_ge(prob_ready, k + 1)
                first_of(L(prob), top[0], pick[0])
                chain(V.scalar_tensor_tensor(L(prob2), L(pick[0]), -2.0, L(prob), ALU.mult, ALU.add))
                first_of(L(prob2), top[1], pick[1])
                V.tensor_tensor(sel[:, 0:TT, :], L(pick[0]), L(pick[1]), ALU.add).then_inc(sel_ready, 1)
                chain(V.tensor_tensor(topsum[:, :], top[0][:, :], top[1][:, :], ALU.add))
                chain(V.reciprocal(topinv[:, :], topsum[:, :]))
                for i in range(2):
                    V.tensor_tensor(wts[:, k, i, :], top[i][:, :], topinv[:, :], ALU.mult)

            def place(k):
                dve.wait_ge(rank_done, k + 1)
                rk = bD[0][:, RK:RK + (TT + 1) * E].rearrange("p (t e) -> p t e", e=E)
                chain(V.tensor_tensor(L(slotf), rk[:, 0:TT, :], experts(cbase), ALU.add))
                for i in range(2):
                    chain(V.tensor_tensor(L(slotp), L(pick[i]), L(slotf), ALU.mult))
                    chain(V.tensor_reduce(rowf[:, i, :], L(slotp), AX.X, ALU.add))
                V.tensor_tensor(cum[:, k * TT:(k + 1) * TT, :], rk[:, 1:TT + 1, :], experts(cnt), ALU.add)
                chain(V.tensor_tensor(cbase[:, :], cbase[:, :], rk[:, TT, :], ALU.add))
                chain(V.tensor_tensor(cnt[:, :], cnt[:, :], rk[:, TT, :], ALU.add))
                V.tensor_copy(rows[:, k, :, :], rowf[:, :, :]).then_inc(rows_ready, 1)

            def schedule():
                chain(V.tensor_scalar(cum[:, :, :], cum[:, :, :], float(P - 1), None, ALU.add))
                chain(V.tensor_copy(cumi[:, :, :], cum[:, :, :]))
                chain(V.tensor_scalar(cumi[:, :, :], cumi[:, :, :], 7, None, ALU.logical_shift_right))
                chain(V.tensor_copy(cum[:, :, :], cumi[:, :, :]))
                V.tensor_copy(pad_row[:, :], cbase[0:1, :])
                chain(V.tensor_copy(ntiles[:, :], cum[:, G * TT - 1, :]))
                chain(V.tensor_tensor(ntq[:, :], ntiles[:, :], emask[:, :], ALU.mult))
                chain(V.tensor_reduce(ntc[:, :], ntq[:, :], AX.X, ALU.add))
                chain(V.tensor_tensor(cvalid[:, :], ntc[:, :], ck[:, :], ALU.is_gt))
                V.tensor_copy(cv16[:, :], cvalid[:, :]).then_inc(cv_ready, 1)
                shared_mul(1, 1)
                dve.wait_ge(cpos_done, 1)
                chain(V.tensor_copy(cpos[:, :], bD[0][:, SC:SC + 1]))
                V.tensor_scalar(onehot[:, :], iota_n[:, :], cpos[:, :], cvalid[:, :], ALU.is_equal,
                                ALU.mult).then_inc(onehot_ready, 1)
                chain(V.tensor_reduce(rounds[:, :], cum[0:1, :, :], AX.X, ALU.max))
                chain(V.tensor_tensor(reqm[:, :, :], rounds[:, :].unsqueeze(2).to_broadcast([1, G * TT, E]),
                                      ntiles[0:1, :].unsqueeze(1).to_broadcast([1, G * TT, E]), ALU.min))
                chain(V.tensor_reduce(reqf[:, :], reqm[:, :, :], AX.X, ALU.add))
                V.tensor_scalar(req[:, :], reqf[:, :], 1.0, None, ALU.add).then_inc(req_ready, 1)
                dve.wait_ge(tab_done, 1)
                def pack(w, vals, base):
                    v = vals.rearrange("a (i m) -> a i m", m=NBUF)
                    chain(V.scalar_tensor_tensor(w[:, :], v[:, :, 2], float(base), v[:, :, 1], ALU.mult, ALU.add))
                    chain(V.scalar_tensor_tensor(w[:, :], w[:, :], float(base), v[:, :, 0], ALU.mult, ALU.add))

                nturns = NT // NBUF
                V.tensor_scalar(tile_blk[:, 0:NT], bD[0][0:1, SC + 1 + NT:SC + 1 + 2 * NT], float(E * RB), None,
                                ALU.add)
                chain(V.tensor_copy(spare[:, :], bD[0][0:1, SC + 1:SC + 1 + NT]))
                pack(packed[0], spare[:, :], E)
                V.scalar_tensor_tensor(tile_e[:, 0:nturns - 1], packed[0][:, 1:nturns], float(E ** NBUF),
                                       packed[0][:, 0:nturns - 1], ALU.mult, ALU.add)
                V.tensor_copy(tile_e[:, nturns - 1:nturns], packed[0][:, nturns - 1:nturns])
                pack(packed[1], tile_blk[:, :], BW)
                V.tensor_copy(tile_row[:, :], packed[1][:, :])
                chain(V.tensor_scalar(spare[:, :], tile_blk[:, :], float(E * RB), None, ALU.is_equal))
                chain(V.tensor_tensor(spare[:, :], spare[:, :], ntail[:, :], ALU.mult))
                chain(V.tensor_tensor(spare[:, :], spare[:, :], tile_blk[:, :], ALU.add))
                pack(packed[2], spare[:, :], BW)
                V.tensor_copy(out_row[:, :], packed[2][:, :]).then_inc(tab_ready, 1)

            def shared_mul(k, j):
                for b in range(B):
                    n = (k * IB + j) * B + b
                    dve.wait_ge(sil_ready, n + 1)
                    V.tensor_tensor(act[b][:, j, :], bC[b][:, :], sil[b], ALU.mult).then_inc(act_ready, 1)

            def shared_out(k, b):
                dve.wait_ge(ysh_done, k * B + b + 1)
                xs = x_all[:, b, k * TG:(k + 1) * TG, :]
                V.tensor_tensor(comb[:, :, :], bB[b][:, :].rearrange("p (t d) -> p t d", d=P),
                                      mod[:, b, 5, :].unsqueeze(1).to_broadcast([P, TG, P]), ALU.mult)\
                    .then_inc(base_ready, 1)
                dve.wait_ge(base_ready, k * B + b + 1)
                chain(V.tensor_tensor(xs, comb[:, :, :], xs, ALU.add))

            V.tensor_scalar(ntail[:, :], iota_n[0:1, :], float(2 * T // P), 0.0, ALU.subtract, ALU.max)
            chain(V.tensor_scalar(cki[:, :], cand[:, :], 3, None, ALU.logical_shift_right))
            V.tensor_copy(cf[:, :], cand[:, :])
            chain(V.tensor_copy(ck[:, :], cki[:, :]))
            chain(V.scalar_tensor_tensor(ce[:, :], ck[:, :], -float(E), cf[:, :], ALU.mult, ALU.add))
            V.tensor_scalar(emask[:, :], iota_e[:, :], ce[:, :], None, ALU.is_equal)
            V.tensor_copy(cvals[:, 0:1], ce[:, :])
            chain(V.scalar_tensor_tensor(cpos[:, :], ce[:, :], float(RB), ck[:, :], ALU.mult, ALU.add))
            chain(V.tensor_scalar(cvals[:, 1:2], cpos[:, :], -float(E * RB), None, ALU.add))

            normalise2(0)
            relu(0)
            normalise2(1)
            residual1(0)
            relu(1)
            logits(0)
            choose(0)
            place(0)
            residual1(1)
            shared_mul(0, 0)
            shared_mul(0, 1)
            shared_out(0, 0)
            shared_out(0, 1)
            logits(1)
            choose(1)
            shared_mul(1, 0)
            place(1)
            schedule()
            shared_out(1, 0)
            shared_out(1, 1)

            def xlo(n, m, turn):
                dve.wait_ge(xhi_ready, n + 1)
                V.tensor_tensor(xT[m][1][:, :], bank[XB[m]][:, 0:P], xT[m][0][:, :].bitcast(F32),
                                ALU.subtract).then_inc(xlo_ready, 1)

            def mul(n, m):
                dve.wait_ge(silt_ready, n + 1)
                V.tensor_tensor(actt[m], bank[m][:, I:2 * I], silt[m], ALU.mult)\
                    .then_inc(actt_ready, 1)

            def alo(n, m):
                dve.wait_ge(ahi_ready, n + 1)
                V.tensor_tensor(aT[m][1][:, :, :], bank[3 + m][:, 0:IB * P].rearrange("p (j n) -> p j n", n=P),
                                aT[m][0][:, :, :].bitcast(F32), ALU.subtract).then_inc(alo_ready, 1)

            pipeline(dve, xlo, mul, alo, lambda n, m, turn: None)

            for u in range(U):
                k, b = divmod(u, B)
                for t in range(TG):
                    q = u * TG + t
                    dve.wait_ge(gathered[q], 32)
                    V.tensor_scalar(comb[:, t, :], got[0][:, q, :], wts[:, k, 0, b * TG + t:b * TG + t + 1], None,
                                    ALU.mult).then_inc(dvc, 1)
                    count2[0] += 1
                dve.wait_ge(dvc, count2[0])
                for t in range(TG):
                    q = u * TG + t
                    last = V.scalar_tensor_tensor(comb[:, t, :], got[1][:, q, :],
                                                  wts[:, k, 1, b * TG + t:b * TG + t + 1], comb[:, t, :],
                                                  ALU.mult, ALU.add)
                chain(last)
                chain(V.tensor_tensor(comb[:, :, :], comb[:, :, :],
                                      mod[:, b, 5, :].unsqueeze(1).to_broadcast([P, TG, P]), ALU.mult))
                V.tensor_tensor(h_all[:, b, k * TG:(k + 1) * TG, :], comb[:, :, :],
                                x_all[:, b, k * TG:(k + 1) * TG, :], ALU.add).then_inc(fin_ready, 1)
                dve.wait_ge(fin_ready, u + 1)

        @block.tensor
        def _(pe):
            def mm(o, lhsT, rhs, start=True, stop=True):
                return nc.tensor.matmul(o, lhsT, rhs, start=start, stop=stop)

            pe.wait_ge(consts, 1)
            pe.wait_ge(vec_in, 16 * 6)
            nv = 5 + HB + E
            nc.tensor.transpose(bank[0][:, 0:nv], vec_rows[:, :], ident[0:nv, 0:nv]).then_inc(pe_setup, 1)
            pe.wait_ge(attn_in, 16 * 10)
            nc.tensor.transpose(bank[1][:, 0:P], wq_sb[:, :], ident[:, :])
            nc.tensor.transpose(bank[1][:, P:2 * P], wk_sb[:, :], ident[:, :])
            for j in range(IB):
                nc.tensor.transpose(bank[2][:, j * P:(j + 1) * P], shg_sb[:, j, :], ident[:, :])
                nc.tensor.transpose(bank[2][:, I + j * P:I + (j + 1) * P], shu_sb[:, j, :], ident[:, :])
                nc.tensor.transpose(bank[3][:, j * P:(j + 1) * P], shd_sb[:, j, :], ident[:, :])
            nc.tensor.transpose(bank[1][:, 2 * P:3 * P], om2[:, :, :].rearrange("p a d -> p (a d)"),
                                ident[:, :]).then_inc(pe_setup, 1)
            pe.wait_ge(setup_used, 2)
            for i, (w, h) in enumerate([(wqT, 0), (wqT, 1), (wkT, 0), (wkT, 1)]):
                last = mm(bank[4 + 2 * h][:, (i // H) * M:(i // H + 1) * M], w[h * DH:(h + 1) * DH, :], om2T[h * DH:(h + 1) * DH, :])
            last.then_inc(pe_setup, 1)
            pe.wait_ge(mod_in, 16)
            pe.wait_ge(silu_bc_done, 1)
            pe.wait_ge(setup_used, 3)
            for b in range(B):
                mm(bank[2 * b][:, :], silu_bc[:, b, :], wmod_sb[:, 0:512])
                mm(bank[2 * b + 1][:, 0:256], silu_bc[:, b, :], wmod_sb[:, 512:768])
            mm(bank[5][:, 0:B], wmod_sb[:, 2 * P:3 * P], silu_c[:, :]).then_inc(pe_setup, 1)
            pe.wait_ge(mod_ready, 1)

            def front_tr(ci):
                for b in range(B):
                    pe.wait_ge(h_staged, ci * B + b + 1)
                    nc.tensor.transpose(bA[b][:, 0:P], hst[b][:, :], ident[:, :]).then_inc(hT_tr, 1)

            def front_proj(ci):
                for b in range(B):
                    pe.wait_ge(hT_ready, ci * B + b + 1)
                    if not isinstance(ci, int) or ci > 1:
                        pe.wait_ge(y_ready, (ci - 2) * B + b + 1)
                    mm(bB[b][:, :], hT[b][:, :], wproj[:, :, :]).then_inc(proj_done, 1)

            def front_v(ci):
                for b in range(B):
                    mm(bD[b][:, 2 * P:3 * P], hT[b][:, :], wv_sb[:, :]).then_inc(v_done, 1)

            def back_tr(ci, first=False, last=False):
                for b in range(B):
                    if not last:
                        pe.wait_ge(feat_ready, ci * B + b + 1)
                    if not first:
                        pe.wait_ge(on_ready, (ci - 1) * B + b + 1)
                        nc.tensor.transpose(bB[b][:, 0:P], o_n[b][:, :, :].rearrange("p h d -> p (h d)"),
                                            ident[:, :]).then_inc(oT_tr, 1)
                    if not last:
                        for j in range(2 * H):
                            tr = nc.tensor.transpose(bC[b][:, j * P:(j + 1) * P], feat[b][:, j, :], ident[:, :])
                        tr.then_inc(featT_tr, 1)

            def back_att(ci):
                for b in range(B):
                    pe.wait_ge(featT_ready, ci * B + b + 1)
                    pe.wait_ge(vext_ready, ci * B + b + 1)
                    for h in range(H):
                        last = mm(bD[b][:, h * P:(h + 1) * P], featT[b][:, H + h, :], featT[b][:, h, :])
                    last.then_inc(att_done, 1)

            def back_o(ci):
                for b in range(B):
                    pe.wait_ge(att_ready, ci * B + b + 1)
                    pe.wait_ge(kfeat_ready, ci * B + b + 1)
                    for h in range(H):
                        o = bA[b][:, 2 * P + h * NV:2 * P + (h + 1) * NV]
                        mm(o, featT[b][:, h, :], state[b][:, h, :], stop=False)
                        last = mm(o, att[b][:, h, :], vext[b][:, h, :], start=False)
                    last.then_inc(o_done, 1)
                    for h in range(H):
                        last = mm(bC[b][:, h * NV:(h + 1) * NV], kfeat[b][:, h, :], vext[b][:, h, :])
                    last.then_inc(st_done, 1)

            def back_wo(ci):
                for b in range(B):
                    pe.wait_ge(oT_ready, ci * B + b + 1)
                    mm(bB[b][:, P:2 * P], oT[b][:, :], wo_sb[:, :]).then_inc(wo_done, 1)

            def step(ci, first=False):
                back_tr(ci, first)
                front_tr(ci + 1)
                if not first:
                    back_wo(ci - 1)
                back_att(ci)
                front_proj(ci + 1)
                back_o(ci)
                front_v(ci + 1)

            front_tr(0)
            front_proj(0)
            front_v(0)
            step(0, first=True)
            with pe.Fori(1, C - 1) as ci:
                step(ci)
            back_tr(C - 1)
            back_wo(C - 2)
            back_att(C - 1)
            back_o(C - 1)
            back_tr(C, last=True)
            back_wo(C - 1)

            def tr_yn(k, b):
                pe.wait_ge(yn_ready, k * B + b + 1)
                for j in range(TG):
                    last = nc.tensor.transpose(bA[b][:, j * P:(j + 1) * P], yn[b][:, j, :], ident[:, :])
                last.then_inc(h2T_tr, 1)

            def ffn1(k, b):
                pe.wait_ge(h2T_ready, k * B + b + 1)
                if k:
                    pe.wait_ge(x1_ready, (k - 1) * B + b + 1)
                for j in range(HB):
                    if j == 3:
                        pe.wait_ge(hid_a, (k * B + b) * (HB // 2) + 1)
                    mm([bB, bC, bD, bB][j][b][:, :], w1_sb[:, j, :], h2T[b][:, :]).then_inc(w1_done, 1)

            def ffn2(k, b):
                pe.wait_ge(hid_a, (k * B + b + 1) * (HB // 2))
                pe.wait_ge(hid_v, (k * B + b + 1) * (HB // 2))
                for j in range(HB):
                    last = mm(bA[b][:, :], w2_sb[:, j, :], hid[b][:, j, :], start=j == 0, stop=j == HB - 1)
                last.then_inc(w2_done, 1)

            def tr_o2(k, b):
                pe.wait_ge(o2T_ready, k * B + b + 1)
                for j in range(TG):
                    last = nc.tensor.transpose(bB[b][:, j * P:(j + 1) * P], o2T[b][:, j * P:(j + 1) * P],
                                               ident[:, :])
                last.then_inc(o2_tr, 1)

            def tr_h3(k, b):
                pe.wait_ge(h3_ready, k * B + b + 1)
                for j in range(TG):
                    last = nc.tensor.transpose(bC[b][:, j * P:(j + 1) * P], h3[k][b][:, j, :], ident[:, :])
                last.then_inc(h3T_tr, 1)

            def router(k, b):
                pe.wait_ge(h3T_ready, k * B + b + 1)
                for j in range(TG):
                    last = mm(bD[b][:, j * E:(j + 1) * E], h3T[k][b][:, j * P:(j + 1) * P],
                              vecT[:, 5 + HB:5 + HB + E])
                last.then_inc(logit_done, 1)

            def ranks(k):
                pe.wait_ge(sel_ready, k + 1)
                rk = bD[0][:, RK:RK + (TT + 1) * E]
                mm(rk, tri[:, :], sel[:, :, :], stop=False)
                for t in range(TT):
                    last = mm(rk[:, (t + 1) * E:], ones[:, :],
                              sel[:, t, :].unsqueeze(1).to_broadcast([P, TT - t, E]), start=False, stop=t == TT - 1)
                last.then_inc(rank_done, 1)

            def shared_gu(k, b, j):
                n = (k * IB + j) * B + b
                if j:
                    pe.wait_ge(act_ready, n - B + 1)
                mm(bA[b][:, :], shgT[:, j * P:(j + 1) * P], h3T[k][b][:, :])
                mm(bC[b][:, :], shuT[:, j * P:(j + 1) * P], h3T[k][b][:, :]).then_inc(g_done, 1)

            def shared_down(k, b):
                pe.wait_ge(act_ready, (k * IB + IB - 1) * B + b + 1)
                for t in range(TG):
                    for j in range(IB):
                        last = mm(bB[b][:, t * P:(t + 1) * P], act[b][:, j, t * P:(t + 1) * P], shdT[:, j, :],
                                  start=j == 0, stop=j == IB - 1)
                last.then_inc(ysh_done, 1)

            pe.wait_ge(ffn_in, 32)
            both = range(B)
            [tr_yn(0, b) for b in both]
            [ffn1(0, b) for b in both]
            [ffn2(0, b) for b in both]
            [tr_o2(0, b) for b in both]
            [tr_yn(1, b) for b in both]
            [ffn1(1, b) for b in both]
            pe.wait_ge(hid_a, 2 * B * HB // 2)
            pe.wait_ge(hid_v, 2 * B * HB // 2)
            [tr_h3(0, b) for b in both]
            [router(0, b) for b in both]
            [ffn2(1, b) for b in both]
            pe.wait_ge(zeros_ready, 1)
            ranks(0)
            [tr_o2(1, b) for b in both]
            for j in range(IB):
                [shared_gu(0, b, j) for b in both]
            for b in both:
                pe.wait_ge(x1_ready, B + b + 1)
                shared_down(0, b)
            pe.wait_ge(rows_ready, 1)
            pe.wait_ge(act_ready, B * IB)
            [tr_h3(1, b) for b in both]
            [router(1, b) for b in both]
            pe.wait_ge(h3T_ready, 2 * B)
            [shared_gu(1, b, 0) for b in both]
            ranks(1)
            [shared_gu(1, b, 1) for b in both]
            pe.wait_ge(cv_ready, 1)
            mm(bD[0][:, SC:SC + 1], tri[:, :], cv16[:, :]).then_inc(cpos_done, 1)
            pe.wait_ge(onehot_ready, 1)
            mm(bD[0][0:1, SC + 1:SC + 1 + NT], cvals[:, 0:1], onehot[:, :])
            mm(bD[0][0:1, SC + 1 + NT:SC + 1 + 2 * NT], cvals[:, 1:2], onehot[:, :]).then_inc(tab_done, 1)
            for b in both:
                pe.wait_ge(base_ready, b + 1)
                shared_down(1, b)

            def tile_experts(i):
                w = pe.value_load(tile_e[0:1, bass.ds(i, 1)], min_val=0, max_val=E ** (2 * NBUF) - 1)
                return [(w // E ** j) % E for j in range(2 * NBUF)]

            def tr_x(n, m, turn):
                pe.wait_ge(xt_in[m], turn * 16 + 16)
                if m == 2:
                    pe.wait_ge(xlo_ready, n - 1)
                elif m == 0 and not (isinstance(n, int) and n == 0):
                    pe.wait_ge(xlo_ready, n)
                nc.tensor.transpose(bank[XB[m]][:, 0:P], xt[m], ident[:, :]).then_inc(xT_tr, 1)

            def gate_up(n, m, e):
                pe.wait_ge(xlo_ready, n + 1)
                mm(bank[m][:, :], xT[m][0][:, :], wgu[0][:, bass.ds(e, 1), :], stop=False)
                mm(bank[m][:, :], xT[m][0][:, :], wgu[1][:, bass.ds(e, 1), :], start=False, stop=False)
                mm(bank[m][:, :], xT[m][1][:, :], wgu[0][:, bass.ds(e, 1), :], start=False).then_inc(gu_done, 1)

            def tr_a(n, m):
                pe.wait_ge(actt_ready, n + 1)
                if not isinstance(n, int) or n >= NBUF:
                    pe.wait_ge(yt_ready, n - 1)
                for j in range(IB):
                    last = nc.tensor.transpose(bank[3 + m][:, j * P:(j + 1) * P], actt[m][:, j * P:(j + 1) * P],
                                               ident[:, :])
                last.then_inc(aT_tr, 1)

            def down(n, m, e):
                pe.wait_ge(alo_ready, n + 1)
                prods = [(j, a, w) for j in range(IB) for a, w in ((0, 0), (0, 1), (1, 0))]
                for i, (j, a, w) in enumerate(prods):
                    last = mm(bank[3 + m][:, IB * P:(IB + 1) * P], aT[m][a][:, j, :], wdn[w][:, bass.ds(e, 1), j * P:(j + 1) * P],
                              start=i == 0, stop=i == len(prods) - 1)
                last.then_inc(yt_done, 1)

            pe.wait_ge(base_ready, 2 * B)
            pe.wait_ge(tab_ready, 1)
            pe.wait_ge(wsplit, 6 * E)
            e = tile_experts(0)
            tr_x(0, 0, 0)
            tr_x(1, 1, 0), gate_up(0, 0, e[0])
            tr_x(2, 2, 0), gate_up(1, 1, e[1]), tr_a(0, 0)
            tr_x(3, 0, 1), gate_up(2, 2, e[2])

            def turn(i, last=False):
                n, e = i * NBUF, tile_experts(i)
                tr_a(n + 1, 1), down(n, 0, e[0])
                tr_x(n + 4, 1, i + 1), gate_up(n + 3, 0, e[3]), tr_a(n + 2, 2), down(n + 1, 1, e[1])
                tr_x(n + 5, 2, i + 1), gate_up(n + 4, 1, e[4]), tr_a(n + 3, 0), down(n + 2, 2, e[2])
                if not last:
                    tr_x(n + 6, 0, i + 2)
                gate_up(n + 5, 2, e[5])

            turns = NT // NBUF
            with pe.Fori(0, turns - 2) as i:
                turn(i)
            turn(turns - 2, last=True)
            n, e = NT - NBUF, tile_experts(turns - 1)
            tr_a(n + 1, 1), down(n, 0, e[0])
            tr_a(n + 2, 2), down(n + 1, 1, e[1])
            down(n + 2, 2, e[2])


_INS = ["L0_attn_batch", "L0_attn_Wq", "L0_attn_Wk", "L0_attn_Wv", "L0_attn_Wo", "L0_attn_omega", "L0_attn_W1",
        "L0_attn_b1", "L0_attn_W2", "L0_attn_b2", "L0_attn_gamma", "L0_attn_beta", "L0_ffn_shared_gate",
        "L0_ffn_shared_up", "L0_ffn_shared_down", "L0_ffn_gate_w", "L0_ffn_up_w", "L0_ffn_down_w",
        "L0_ffn_router_w", "L0_ffn_routing_bias", "L0_c", "L0_wmod"]


def kernel(**inputs):
    import numpy as _np
    import concourse.bacc as _bacc
    from concourse import mybir as _mybir
    from concourse.bass_utils import run_bass_kernel_spmd as _run

    nc = _bacc.Bacc("TRN2", target_bir_lowering=False, num_devices=1)
    arrays, args = {}, []
    for name in _INS:
        a = _np.ascontiguousarray(inputs[name])
        arrays[f"in_{name}"] = a
        args.append(nc.dram_tensor(f"in_{name}", a.shape, _mybir.dt.from_np(a.dtype), kind="ExternalInput").ap())
    out = nc.dram_tensor("out", inputs["L0_attn_batch"].shape, _mybir.dt.float32, kind="ExternalOutput").ap()
    rows = 8 * (2 * 1024 + 128) + 8 * 128
    xdisp = nc.dram_tensor("xdisp", [rows, 128], _mybir.dt.float32, kind="Internal").ap()
    ydisp = nc.dram_tensor("ydisp", [rows, 128], _mybir.dt.float32, kind="Internal").ap()
    adaln_block(nc, xdisp, ydisp, *args, out)
    r = _run(nc, [arrays], core_ids=[0])
    return r.results[0]["out"]
```

```python
from contextlib import ExitStack

import concourse.bass as bass
from concourse import mybir

P = 128
F32 = mybir.dt.float32
F32R = mybir.dt.float32r
BF16 = mybir.dt.bfloat16
I32 = mybir.dt.int32
ALU = mybir.AluOpType
ACT = mybir.ActivationFunctionType
AX = mybir.AxisListType

LN_EPS = 1e-5
ATTN_LN_EPS = 1e6
FEAT_EPS = 1e-6


def adaln_block(nc, xdisp, ydisp, x, wq, wk, wv, wo, omega, w1, b1, w2, b2, gamma, beta,
                sh_gate, sh_up, sh_down, gate_w, up_w, down_w, router_w, routing_bias,
                c, wmod, out):
    B, S, D = x.shape
    M, DH = omega.shape
    H = D // DH
    HB = w1.shape[1] // P
    E, _, I = gate_w.shape
    E_BITS = E.bit_length() - 1
    IB = I // P
    C = S // P
    TG = 4
    G = C // TG
    NV = DH + 1
    INV_SQRT_M = float(M) ** -0.5
    QK_SCALE = float(DH) ** -0.25
    U = G * B
    TT = B * TG
    T = B * S
    RB = T // P + 1
    NT = (2 * T + E * (P - 1)) // P
    NU = NT - 2 * T // P + 1
    YB = ydisp.shape[0] // P
    YN = 2 * C
    NBUF = 3
    BW = YB
    assert 2 * BW ** NBUF <= 1 << 24 and E ** (2 * NBUF) <= 1 << 24
    assert YB >= E * RB + NU and YB % YN == 0
    assert NT % NBUF == 0 and E * (T // P) == P
    assert D == P and M == P and B == 2 and H == 2 and IB == 2 and HB == 4 and G == 2 and E == 1 << E_BITS

    with ExitStack() as ctx:
        def sb(name, shape, dt=F32):
            return ctx.enter_context(nc.sbuf_tensor(name, shape, dt))

        def sem(name):
            return ctx.enter_context(nc.semaphore(name))

        ident = sb("ident", [P, P])
        causal = sb("causal", [P, H, P])
        x_all = sb("x_all", [P, B, C, P])
        xn_all = sb("xn_all", [P, B, C, P])
        h_all = sb("h_all", [P, B, C, P])
        stats = sb("stats", [P, B, C, 6])
        stats3 = sb("stats3", [P, B, TG, 6])
        mean = sb("mean", [P, B, C])
        var = sb("var", [P, B, C])
        rstd = sb("rstd", [P, B, C])
        lt = [sb(f"lt{i}", [P, B, C]) for i in range(3)]
        l3 = [sb(f"l3{i}", [P, B, TG]) for i in range(6)]
        c_rows = sb("c_rows", [B, P])
        vec_rows = sb("vec_rows", [3 + HB + E, P])
        vecT = sb("vecT", [P, 3 + HB + E])
        rbias = sb("rbias", [P, E])
        silu_c = sb("silu_c", [P, B])
        silu_bc = sb("silu_bc", [P, B, P])
        warm = sb("warm", [P, B])
        mod = sb("mod", [P, B, 6, P])
        ga_col = sb("ga_col", [P, B])
        ga_abs = sb("ga_abs", [P, B])
        gab2 = sb("gab2", [P, B])
        gsign = silu_bc
        wq_sb, wk_sb, wv_sb, wo_sb = (sb(n, [P, P]) for n in ("wq_sb", "wk_sb", "wv_sb", "wo_sb"))
        om2 = sb("om2", [P, 2, DH])
        wqT, wkT, om2T = (sb(n, [P, P]) for n in ("wqT", "wkT", "om2T"))
        wproj = sb("wproj", [P, 2 * H, M])
        w1_sb = sb("w1_sb", [P, HB, P])
        w2_sb = sb("w2_sb", [P, HB, P])
        shg_sb = sb("shg_sb", [P, IB, P])
        shu_sb = sb("shu_sb", [P, IB, P])
        shd_sb = sb("shd_sb", [P, IB, P])
        shgT = sb("shgT", [P, I])
        shuT = sb("shuT", [P, I])
        shdT = sb("shdT", [P, IB, P])
        gate_sb = sb("gate_sb", [P, E, I])
        up_sb = sb("up_sb", [P, E, I])
        down_sb = sb("down_sb", [P, E, IB, P])
        hmul = [sb(f"hmul{b}", [P, P]) for b in range(B)]
        hst = [sb(f"hst{b}", [P, P]) for b in range(B)]
        hT = [sb(f"hT{b}", [P, P]) for b in range(B)]
        negmax = [sb(f"negmax{b}", [P, 2 * H]) for b in range(B)]
        feat = [sb(f"feat{b}", [P, 2 * H, M]) for b in range(B)]
        featT = [sb(f"featT{b}", [P, 2 * H, P]) for b in range(B)]
        kfeat = [sb(f"kfeat{b}", [P, H, M]) for b in range(B)]
        vext = [sb(f"vext{b}", [P, H, NV]) for b in range(B)]
        att = [sb(f"att{b}", [P, H, P]) for b in range(B)]
        state = [sb(f"state{b}", [P, H, NV]) for b in range(B)]
        den = [sb(f"den{b}", [P, H]) for b in range(B)]
        rden = [sb(f"rden{b}", [P, H]) for b in range(B)]
        o_n = [sb(f"o_n{b}", [P, H, DH]) for b in range(B)]
        oT = [sb(f"oT{b}", [P, P]) for b in range(B)]
        yn = [sb(f"yn{b}", [P, TG, P]) for b in range(B)]
        h2T = [sb(f"h2T{b}", [P, TG * P]) for b in range(B)]
        hid = [sb(f"hid{b}", [P, HB, TG * P]) for b in range(B)]
        wmod_sb = hid[0][:, 0:2, :].rearrange("p j n -> p (j n)")[:, 0:6 * P]
        blank = hid[1][:, :, :].rearrange("p j n -> p (j n)")
        o2T = [sb(f"o2T{b}", [P, TG * P]) for b in range(B)]
        x1n = [sb(f"x1n{b}", [P, TG, P]) for b in range(B)]
        h3 = [[sb(f"h3{k}{b}", [P, TG, P]) for b in range(B)] for k in range(G)]
        h3T = [[sb(f"h3T{k}{b}", [P, TG * P]) for b in range(B)] for k in range(G)]
        logit = sb("logit", [P, TT, E])
        prob = sb("prob", [P, TT, E])
        prob2 = sb("prob2", [P, TT, E])
        first8 = sb("first8", [P, TT, E])
        hit = sb("hit", [P, TT, E])
        pick = [sb(f"pick{i}", [P, TT, E]) for i in range(2)]
        top = [sb(f"top{i}", [P, TT]) for i in range(2)]
        hitmax = sb("hitmax", [P, TT])
        topsum = sb("topsum", [P, TT])
        topinv = sb("topinv", [P, TT])
        wts = sb("wts", [P, G, 2, TT])
        sel = sb("sel", [P, TT + 1, E], BF16)
        slotf = sb("slotf", [P, TT, E])
        slotp = sb("slotp", [P, TT, E])
        rowf = sb("rowf", [P, 2, TT])
        rows = sb("rows", [P, G, 2, TT], I32)
        cnt = sb("cnt", [P, E])
        cbase = sb("cbase", [P, E])
        cum = sb("cum", [P, G * TT, E])
        tri = sb("tri", [P, P], BF16)
        ones = sb("ones", [P, P], BF16)
        cand = sb("cand", [P, 1], I32)
        cki = sb("cki", [P, 1], I32)
        cf, ck, ce, cvalid, cpos = (sb(n, [P, 1]) for n in ("cf", "ck", "ce", "cvalid", "cpos"))
        iota_e = sb("iota_e", [P, E])
        iota_p = sb("iota_p", [P, P])
        emask = sb("emask", [P, E])
        cumc, notyet = sb("cumc", [P, G * TT]), sb("notyet", [P, G * TT])
        since, key, cstart = (sb(n, [P, 1]) for n in ("since", "key", "cstart"))
        diag = sb("diag", [P, P], BF16)
        keys = sb("keys", [P, P])
        needed = sb("needed", [P, G * TT], BF16)
        cvals = sb("cvals", [P, 3], BF16)
        cq = sb("cq", [P, G * TT, E])
        cend, ctop = sb("cend", [P, 1]), sb("ctop", [P, 1])
        late = sb("late", [1, NT // NBUF])
        onehot = sb("onehot", [P, NT], BF16)
        tile_e = sb("tile_e", [1, NT // NBUF], I32)
        first_rows = sb("first_rows", [1, 2], I32)
        tile_rows = sb("tile_rows", [1, NT // NBUF, 2], I32)
        packed = [sb(f"packed{i}", [1, NT // NBUF]) for i in range(3)]
        tile_blk = sb("tile_blk", [1, NT])
        spare = sb("spare", [1, NT])
        ntail = sb("ntail", [1, NT])
        pad_row = sb("pad_row", [1, E], I32)
        req = sb("req", [1, G * TT], I32)
        zeros = sb("zeros", [P, P])
        act = [hid[b][:, 0:IB, :] for b in range(B)]
        sil = [hid[b][:, IB, :] for b in range(B)]
        wgu = [sb(f"wgu_{n}", [P, E, 2 * I], F32R) for n in ("hi", "lo")]
        wdn_parts = sb("wdn_parts", [P, E, 2, IB * P], F32R)
        wdn = [wdn_parts[:, :, i, :] for i in range(2)]
        xt = [kfeat[m // 2][:, m % 2, :] for m in range(NBUF)]
        xT = [[sb(f"xT_{n}{m}", [P, P], F32R) for n in ("hi", "lo")] for m in range(NBUF)]
        silt = [feat[m // 2][:, 2 * (m % 2):2 * (m % 2) + 2, :].rearrange("p a n -> p (a n)") for m in range(NBUF)]
        actt = [featT[m // 2][:, 2 * (m % 2):2 * (m % 2) + 2, :].rearrange("p a n -> p (a n)") for m in range(NBUF)]
        aT = [[sb(f"aT_{n}{m}", [P, IB, P], F32R) for n in ("hi", "lo")] for m in range(NBUF)]
        yt = [att[m // 2][:, m % 2, :] for m in range(NBUF)]
        got = [xn_all[:, :, :, :].rearrange("p b c d -> p (b c) d"),
               gate_sb[:, :, :].rearrange("p e (a d) -> p (e a) d", d=P)]
        comb = yn[0]

        bank = [ctx.enter_context(nc.psum_tensor(f"bank{i}", [P, 512], F32)) for i in range(8)]
        bA, bB, bC, bD = ([bank[4 * b + k] for b in range(B)] for k in range(4))

        x_in = [sem(f"x_in{b}") for b in range(B)]
        c_in, vec_in, qk_in, vo_in, sh_in = map(sem, ("c_in", "vec_in", "qk_in", "vo_in", "sh_in"))
        mod_in, ffn_in, moe_in = map(sem, ("mod_in", "ffn_in", "moe_in"))
        consts = sem("consts")
        pe_setup = sem("pe_setup")
        setup_used = sem("setup_used")
        silu_done = sem("silu_done")
        silu_bc_done = sem("silu_bc_done")
        vec_ready, mod_rest_in = sem("vec_ready"), sem("mod_rest_in")
        halves, row_ready, out_ready = sem("halves"), sem("row_ready"), sem("out_ready")
        sa_ready, ca_ready, mod_copied, mod_ready = map(sem, ("sa_ready", "ca_ready", "mod_copied", "mod_ready"))
        xn_ready = sem("xn_ready")
        dv = sem("dv")
        pl = sem("pl")
        h_staged = sem("h_staged")
        hT_tr, hT_ready = sem("hT_tr"), sem("hT_ready")
        proj_done, max_ready, feat_ready = sem("proj_done"), sem("max_ready"), sem("feat_ready")
        featT_tr, featT_ready, kfeat_ready = sem("featT_tr"), sem("featT_ready"), sem("kfeat_ready")
        v_done, vext_ready = sem("v_done"), sem("vext_ready")
        att_done, att_ready = sem("att_done"), sem("att_ready")
        o_done, st_done, on_ready = sem("o_done"), sem("st_done"), sem("on_ready")
        oT_tr, oT_ready, wo_done, y_ready = sem("oT_tr"), sem("oT_ready"), sem("wo_done"), sem("y_ready")
        den_ready, rden_ready = sem("den_ready"), sem("rden_ready")
        dv2 = sem("dv2")
        dvc = sem("dvc")
        yn_ready, h2T_tr, h2T_ready = sem("yn_ready"), sem("h2T_tr"), sem("h2T_ready")
        w1_done, hid_a, hid_v = sem("w1_done"), sem("hid_a"), sem("hid_v")
        w2_done, o2T_ready, o2_tr, x1_ready = sem("w2_done"), sem("o2T_ready"), sem("o2_tr"), sem("x1_ready")
        h3_ready, h3T_tr, h3T_ready = sem("h3_ready"), sem("h3T_tr"), sem("h3T_ready")
        logit_done, logit_ready, prob_ready = sem("logit_done"), sem("logit_ready"), sem("prob_ready")
        sel_ready, rank_done, rows_ready = sem("sel_ready"), sem("rank_done"), sem("rows_ready")
        cv_ready, cpos_done, onehot_ready = sem("cv_ready"), sem("cpos_done"), sem("onehot_ready")
        tab_done, tab_ready = sem("tab_done"), sem("tab_ready")
        blank_ready, blanked = sem("blank_ready"), sem("blanked")
        scattered, padded, pad_ready = [sem(f"scattered{k}") for k in range(G)], sem("padded"), sem("pad_ready")
        zeros_ready, req_ready = sem("zeros_ready"), sem("req_ready")
        wsplit = sem("wsplit")
        g_done, sil_ready, act_ready = sem("g_done"), sem("sil_ready"), sem("act_ready")
        ysh_done, base_ready = sem("ysh_done"), sem("base_ready")
        xt_in = [sem(f"xt_in{m}") for m in range(NBUF)]
        xT_tr, xhi_ready, xlo_ready = sem("xT_tr"), sem("xhi_ready"), sem("xlo_ready")
        gu_done, silt_ready, actt_ready = sem("gu_done"), sem("silt_ready"), sem("actt_ready")
        aT_tr, ahi_ready, alo_ready = sem("aT_tr"), sem("ahi_ready"), sem("alo_ready")
        yt_done, yt_ready = sem("yt_done"), sem("yt_ready")
        yt_out = [sem(f"yt_out{m}") for m in range(NBUF)]
        gathered = [sem(f"gathered{i}") for i in range(G * TT)]
        weighted = sem("weighted")
        fin_ready, stored = sem("fin_ready"), sem("stored")

        block = ctx.enter_context(nc.Block())
        nv = 3 + HB + E
        RK, SC, KC, RQ = 64, 192, 320, 448
        XB = [6, 7, 6]

        pieces = [(u, 0, TG) for u in range(U - 1)] + [(U - 1, 0, TG - 1), (U - 1, TG - 1, TG)]

        def pipeline(eng, s0, s1, s2, s3):
            s0(0, 0, 0)
            s0(1, 1, 0), s1(0, 0)
            s0(2, 2, 0), s1(1, 1), s2(0, 0)
            with eng.Fori(0, NT // NBUF - 1) as i:
                for m in range(NBUF):
                    n = i * NBUF + m
                    s0(n + 3, m, i + 1)
                    s1(n + 2, (m + 2) % NBUF)
                    s2(n + 1, (m + 1) % NBUF)
                    s3(n, m, i)
            n = NT - NBUF
            s1(n + 2, 2), s2(n + 1, 1), s3(n, 0, n // NBUF)
            s2(n + 2, 2), s3(n + 1, 1, n // NBUF)
            s3(n + 2, 2, n // NBUF)

        @block.sync
        def _(sp):
            for b in range(B):
                sp.dma_start(x_all[:, b, :, :], x[b].rearrange("(c p) d -> p c d", p=P)).then_inc(x_in[b], 16)
            sp.dma_start(wv_sb[:, :], wv).then_inc(vo_in, 16)
            sp.dma_start(wo_sb[:, :], wo).then_inc(vo_in, 16)
            sp.dma_start(vec_rows[0:1, :], gamma.rearrange("(a n) -> a n", a=1)).then_inc(vec_in, 16)
            sp.dma_start(vec_rows[1:2, :], beta.rearrange("(a n) -> a n", a=1)).then_inc(vec_in, 16)
            sp.dma_start(vec_rows[2:3, :], b2.rearrange("(a n) -> a n", a=1)).then_inc(vec_in, 16)
            sp.dma_start(vec_rows[3:3 + HB, :], b1.rearrange("(a n) -> a n", n=P)).then_inc(vec_in, 16)
            sp.dma_start(vec_rows[3 + HB:3 + HB + E, :], router_w).then_inc(vec_in, 16)
            sp.dma_start(wmod_sb[:, 2 * P:6 * P], wmod[:, 2 * P:6 * P]).then_inc(mod_rest_in, 16)
            sp.dma_start(shg_sb[:, :, :], sh_gate.rearrange("(j p) h -> p j h", p=P)).then_inc(sh_in, 16)
            sp.dma_start(shu_sb[:, :, :], sh_up.rearrange("(j p) h -> p j h", p=P)).then_inc(sh_in, 16)
            sp.dma_start(shd_sb[:, :, :], sh_down.rearrange("h (j p) -> h j p", p=P)).then_inc(sh_in, 16)
            sp.dma_start(rbias[:, :], routing_bias.partition_broadcast(P)).then_inc(sh_in, 16)
            sp.dma_start(w1_sb[:, :, :], w1.rearrange("d (j n) -> d j n", n=P)).then_inc(ffn_in, 16)
            sp.dma_start(w2_sb[:, :, :], w2.rearrange("(j p) n -> p j n", p=P)).then_inc(ffn_in, 16)
            sp.dma_start(gate_sb[:, :, :], gate_w.rearrange("e h i -> h e i")).then_inc(moe_in, 16)
            sp.dma_start(up_sb[:, :, :], up_w.rearrange("e h i -> h e i")).then_inc(moe_in, 16)
            sp.dma_start(down_sb[:, :, :, :], down_w.rearrange("e (j p) n -> p e j n", p=P)).then_inc(moe_in, 16)
            sp.wait_ge(blank_ready, 1)
            for r0 in range(0, YB, YN):
                sp.dma_start(ydisp[r0 * P:(r0 + YN) * P, :].rearrange("(p r) d -> p (r d)", p=P),
                             blank).then_inc(blanked, 16)
            sp.wait_ge(zeros_ready, 1)
            sp.dma_start(xdisp[E * RB * P:(E * RB + 1) * P, :], zeros[:, :]).then_inc(padded, 16)
            sp.wait_ge(pad_ready, 1)
            ends = nc.values_load_multi_w_load_instructions(
                pad_row[0:1, :], engines=[mybir.EngineType.SP], min_val=0, max_val=E * RB * P - P)[1]
            for e in range(E):
                sp.dma_start(xdisp[bass.ds(ends[e], P), :], zeros[:, :]).then_inc(padded, 16)

            def words(table):
                return nc.values_load_multi_w_load_instructions(
                    table, engines=[mybir.EngineType.SP], min_val=0, max_val=2 * BW ** NBUF - 1)[1]

            def block(w, m):
                return bass.ds((w // BW ** m) % BW, 1)

            xblocks = xdisp.rearrange("(n p) d -> n p d", p=P)
            yblocks = ydisp.rearrange("(n p) d -> n p d", p=P)

            def rows_there(w):
                sp.wait_ge(halves, w // BW ** NBUF + 1)

            def load(w, m):
                sp.dma_start(xt[m], xblocks[block(w, m), :, :]).then_inc(xt_in[m], 16)

            def store(w, i, m):
                sp.wait_ge(yt_ready, i * NBUF + m + 2)
                sp.dma_start(yblocks[block(w, m), :, :], yt[m]).then_inc(yt_out[m], 16)

            for m in range(NBUF):
                sp.sem_inc(yt_out[m], 16)
            sp.sem_inc(yt_ready, 1)
            sp.wait_ge(row_ready, 1)
            sp.wait_ge(padded, 16 * (E + 1))
            sp.wait_ge(blanked, 16 * YB // YN)

            first = words(first_rows[0:1, :])
            for i in range(2):
                rows_there(first[i])
                for m in range(NBUF):
                    if i:
                        sp.wait_ge(xT_tr, m + 1)
                    load(first[i], m)
            sp.wait_ge(out_ready, 1)

            def turn(i, ahead, now):
                rows_there(ahead)
                for m in range(NBUF):
                    sp.wait_ge(xT_tr, (i + 1) * NBUF + m + 1)
                    load(ahead, m)
                    if m:
                        store(now, i, m - 1)
                store(now, i, NBUF - 1)

            turns = NT // NBUF - 2
            with sp.Fori(0, turns // 2) as i2:
                w = words(tile_rows[0:1, bass.ds(i2 * 2, 2), :].rearrange("a i w -> a (i w)"))
                turn(i2 * 2, w[0], w[1])
                turn(i2 * 2 + 1, w[2], w[3])
            for i in range(turns // 2 * 2, turns):
                turn(i, *words(tile_rows[0:1, i, :]))
            for i in range(turns, NT // NBUF):
                _, now = words(tile_rows[0:1, i, :])
                for m in range(NBUF):
                    store(now, i, m)
            for m in range(NBUF):
                sp.wait_ge(yt_out[m], 16 * (NT // NBUF + 1))
            for i, (u, t0, t1) in enumerate(pieces):
                k, b = divmod(u, B)
                sp.wait_ge(fin_ready, i + 1)
                sp.dma_start(out[b].rearrange("(c p) d -> p c d", p=P)[:, k * TG + t0:k * TG + t1, :],
                             h_all[:, b, k * TG + t0:k * TG + t1, :]).then_inc(stored, 16)
            sp.wait_ge(stored, 16 * len(pieces))

        @block.gpsimd
        def _(pool):
            nc.gpsimd.memset(ident[:, :], 0.0).then_inc(pl, 1)
            nc.gpsimd.memset(causal[:, :, :], 1.0).then_inc(pl, 1)
            nc.gpsimd.memset(tri[:, :], 1.0).then_inc(pl, 1)
            pool.wait_ge(pl, 3)
            nc.gpsimd.affine_select(out=ident[:, :], in_=ident[:, :], compare_op=ALU.not_equal, fill=1.0,
                                    base=0, pattern=[[-1, P]], channel_multiplier=1).then_inc(consts, 1)
            nc.gpsimd.affine_select(out=causal[:, :, :], in_=causal[:, :, :], compare_op=ALU.is_ge, fill=0.0,
                                    base=0, pattern=[[0, H], [1, P]], channel_multiplier=-1).then_inc(consts, 1)
            nc.gpsimd.affine_select(out=tri[:, :], in_=tri[:, :], compare_op=ALU.is_gt, fill=0.0,
                                    base=0, pattern=[[1, P]], channel_multiplier=-1)
            nc.gpsimd.iota(first8[:, :, :], pattern=[[0, TT], [-1, E]], base=E, channel_multiplier=0,
                           allow_small_or_imprecise_dtypes=True)
            nc.gpsimd.iota(iota_e[:, :], pattern=[[1, E]], base=0, channel_multiplier=0,
                           allow_small_or_imprecise_dtypes=True)
            nc.gpsimd.iota(iota_p[:, :], pattern=[[1, P]], base=0, channel_multiplier=0,
                           allow_small_or_imprecise_dtypes=True)
            nc.gpsimd.iota(cbase[:, :], pattern=[[RB * P, E]], base=0, channel_multiplier=0,
                           allow_small_or_imprecise_dtypes=True)
            nc.gpsimd.iota(cand[:, :], pattern=[[0, 1]], base=0, channel_multiplier=1)
            nc.gpsimd.memset(ones[:, :], 1.0)
            nc.gpsimd.memset(sel[:, :, :], 0.0)
            nc.gpsimd.memset(cnt[:, :], 0.0)
            nc.gpsimd.memset(blank, 0.0).then_inc(blank_ready, 1)
            nc.gpsimd.memset(zeros[:, :], 0.0).then_inc(zeros_ready, 1)

            def stage(ci, first=False):
                pool.wait_ge(xn_ready, ci + 1)
                for b in range(B):
                    nc.gpsimd.tensor_tensor(hmul[b][:, :], xn_all[:, b, bass.ds(ci, 1), :], mod[:, b, 1, :],
                                            ALU.mult).then_inc(pl, 1)
                    pool.wait_ge(pl, ci * 2 * B + 2 * b + 4)
                    if not first:
                        pool.wait_ge(hT_tr, ci * B + b - B + 1)
                    nc.gpsimd.tensor_tensor(hst[b][:, :], hmul[b][:, :], mod[:, b, 0, :],
                                            ALU.add).then_inc(h_staged, 1)
                    nc.gpsimd.tensor_tensor(h_all[:, b, bass.ds(ci, 1), :], hmul[b][:, :], mod[:, b, 0, :],
                                            ALU.add).then_inc(pl, 1)

            pool.wait_ge(sa_ready, B)
            pool.wait_ge(ca_ready, 1)
            stage(0, first=True)
            with pool.Fori(1, C) as ci:
                stage(ci)
            pool.wait_ge(moe_in, 16 * 3)
            with pool.Fori(0, E) as e:
                parts = [(wgu, 0, I, gate_sb[:, bass.ds(e, 1), :]), (wgu, I, 2 * I, up_sb[:, bass.ds(e, 1), :]),
                         (wdn, 0, IB * P, down_sb[:, bass.ds(e, 1), :, :])]
                for w, lo, hi, src in parts:
                    nc.gpsimd.tensor_copy(w[0][:, bass.ds(e, 1), lo:hi], src).then_inc(wsplit, 1)
                pool.wait_ge(wsplit, e * 6 + 3)
                for w, lo, hi, src in parts:
                    nc.gpsimd.tensor_tensor(w[1][:, bass.ds(e, 1), lo:hi], src,
                                            w[0][:, bass.ds(e, 1), lo:hi].bitcast(F32),
                                            ALU.subtract).then_inc(wsplit, 1)
            for k in range(G):
                if k:
                    pool.wait_ge(scattered[0], 16 * 2 * TT)
                    pool.sem_inc(halves, 1)
                pool.wait_ge(h3_ready, (k + 1) * B)
                pool.wait_ge(rows_ready, k + 1)
                for t in range(TT):
                    for i in range(2):
                        nc.gpsimd.indirect_dma_start(
                            out=xdisp, out_offset=bass.IndirectOffsetOnAxis(ap=rows[:, k, i, t:t + 1], axis=0),
                            in_=h3[k][t // TG][:, t % TG, :], in_offset=None).then_inc(scattered[k], 16)
            pool.wait_ge(scattered[1], 16 * 2 * TT)
            pool.sem_inc(halves, 1)
            pool.wait_ge(req_ready, 1)
            for q in range(G * TT):
                n = pool.value_load(req[0:1, q:q + 1], min_val=1, max_val=NT)
                for m in range(NBUF):
                    pool.wait_ge(yt_out[m], (n + NBUF - 1) // NBUF * 16 + 16)
                pool.sem_inc(pl, 1)
                for i in range(2):
                    nc.gpsimd.indirect_dma_start(
                        out=got[i][:, q, :], out_offset=None, in_=ydisp,
                        in_offset=bass.IndirectOffsetOnAxis(ap=rows[:, q // TT, i, q % TT:q % TT + 1], axis=0))\
                        .then_inc(gathered[q], 16)

        @block.scalar
        def _(act_e):
            act_e.dma_start(c_rows[:, :], c).then_inc(c_in, 16)
            act_e.dma_start(wmod_sb[:, 0:2 * P], wmod[:, 0:2 * P]).then_inc(mod_in, 16)
            act_e.dma_start(wq_sb[:, :], wq).then_inc(qk_in, 16)
            act_e.dma_start(wk_sb[:, :], wk).then_inc(qk_in, 16)
            act_e.dma_start(om2[:, 0, :], omega).then_inc(qk_in, 16)
            act_e.dma_start(om2[:, 1, :], omega).then_inc(qk_in, 16)
            act_e.wait_ge(pe_setup, 1)
            nc.scalar.activation(silu_bc[:, :, :], bank[0][:, 0:B].unsqueeze(2).to_broadcast([P, B, P]),
                                 ACT.Silu).then_inc(silu_bc_done, 1)
            nc.scalar.activation(silu_c[:, :], bank[0][:, 0:B], ACT.Silu).then_inc(silu_done, 1)
            act_e.wait_ge(pe_setup, 2)
            nc.scalar.copy(wqT[:, :], bank[1][:, 0:P])
            nc.scalar.copy(wkT[:, :], bank[1][:, P:2 * P])
            nc.scalar.copy(om2T[:, :], bank[1][:, 2 * P:3 * P]).then_inc(setup_used, 1)
            act_e.wait_ge(pe_setup, 3)
            for b in range(B):
                nc.scalar.copy(mod[:, b, 0, :], bank[2 + b][:, 0:P]).then_inc(sa_ready, 1)
            act_e.wait_ge(pe_setup, 4)
            for h in range(H):
                last = nc.scalar.activation(wproj[:, h:2 * H:H, :], bank[4 + 2 * h][:, 0:2 * M].rearrange(
                    "p (j m) -> p j m", m=M), ACT.Identity, scale=QK_SCALE)
            last.then_inc(setup_used, 1)
            act_e.wait_ge(silu_done, 1)
            nc.scalar.activation(warm[:, :], silu_c[:, :], ACT.Exp)

            def front_hT(ci):
                for b in range(B):
                    act_e.wait_ge(hT_tr, ci * B + b + 1)
                    nc.scalar.copy(hT[b][:, :], bA[b][:, 0:P]).then_inc(hT_ready, 1)

            def front_exp(ci):
                for b in range(B):
                    act_e.wait_ge(max_ready, ci * B + b + 1)
                    for j in range(2 * H):
                        a = nc.scalar.activation(feat[b][:, j, :], bB[b][:, j * M:(j + 1) * M], ACT.Exp,
                                                 bias=negmax[b][:, j:j + 1])
                    a.then_inc(feat_ready, 1)

            def front_v(ci):
                for b in range(B):
                    act_e.wait_ge(v_done, ci * B + b + 1)
                    nc.scalar.copy(vext[b][:, :, 0:DH],
                                   bD[b][:, 2 * P:3 * P].rearrange("p (h d) -> p h d", h=H)).then_inc(vext_ready, 1)

            def back(ci):
                for b in range(B):
                    act_e.wait_ge(oT_tr, ci * B + b + 1)
                    nc.scalar.copy(oT[b][:, :], bB[b][:, 0:P]).then_inc(oT_ready, 1)

            def front(ci):
                front_hT(ci)
                front_exp(ci)
                front_v(ci)

            front(0)
            front(1)
            with act_e.Fori(1, C - 1) as ci:
                back(ci - 1)
                front(ci + 1)
            back(C - 2)
            back(C - 1)

            act_e.wait_ge(pe_setup, 5)
            nc.scalar.copy(vecT[:, :], bA[0][:, 0:nv]).then_inc(vec_ready, 1)
            act_e.wait_ge(pe_setup, 6)
            for b in range(B):
                nc.scalar.copy(mod[:, b, 2:6, :], bD[b][:, :])
            nc.scalar.copy(ga_col[:, :], bA[1][:, 0:B]).then_inc(mod_copied, 1)
            act_e.wait_ge(pe_setup, 7)
            nc.scalar.copy(shgT[:, :], bC[0][:, 0:I])
            nc.scalar.copy(shuT[:, :], bC[0][:, I:2 * I])
            nc.scalar.copy(shdT[:, :, :], bC[1][:, 0:I]).then_inc(setup_used, 1)

            def h2T_copy(k, b):
                act_e.wait_ge(h2T_tr, k * B + b + 1)
                nc.scalar.activation(h2T[b][:, :], bA[b][:, :], ACT.Identity, bias=vecT[:, 1:2],
                                     scale=vecT[:, 0:1]).then_inc(h2T_ready, 1)

            def relu(k, b):
                if k == 0 and b == 1:
                    act_e.wait_ge(blanked, 16 * YB // YN)
                for j in range(0, HB, 2):
                    act_e.wait_ge(w1_done, (k * B + b) * HB + j + 1)
                    nc.scalar.activation(hid[b][:, j, :], [bB, bC, bD, bB][j][b][:, :], ACT.Relu,
                                         bias=vecT[:, 3 + j:4 + j]).then_inc(hid_a, 1)

            def o2T_copy(k, b):
                if k == 0 and b == 0:
                    act_e.wait_ge(mod_ready, 1)
                act_e.wait_ge(w2_done, k * B + b + 1)
                nc.scalar.activation(o2T[b][:, :], bA[b][:, :], ACT.Identity, bias=gab2[:, b:b + 1],
                                     scale=ga_col[:, b:b + 1]).then_inc(o2T_ready, 1)

            def h3T_copy(k, b):
                act_e.wait_ge(h3T_tr, k * B + b + 1)
                nc.scalar.copy(h3T[k][b][:, :], (bB if k else bC)[b][:, :]).then_inc(h3T_ready, 1)

            def sigmoid(k):
                act_e.wait_ge(logit_ready, k + 1)
                nc.scalar.activation(prob[:, :, :], logit[:, :, :], ACT.Sigmoid).then_inc(prob_ready, 1)

            def shared_silu(k, j):
                for b in range(B):
                    n = (k * IB + j) * B + b
                    act_e.wait_ge(g_done, n + 1)
                    if n >= B:
                        act_e.wait_ge(act_ready, n - B + 1)
                    nc.scalar.activation(sil[b], bA[b][:, :], ACT.Silu).then_inc(sil_ready, 1)

            both = range(B)
            [h2T_copy(0, b) for b in both]
            [relu(0, b) for b in both]
            [o2T_copy(0, b) for b in both]
            [h2T_copy(1, b) for b in both]
            [relu(1, b) for b in both]
            o2T_copy(1, 0)
            [h3T_copy(0, b) for b in both]
            sigmoid(0)
            o2T_copy(1, 1)
            shared_silu(0, 0)
            shared_silu(0, 1)
            [h3T_copy(1, b) for b in both]
            sigmoid(1)
            shared_silu(1, 0)
            shared_silu(1, 1)

            def xhi(n, m, turn):
                act_e.wait_ge(xT_tr, n + 1)
                nc.scalar.copy(xT[m][0][:, :], bank[XB[m]][:, 0:P]).then_inc(xhi_ready, 1)

            def silu(n, m):
                act_e.wait_ge(gu_done, n + 1)
                nc.scalar.activation(silt[m], bank[m][:, 0:I], ACT.Silu).then_inc(silt_ready, 1)

            def ahi(n, m):
                act_e.wait_ge(aT_tr, n + 1)
                nc.scalar.copy(aT[m][0][:, :, :], bank[3 + m][:, 0:IB * P]).then_inc(ahi_ready, 1)

            pipeline(act_e, xhi, silu, ahi, lambda n, m, turn: None)

            for q in range(TG, G * TT):
                k, t = divmod(q, TT)
                act_e.wait_ge(gathered[q], 32)
                nc.scalar.activation(got[0][:, q, :], got[0][:, q, :], ACT.Identity,
                                     scale=wts[:, k, 0, t:t + 1]).then_inc(weighted, 1)

        @block.vector
        def _(dve):
            V = nc.vector
            count = [0]

            def link(ins):
                ins.then_inc(dv, 1)
                count[0] += 1
                dve.wait_ge(dv, count[0])

            def moments(st, mn, vr, chain, u, v_, w):
                V.tensor_tensor(mn, st[:, :, :, 1], st[:, :, :, 4], ALU.add)
                V.tensor_tensor(u, st[:, :, :, 1], st[:, :, :, 4], ALU.subtract)
                chain(V.tensor_tensor(v_, st[:, :, :, 2], st[:, :, :, 5], ALU.add))
                V.tensor_scalar(mn, mn, 0.5, None, ALU.mult)
                chain(V.scalar_tensor_tensor(w, u, 0.25, u, ALU.mult, ALU.mult))
                chain(V.scalar_tensor_tensor(vr, v_, 1.0 / P, w, ALU.mult, ALU.add))

            def rsqrt(r, v_, eps, chain, u, w, t):
                chain(V.tensor_scalar(w, v_, eps, None, ALU.add))
                chain(V.tensor_scalar(u.bitcast(I32), w.bitcast(I32), 1, None, ALU.logical_shift_right))
                chain(V.tensor_scalar(r.bitcast(I32), u.bitcast(I32), -1.0, float(0x5F3759DF), ALU.mult, ALU.add))
                for _ in range(3):
                    chain(V.tensor_tensor(u, r, r, ALU.mult))
                    chain(V.scalar_tensor_tensor(t, u, -0.5, w, ALU.mult, ALU.mult))
                    chain(V.scalar_tensor_tensor(r, t, 1.5, r, ALU.add, ALU.mult))

            L = lambda t: t[:, :, :]
            V.memset(vext[0][:, :, DH:NV], 1.0)
            V.memset(vext[1][:, :, DH:NV], 1.0)
            V.memset(state[0][:, :, :], 0.0)
            V.memset(state[1][:, :, :], 0.0)
            for b in range(B):
                dve.wait_ge(x_in[b], 16)
                for ci in range(C):
                    V.bn_stats(stats[:, b, ci, :], x_all[:, b, ci, :]).then_inc(dv, 1)
                    count[0] += 1
            dve.wait_ge(dv, count[0])
            moments(stats, L(mean), L(var), link, L(lt[0]), L(lt[1]), L(lt[2]))
            rsqrt(L(rstd), L(var), LN_EPS, link, L(lt[0]), L(lt[1]), L(lt[2]))
            dve.wait_ge(sa_ready, B)
            for b in range(B):
                last = V.tensor_scalar(mod[:, b, 1, :], bank[2 + b][:, P:2 * P], 1.0, None, ALU.add)
            last.then_inc(ca_ready, 1)
            for ci in range(C):
                for b in range(B):
                    last = V.tensor_scalar(xn_all[:, b, ci, :], x_all[:, b, ci, :], mean[:, b, ci:ci + 1],
                                           rstd[:, b, ci:ci + 1], ALU.subtract, ALU.mult)
                last.then_inc(xn_ready, 1)

            def gates():
                dve.wait_ge(mod_copied, 1)
                dve.wait_ge(vec_ready, 1)
                V.tensor_scalar(mod[:, :, 4, :], mod[:, :, 4, :], 1.0, None, ALU.add)
                V.tensor_scalar(gsign[:, :, :], mod[:, :, 5, :], 0.0, 2.0, ALU.is_ge, ALU.mult)
                chain(V.scalar_tensor_tensor(ga_abs[:, :], ga_col[:, :], -1.0, ga_col[:, :], ALU.mult, ALU.max))
                V.tensor_scalar(ga_abs[:, :], ga_abs[:, :], 0.25, None, ALU.max)
                chain(V.tensor_scalar(ga_col[:, :], ga_col[:, :], 0.0, 2.0, ALU.is_ge, ALU.mult))
                chain(V.scalar_tensor_tensor(mod[:, :, 5, :], mod[:, :, 5, :], -1.0, mod[:, :, 5, :], ALU.mult,
                                             ALU.max))
                V.scalar_tensor_tensor(ga_col[:, :], ga_col[:, :], -1.0, ga_abs[:, :], ALU.add, ALU.mult)
                chain(V.tensor_scalar(mod[:, :, 5, :], mod[:, :, 5, :], 0.25, None, ALU.max))
                V.scalar_tensor_tensor(mod[:, :, 5, :], gsign[:, :, :], -1.0, mod[:, :, 5, :], ALU.add, ALU.mult)
                V.tensor_scalar(gab2[:, :], ga_col[:, :], vecT[:, 2:3], None, ALU.mult).then_inc(mod_ready, 1)

            def front_max(ci):
                for b in range(B):
                    dve.wait_ge(proj_done, ci * B + b + 1)
                    V.tensor_reduce(negmax[b][:, :], bB[b][:, :].rearrange("p (j m) -> p j m", m=M), AX.X,
                                    ALU.max, negate=True).then_inc(max_ready, 1)

            def back_feat(ci):
                for b in range(B):
                    dve.wait_ge(featT_tr, ci * B + b + 1)
                    V.tensor_scalar(featT[b][:, :, :], bC[b][:, :], INV_SQRT_M, FEAT_EPS, ALU.mult,
                                    ALU.add).then_inc(featT_ready, 1)
                    V.tensor_scalar(kfeat[b][:, :, :], feat[b][:, H:2 * H, :], INV_SQRT_M, FEAT_EPS, ALU.mult,
                                    ALU.add).then_inc(kfeat_ready, 1)

            def back_mask(ci):
                for b in range(B):
                    dve.wait_ge(att_done, ci * B + b + 1)
                    V.tensor_tensor(att[b][:, :, :], bD[b][:, 0:H * P], causal[:, :, :], ALU.mult)\
                        .then_inc(att_ready, 1)

            def back_out(ci):
                for b in range(B):
                    o = bA[b][:, 2 * P:2 * P + H * NV].rearrange("p (h n) -> p h n", h=H)
                    dve.wait_ge(o_done, ci * B + b + 1)
                    V.tensor_scalar(den[b][:, :], o[:, :, DH], FEAT_EPS, None, ALU.add).then_inc(den_ready, 1)
                    dve.wait_ge(den_ready, ci * B + b + 1)
                    V.reciprocal(rden[b][:, :], den[b][:, :]).then_inc(rden_ready, 1)
                    dve.wait_ge(st_done, ci * B + b + 1)
                    V.tensor_tensor(state[b][:, :, :], bC[b][:, 0:H * NV], state[b][:, :, :], ALU.add)
                    dve.wait_ge(rden_ready, ci * B + b + 1)
                    V.tensor_tensor(o_n[b][:, :, :], o[:, :, 0:DH],
                                    rden[b][:, :].unsqueeze(2).to_broadcast([P, H, DH]), ALU.mult)\
                        .then_inc(on_ready, 1)

            def back_y(ci):
                if isinstance(ci, int) and ci == C - 1:
                    dve.wait_ge(pl, 3 + C * 2 * B)
                for b in range(B):
                    dve.wait_ge(wo_done, ci * B + b + 1)
                    V.tensor_tensor(h_all[:, b, bass.ds(ci, 1), :], bB[b][:, P:2 * P],
                                    h_all[:, b, bass.ds(ci, 1), :], ALU.add).then_inc(y_ready, 1)

            def back_stats(ci):
                dve.wait_ge(y_ready, (ci + 1) * B)
                V.memset(lt[0][0:1, 0, 0:1], 0.0)
                for b in range(B):
                    V.bn_stats(stats[:, b, bass.ds(ci, 1), :], h_all[:, b, bass.ds(ci, 1), :]).then_inc(dv2, 1)

            front_max(0)
            back_feat(0)
            back_mask(0)
            front_max(1)
            back_out(0)
            with dve.Fori(1, C - 1) as ci:
                back_feat(ci)
                back_y(ci - 1)
                back_mask(ci)
                back_stats(ci - 1)
                front_max(ci + 1)
                back_out(ci)
            back_feat(C - 1)
            back_y(C - 2)
            back_mask(C - 1)
            back_stats(C - 2)
            back_out(C - 1)
            back_y(C - 1)
            back_stats(C - 1)
            dve.wait_ge(dv2, B * C)
            moments(stats, L(mean), L(var), link, L(lt[0]), L(lt[1]), L(lt[2]))
            rsqrt(L(rstd), L(var), ATTN_LN_EPS, link, L(lt[0]), L(lt[1]), L(lt[2]))

            count2 = [0]

            def chain(ins):
                ins.then_inc(dvc, 1)
                count2[0] += 1
                dve.wait_ge(dvc, count2[0])

            def normalise2(k):
                for b in range(B):
                    if k:
                        dve.wait_ge(h2T_tr, (k - 1) * B + b + 1)
                    for j in range(TG):
                        c_ = k * TG + j
                        last = V.tensor_scalar(yn[b][:, j, :], h_all[:, b, c_, :], mean[:, b, c_:c_ + 1],
                                               rstd[:, b, c_:c_ + 1], ALU.subtract, ALU.mult)
                    last.then_inc(yn_ready, 1)

            def relu(k):
                for b in range(B):
                    if k == 0 and b == 1:
                        dve.wait_ge(blanked, 16 * YB // YN)
                    for j in range(1, HB, 2):
                        dve.wait_ge(w1_done, (k * B + b) * HB + j + 1)
                        V.tensor_scalar(hid[b][:, j, :], [bB, bC, bD, bB][j][b][:, :], vecT[:, 3 + j:4 + j], 0.0,
                                        ALU.add, ALU.max).then_inc(hid_v, 1)

            def residual1(k):
                for b in range(B):
                    xs = x_all[:, b, k * TG:(k + 1) * TG, :]
                    dve.wait_ge(o2_tr, k * B + b + 1)
                    V.tensor_tensor(xs, bB[b][:, :].rearrange("p (t d) -> p t d", d=P), xs, ALU.add)\
                        .then_inc(x1_ready, 1)
                for b in range(B):
                    dve.wait_ge(x1_ready, k * B + b + 1)
                    for j in range(TG):
                        last = V.bn_stats(stats3[:, b, j, :], x_all[:, b, k * TG + j, :])
                chain(last)

            def moments3():
                moments(stats3, L(l3[0]), L(l3[1]), chain, L(l3[2]), L(l3[4]), L(l3[3]))
                rsqrt(L(l3[2]), L(l3[1]), LN_EPS, chain, L(l3[3]), L(l3[4]), L(l3[5]))

            def normalise3(k):
                for b in range(B):
                    for j in range(TG):
                        last = V.scalar_tensor_tensor(x1n[b][:, j, :], x_all[:, b, k * TG + j, :],
                                                      l3[0][:, b, j:j + 1], mod[:, b, 4, :], ALU.subtract, ALU.mult)
                    chain(last)
                    for j in range(TG):
                        last = V.scalar_tensor_tensor(h3[k][b][:, j, :], x1n[b][:, j, :], l3[2][:, b, j:j + 1],
                                                      mod[:, b, 3, :], ALU.mult, ALU.add)
                    last.then_inc(h3_ready, 1)

            def tiles(t):
                return t[:, :].unsqueeze(2).to_broadcast([P, TT, E])

            def experts(t):
                return t[:, :].unsqueeze(1).to_broadcast([P, TT, E])

            def first_of(p_ap, top_, onehot_):
                chain(V.tensor_reduce(top_[:, :], p_ap, AX.X, ALU.max))
                chain(V.tensor_tensor(L(hit), p_ap, tiles(top_), ALU.is_equal))
                chain(V.tensor_tensor(L(hit), L(hit), L(first8), ALU.mult))
                chain(V.tensor_reduce(hitmax[:, :], L(hit), AX.X, ALU.max))
                chain(V.tensor_tensor(L(onehot_), L(hit), tiles(hitmax), ALU.is_equal))

            def logits(k):
                dve.wait_ge(sh_in, 16 * 4)
                for b in range(B):
                    dve.wait_ge(logit_done, k * B + b + 1)
                    last = V.tensor_tensor(logit[:, b * TG:(b + 1) * TG, :],
                                           bD[b][:, 0:TG * E].rearrange("p (t e) -> p t e", e=E),
                                           rbias[:, :].unsqueeze(1).to_broadcast([P, TG, E]), ALU.add)
                last.then_inc(logit_ready, 1)

            def choose(k):
                dve.wait_ge(prob_ready, k + 1)
                first_of(L(prob), top[0], pick[0])
                chain(V.scalar_tensor_tensor(L(prob2), L(pick[0]), -2.0, L(prob), ALU.mult, ALU.add))
                first_of(L(prob2), top[1], pick[1])
                V.tensor_tensor(sel[:, 0:TT, :], L(pick[0]), L(pick[1]), ALU.add).then_inc(sel_ready, 1)
                chain(V.tensor_tensor(topsum[:, :], top[0][:, :], top[1][:, :], ALU.add))
                chain(V.reciprocal(topinv[:, :], topsum[:, :]))
                for i in range(2):
                    V.tensor_tensor(wts[:, k, i, :], top[i][:, :], topinv[:, :], ALU.mult)

            def place(k):
                dve.wait_ge(rank_done, k + 1)
                rk = bD[0][:, RK:RK + (TT + 1) * E].rearrange("p (t e) -> p t e", e=E)
                chain(V.tensor_tensor(L(slotf), rk[:, 0:TT, :], experts(cbase), ALU.add))
                for i in range(2):
                    chain(V.tensor_tensor(L(slotp), L(pick[i]), L(slotf), ALU.mult))
                    chain(V.tensor_reduce(rowf[:, i, :], L(slotp), AX.X, ALU.add))
                V.tensor_tensor(cum[:, k * TT:(k + 1) * TT, :], rk[:, 1:TT + 1, :], experts(cnt), ALU.add)
                chain(V.tensor_tensor(cbase[:, :], cbase[:, :], rk[:, TT, :], ALU.add))
                chain(V.tensor_tensor(cnt[:, :], cnt[:, :], rk[:, TT, :], ALU.add))
                V.tensor_copy(rows[:, k, :, :], rowf[:, :, :]).then_inc(rows_ready, 1)
                if k:
                    V.tensor_copy(pad_row[:, :], cbase[0:1, :]).then_inc(pad_ready, 1)

            def schedule():
                chain(V.tensor_tensor(cq[:, :, :], cum[:, :, :],
                                      emask[:, :].unsqueeze(1).to_broadcast([P, G * TT, E]), ALU.mult))
                chain(V.tensor_reduce(cumc[:, :], cq[:, :, :], AX.X, ALU.add))
                chain(V.tensor_scalar(notyet[:, :], cumc[:, :], cstart[:, :], None, ALU.is_le))
                chain(V.tensor_reduce(since[:, :], notyet[:, :], AX.X, ALU.add))
                V.tensor_scalar(diag[:, :], ident[:, :], since[:, :], None, ALU.mult).then_inc(cv_ready, 1)
                V.tensor_scalar(cvalid[:, :], since[:, :], float(G * TT), None, ALU.is_lt)
                V.scalar_tensor_tensor(key[:, :], since[:, :], float(P), cf[:, :], ALU.mult, ALU.add)
                V.tensor_scalar(needed[:, :], iota_p[:, 0:G * TT], since[:, :], None, ALU.is_ge)
                chain(V.tensor_tensor(cend[:, :], ctop[:, :], cumc[:, G * TT - 1:G * TT], ALU.min))
                chain(V.tensor_tensor(cvals[:, 2:3], cend[:, :], cumc[:, TT - 1:TT], ALU.is_gt))
                shared_mul(1, 0)
                dve.wait_ge(cpos_done, 1)
                chain(V.scalar_tensor_tensor(keys[:, :], bD[0][:, KC:KC + P], float(P), iota_p[:, :], ALU.mult,
                                             ALU.add))
                chain(V.tensor_scalar(keys[:, :], keys[:, :], key[:, :], None, ALU.is_lt))
                chain(V.tensor_reduce(cpos[:, :], keys[:, :], AX.X, ALU.add))
                V.tensor_scalar(onehot[:, :], iota_p[:, 0:NT], cpos[:, :], cvalid[:, :], ALU.is_equal,
                                ALU.mult).then_inc(onehot_ready, 1)
                shared_out(0, 0)
                dve.wait_ge(tab_done, 1)

                def pack(w, vals, base):
                    v = vals.rearrange("a (i m) -> a i m", m=NBUF)
                    chain(V.scalar_tensor_tensor(w[:, :], v[:, :, 2], float(base), v[:, :, 1], ALU.mult, ALU.add))
                    chain(V.scalar_tensor_tensor(w[:, :], w[:, :], float(base), v[:, :, 0], ALU.mult, ALU.add))

                nturns = NT // NBUF
                chain(V.tensor_reduce(late[:, :], bD[0][0:1, SC + 1 + 2 * NT:SC + 1 + 3 * NT].rearrange(
                    "a (i m) -> a i m", m=NBUF), AX.X, ALU.max))
                chain(V.tensor_scalar(tile_blk[:, 0:NT], bD[0][0:1, SC + 1 + NT:SC + 1 + 2 * NT], float(E * RB), None,
                                      ALU.add))
                pack(packed[1], tile_blk[:, :], BW)
                V.scalar_tensor_tensor(first_rows[:, :], late[:, 0:2], float(BW ** NBUF), packed[1][:, 0:2],
                                       ALU.mult, ALU.add).then_inc(row_ready, 1)
                V.scalar_tensor_tensor(tile_rows[:, 0:nturns - 2, 0], late[:, 2:nturns], float(BW ** NBUF),
                                       packed[1][:, 2:nturns], ALU.mult, ALU.add)
                chain(V.tensor_copy(spare[:, :], bD[0][0:1, SC + 1:SC + 1 + NT]))
                pack(packed[0], spare[:, :], E)
                V.scalar_tensor_tensor(tile_e[:, 0:nturns - 1], packed[0][:, 1:nturns], float(E ** NBUF),
                                       packed[0][:, 0:nturns - 1], ALU.mult, ALU.add)
                V.tensor_copy(tile_e[:, nturns - 1:nturns], packed[0][:, nturns - 1:nturns]).then_inc(tab_ready, 1)
                shared_mul(1, 1)
                shared_out(0, 1)
                chain(V.tensor_scalar(spare[:, :], tile_blk[:, :], float(E * RB), None, ALU.is_equal))
                chain(V.tensor_tensor(spare[:, :], spare[:, :], ntail[:, :], ALU.mult))
                chain(V.tensor_tensor(spare[:, :], spare[:, :], tile_blk[:, :], ALU.add))
                pack(packed[2], spare[:, :], BW)
                V.tensor_copy(tile_rows[:, :, 1], packed[2][:, :]).then_inc(out_ready, 1)
                V.tensor_copy(req[:, :], bD[0][0:1, RQ:RQ + G * TT]).then_inc(req_ready, 1)
                shared_out(1, 0)
                shared_out(1, 1)

            def shared_mul(k, j):
                for b in range(B):
                    n = (k * IB + j) * B + b
                    dve.wait_ge(sil_ready, n + 1)
                    V.tensor_tensor(act[b][:, j, :], bC[b][:, :], sil[b], ALU.mult).then_inc(act_ready, 1)

            def shared_out(k, b):
                dve.wait_ge(ysh_done, k * B + b + 1)
                xs = x_all[:, b, k * TG:(k + 1) * TG, :]
                V.tensor_tensor(comb[:, :, :], bB[b][:, :].rearrange("p (t d) -> p t d", d=P),
                                mod[:, b, 5, :].unsqueeze(1).to_broadcast([P, TG, P]), ALU.mult)\
                    .then_inc(base_ready, 1)
                dve.wait_ge(base_ready, k * B + b + 1)
                chain(V.tensor_tensor(xs, comb[:, :, :], xs, ALU.add))

            normalise2(0)
            gates()
            relu(0)
            normalise2(1)
            V.tensor_scalar(ntail[:, :], iota_p[0:1, 0:NT], float(2 * T // P), 0.0, ALU.subtract, ALU.max)
            chain(V.tensor_scalar(cki[:, :], cand[:, :], E_BITS, None, ALU.logical_shift_right))
            V.tensor_copy(cf[:, :], cand[:, :])
            chain(V.tensor_copy(ck[:, :], cki[:, :]))
            chain(V.scalar_tensor_tensor(ce[:, :], ck[:, :], -float(E), cf[:, :], ALU.mult, ALU.add))
            V.tensor_scalar(cstart[:, :], ck[:, :], float(P), None, ALU.mult)
            V.tensor_scalar(ctop[:, :], ck[:, :], float(P), float(P), ALU.mult, ALU.add)
            V.tensor_scalar(emask[:, :], iota_e[:, :], ce[:, :], None, ALU.is_equal)
            V.tensor_copy(cvals[:, 0:1], ce[:, :])
            chain(V.scalar_tensor_tensor(cpos[:, :], ce[:, :], float(RB), ck[:, :], ALU.mult, ALU.add))
            chain(V.tensor_scalar(cvals[:, 1:2], cpos[:, :], -float(E * RB), None, ALU.add))
            V.memset(tile_rows[:, :, :], 0)
            residual1(0)
            moments3()
            relu(1)
            normalise3(0)
            logits(0)
            choose(0)
            place(0)
            residual1(1)
            shared_mul(0, 0)
            moments3()
            normalise3(1)
            shared_mul(0, 1)
            logits(1)
            choose(1)
            place(1)
            schedule()

            def xlo(n, m, turn):
                dve.wait_ge(xhi_ready, n + 1)
                V.tensor_tensor(xT[m][1][:, :], bank[XB[m]][:, 0:P], xT[m][0][:, :].bitcast(F32),
                                ALU.subtract).then_inc(xlo_ready, 1)

            def mul(n, m):
                dve.wait_ge(silt_ready, n + 1)
                V.tensor_tensor(actt[m], bank[m][:, I:2 * I], silt[m], ALU.mult)\
                    .then_inc(actt_ready, 1)

            def alo(n, m):
                dve.wait_ge(ahi_ready, n + 1)
                V.tensor_tensor(aT[m][1][:, :, :], bank[3 + m][:, 0:IB * P].rearrange("p (j n) -> p j n", n=P),
                                aT[m][0][:, :, :].bitcast(F32), ALU.subtract).then_inc(alo_ready, 1)

            def yout(n, m, turn):
                dve.wait_ge(yt_done, n + 1)
                dve.wait_ge(yt_out[m], turn * 16 + 16)
                V.tensor_reduce(yt[m], bank[3 + m][:, IB * P:(IB + 2) * P].rearrange("p (w n) -> p n w", w=2),
                                AX.X, ALU.add).then_inc(yt_ready, 1)

            pipeline(dve, xlo, mul, alo, yout)

            for i, (u, t0, t1) in enumerate(pieces):
                k, b = divmod(u, B)
                mix = yn[i % 2]
                row = mod[:, b, 5, :].unsqueeze(1).to_broadcast([P, t1 - t0, P])
                if u == 0:
                    for q in range(TG):
                        dve.wait_ge(gathered[q], 32)
                        last = V.tensor_scalar(got[0][:, q, :], got[0][:, q, :], wts[:, 0, 0, q:q + 1], None,
                                               ALU.mult)
                    chain(last)
                for t in range(t0, t1):
                    q = u * TG + t
                    dve.wait_ge(gathered[q], 32)
                    if u:
                        dve.wait_ge(weighted, q - TG + 1)
                    last = V.scalar_tensor_tensor(mix[:, t, :], got[1][:, q, :],
                                                  wts[:, k, 1, b * TG + t:b * TG + t + 1], got[0][:, q, :],
                                                  ALU.mult, ALU.add)
                chain(last)
                chain(V.tensor_tensor(mix[:, t0:t1, :], mix[:, t0:t1, :], row, ALU.mult))
                V.tensor_tensor(h_all[:, b, k * TG + t0:k * TG + t1, :], mix[:, t0:t1, :],
                                x_all[:, b, k * TG + t0:k * TG + t1, :], ALU.add).then_inc(fin_ready, 1)
                if i:
                    dve.wait_ge(fin_ready, i)

        @block.tensor
        def _(pe):
            def mm(o, lhsT, rhs, start=True, stop=True):
                return nc.tensor.matmul(o, lhsT, rhs, start=start, stop=stop)

            pe.wait_ge(consts, 1)
            pe.wait_ge(c_in, 16)
            nc.tensor.transpose(bank[0][:, 0:B], c_rows[:, :], ident[0:B, 0:B]).then_inc(pe_setup, 1)
            pe.wait_ge(qk_in, 16 * 4)
            nc.tensor.transpose(bank[1][:, 0:P], wq_sb[:, :], ident[:, :])
            nc.tensor.transpose(bank[1][:, P:2 * P], wk_sb[:, :], ident[:, :])
            nc.tensor.transpose(bank[1][:, 2 * P:3 * P], om2[:, :, :].rearrange("p a d -> p (a d)"),
                                ident[:, :]).then_inc(pe_setup, 1)
            pe.wait_ge(mod_in, 16)
            pe.wait_ge(silu_bc_done, 1)
            for b in range(B):
                last = mm(bank[2 + b][:, 0:2 * P], silu_bc[:, b, :], wmod_sb[:, 0:2 * P])
            last.then_inc(pe_setup, 1)
            pe.wait_ge(setup_used, 1)
            for i, (w, h) in enumerate([(wqT, 0), (wqT, 1), (wkT, 0), (wkT, 1)]):
                last = mm(bank[4 + 2 * h][:, (i // H) * M:(i // H + 1) * M], w[h * DH:(h + 1) * DH, :],
                          om2T[h * DH:(h + 1) * DH, :])
            last.then_inc(pe_setup, 1)
            pe.wait_ge(setup_used, 2)

            def late_setup():
                pe.wait_ge(vec_in, 16 * 5)
                nc.tensor.transpose(bA[0][:, 0:nv], vec_rows[:, :], ident[0:nv, 0:nv]).then_inc(pe_setup, 1)
                pe.wait_ge(mod_rest_in, 16)
                for b in range(B):
                    mm(bD[b][:, :], silu_bc[:, b, :], wmod_sb[:, 2 * P:6 * P])
                mm(bA[1][:, 0:B], wmod_sb[:, 2 * P:3 * P], silu_c[:, :]).then_inc(pe_setup, 1)
                pe.wait_ge(sh_in, 16 * 4)
                for j in range(IB):
                    nc.tensor.transpose(bC[0][:, j * P:(j + 1) * P], shg_sb[:, j, :], ident[:, :])
                    nc.tensor.transpose(bC[0][:, I + j * P:I + (j + 1) * P], shu_sb[:, j, :], ident[:, :])
                for j in range(IB):
                    last = nc.tensor.transpose(bC[1][:, j * P:(j + 1) * P], shd_sb[:, j, :], ident[:, :])
                last.then_inc(pe_setup, 1)

            def front_tr(ci):
                for b in range(B):
                    pe.wait_ge(h_staged, ci * B + b + 1)
                    nc.tensor.transpose(bA[b][:, 0:P], hst[b][:, :], ident[:, :]).then_inc(hT_tr, 1)

            def front_proj(ci):
                for b in range(B):
                    pe.wait_ge(hT_ready, ci * B + b + 1)
                    if not isinstance(ci, int) or ci > 1:
                        pe.wait_ge(y_ready, (ci - 2) * B + b + 1)
                    mm(bB[b][:, :], hT[b][:, :], wproj[:, :, :]).then_inc(proj_done, 1)

            def front_v(ci):
                for b in range(B):
                    mm(bD[b][:, 2 * P:3 * P], hT[b][:, :], wv_sb[:, :]).then_inc(v_done, 1)

            def back_tr(ci, first=False, last=False):
                for b in range(B):
                    if not last:
                        pe.wait_ge(feat_ready, ci * B + b + 1)
                    if not first:
                        pe.wait_ge(on_ready, (ci - 1) * B + b + 1)
                        nc.tensor.transpose(bB[b][:, 0:P], o_n[b][:, :, :].rearrange("p h d -> p (h d)"),
                                            ident[:, :]).then_inc(oT_tr, 1)
                    if not last:
                        for j in range(2 * H):
                            tr = nc.tensor.transpose(bC[b][:, j * P:(j + 1) * P], feat[b][:, j, :], ident[:, :])
                        tr.then_inc(featT_tr, 1)

            def back_att(ci):
                for b in range(B):
                    pe.wait_ge(featT_ready, ci * B + b + 1)
                    pe.wait_ge(vext_ready, ci * B + b + 1)
                    for h in range(H):
                        last = mm(bD[b][:, h * P:(h + 1) * P], featT[b][:, H + h, :], featT[b][:, h, :])
                    last.then_inc(att_done, 1)

            def back_o(ci):
                for b in range(B):
                    pe.wait_ge(att_ready, ci * B + b + 1)
                    pe.wait_ge(kfeat_ready, ci * B + b + 1)
                    for h in range(H):
                        o = bA[b][:, 2 * P + h * NV:2 * P + (h + 1) * NV]
                        mm(o, featT[b][:, h, :], state[b][:, h, :], stop=False)
                        last = mm(o, att[b][:, h, :], vext[b][:, h, :], start=False)
                    last.then_inc(o_done, 1)
                    for h in range(H):
                        last = mm(bC[b][:, h * NV:(h + 1) * NV], kfeat[b][:, h, :], vext[b][:, h, :])
                    last.then_inc(st_done, 1)

            def back_wo(ci):
                for b in range(B):
                    pe.wait_ge(oT_ready, ci * B + b + 1)
                    mm(bB[b][:, P:2 * P], oT[b][:, :], wo_sb[:, :]).then_inc(wo_done, 1)

            def step(ci, first=False):
                back_tr(ci, first)
                front_tr(ci + 1)
                if not first:
                    back_wo(ci - 1)
                back_att(ci)
                front_proj(ci + 1)
                back_o(ci)
                front_v(ci + 1)

            front_tr(0)
            front_proj(0)
            pe.wait_ge(vo_in, 32)
            front_v(0)
            step(0, first=True)
            with pe.Fori(1, C - 1) as ci:
                step(ci)
            back_tr(C - 1)
            back_wo(C - 2)
            back_att(C - 1)
            back_o(C - 1)
            back_tr(C, last=True)
            back_wo(C - 1)
            late_setup()
            pe.wait_ge(setup_used, 3)

            def tr_yn(k, b):
                pe.wait_ge(yn_ready, k * B + b + 1)
                for j in range(TG):
                    last = nc.tensor.transpose(bA[b][:, j * P:(j + 1) * P], yn[b][:, j, :], ident[:, :])
                last.then_inc(h2T_tr, 1)

            def ffn1(k, b):
                pe.wait_ge(h2T_ready, k * B + b + 1)
                if k:
                    pe.wait_ge(x1_ready, (k - 1) * B + b + 1)
                for j in range(HB):
                    if j == 3:
                        pe.wait_ge(hid_a, (k * B + b) * (HB // 2) + 1)
                    mm([bB, bC, bD, bB][j][b][:, :], w1_sb[:, j, :], h2T[b][:, :]).then_inc(w1_done, 1)

            def ffn2(k, b):
                pe.wait_ge(hid_a, (k * B + b + 1) * (HB // 2))
                pe.wait_ge(hid_v, (k * B + b + 1) * (HB // 2))
                for j in range(HB):
                    last = mm(bA[b][:, :], w2_sb[:, j, :], hid[b][:, j, :], start=j == 0, stop=j == HB - 1)
                last.then_inc(w2_done, 1)

            def tr_o2(k, b):
                pe.wait_ge(o2T_ready, k * B + b + 1)
                for j in range(TG):
                    last = nc.tensor.transpose(bB[b][:, j * P:(j + 1) * P], o2T[b][:, j * P:(j + 1) * P],
                                               ident[:, :])
                last.then_inc(o2_tr, 1)

            def tr_h3(k, b):
                pe.wait_ge(h3_ready, k * B + b + 1)
                for j in range(TG):
                    last = nc.tensor.transpose((bB if k else bC)[b][:, j * P:(j + 1) * P], h3[k][b][:, j, :],
                                               ident[:, :])
                last.then_inc(h3T_tr, 1)

            def router(k, b):
                pe.wait_ge(h3T_ready, k * B + b + 1)
                for j in range(TG):
                    last = mm(bD[b][:, j * E:(j + 1) * E], h3T[k][b][:, j * P:(j + 1) * P],
                              vecT[:, 3 + HB:3 + HB + E])
                last.then_inc(logit_done, 1)

            def ranks(k):
                pe.wait_ge(sel_ready, k + 1)
                rk = bD[0][:, RK:RK + (TT + 1) * E]
                mm(rk, tri[:, :], sel[:, :, :], stop=False)
                for t in range(TT):
                    last = mm(rk[:, (t + 1) * E:], ones[:, :],
                              sel[:, t, :].unsqueeze(1).to_broadcast([P, TT - t, E]), start=False, stop=t == TT - 1)
                last.then_inc(rank_done, 1)

            def shared_gu(k, b, j):
                n = (k * IB + j) * B + b
                if j:
                    pe.wait_ge(act_ready, n - B + 1)
                mm(bA[b][:, :], shgT[:, j * P:(j + 1) * P], h3T[k][b][:, :])
                mm(bC[b][:, :], shuT[:, j * P:(j + 1) * P], h3T[k][b][:, :]).then_inc(g_done, 1)

            def shared_down(k, b):
                pe.wait_ge(act_ready, (k * IB + IB - 1) * B + b + 1)
                for t in range(TG):
                    for j in range(IB):
                        last = mm(bB[b][:, t * P:(t + 1) * P], act[b][:, j, t * P:(t + 1) * P], shdT[:, j, :],
                                  start=j == 0, stop=j == IB - 1)
                last.then_inc(ysh_done, 1)

            pe.wait_ge(ffn_in, 32)
            both = range(B)
            [tr_yn(0, b) for b in both]
            [ffn1(0, b) for b in both]
            [ffn2(0, b) for b in both]
            [tr_o2(0, b) for b in both]
            [tr_yn(1, b) for b in both]
            [ffn1(1, b) for b in both]
            ffn2(1, 0)
            pe.wait_ge(hid_a, 2 * B * HB // 2)
            pe.wait_ge(hid_v, 2 * B * HB // 2)
            [tr_h3(0, b) for b in both]
            [router(0, b) for b in both]
            ffn2(1, 1)
            tr_o2(1, 0)
            pe.wait_ge(zeros_ready, 1)
            ranks(0)
            tr_o2(1, 1)
            [shared_gu(0, b, 0) for b in both]
            [shared_gu(0, b, 1) for b in both]
            pe.wait_ge(x1_ready, 2 * B)
            [tr_h3(1, b) for b in both]
            pe.wait_ge(rows_ready, 1)
            [router(1, b) for b in both]
            [shared_down(0, b) for b in both]
            ranks(1)
            [shared_gu(1, b, 0) for b in both]
            pe.wait_ge(cv_ready, 1)
            mm(bD[0][:, KC:KC + P], ones[:, :], diag[:, :]).then_inc(cpos_done, 1)
            shared_gu(1, 0, 1)
            pe.wait_ge(onehot_ready, 1)
            mm(bD[0][0:1, SC + 1:SC + 1 + NT], cvals[:, 0:1], onehot[:, :])
            mm(bD[0][0:1, RQ:RQ + G * TT], ones[:, 0:1], needed[:, :])
            mm(bD[0][0:1, SC + 1 + NT:SC + 1 + 2 * NT], cvals[:, 1:2], onehot[:, :])
            mm(bD[0][0:1, SC + 1 + 2 * NT:SC + 1 + 3 * NT], cvals[:, 2:3], onehot[:, :]).then_inc(tab_done, 1)
            shared_gu(1, 1, 1)
            for b in both:
                pe.wait_ge(base_ready, b + 1)
                shared_down(1, b)

            def tile_experts(i, turns=1):
                w = nc.values_load_multi_w_load_instructions(
                    tile_e[0:1, bass.ds(i, turns)], engines=[mybir.EngineType.PE], min_val=0,
                    max_val=E ** (2 * NBUF) - 1)[1]
                return [[(w[t] // E ** j) % E for j in range(2 * NBUF)] for t in range(turns)]

            def tr_x(n, m, turn):
                pe.wait_ge(xt_in[m], turn * 16 + 16)
                if m == 2:
                    pe.wait_ge(xlo_ready, n - 1)
                elif m == 0 and not (isinstance(n, int) and n == 0):
                    pe.wait_ge(xlo_ready, n)
                nc.tensor.transpose(bank[XB[m]][:, 0:P], xt[m], ident[:, :]).then_inc(xT_tr, 1)

            def gate_up(n, m, e):
                pe.wait_ge(xlo_ready, n + 1)
                mm(bank[m][:, :], xT[m][0][:, :], wgu[0][:, bass.ds(e, 1), :], stop=False)
                mm(bank[m][:, :], xT[m][0][:, :], wgu[1][:, bass.ds(e, 1), :], start=False, stop=False)
                mm(bank[m][:, :], xT[m][1][:, :], wgu[0][:, bass.ds(e, 1), :], start=False).then_inc(gu_done, 1)

            def tr_a(n, m):
                pe.wait_ge(actt_ready, n + 1)
                if not isinstance(n, int) or n >= NBUF:
                    pe.wait_ge(yt_ready, n - 1)
                for j in range(IB):
                    last = nc.tensor.transpose(bank[3 + m][:, j * P:(j + 1) * P], actt[m][:, j * P:(j + 1) * P],
                                               ident[:, :])
                last.then_inc(aT_tr, 1)

            def down(n, m, e):
                pe.wait_ge(alo_ready, n + 1)
                y = bank[3 + m][:, IB * P:(IB + 2) * P]
                mm(y, aT[m][0][:, 0, :], wdn_parts[:, bass.ds(e, 1), :, 0:P], stop=False)
                for j in range(IB):
                    mm(y[:, 0:P], aT[m][1][:, j, :], wdn[0][:, bass.ds(e, 1), j * P:(j + 1) * P], start=False,
                       stop=False)
                mm(y, aT[m][0][:, 1, :], wdn_parts[:, bass.ds(e, 1), :, P:2 * P], start=False).then_inc(yt_done, 1)

            pe.wait_ge(base_ready, 2 * B)
            pe.wait_ge(tab_ready, 1)
            pe.wait_ge(wsplit, 6 * E)
            e, = tile_experts(0)
            tr_x(0, 0, 0)
            tr_x(1, 1, 0), gate_up(0, 0, e[0])
            tr_x(2, 2, 0), gate_up(1, 1, e[1]), tr_a(0, 0)
            tr_x(3, 0, 1), gate_up(2, 2, e[2]), tr_a(1, 1)

            def turn(i, e, last=False):
                n = i * NBUF
                down(n, 0, e[0])
                tr_x(n + 4, 1, i + 1), gate_up(n + 3, 0, e[3]), tr_a(n + 2, 2), down(n + 1, 1, e[1])
                tr_x(n + 5, 2, i + 1), gate_up(n + 4, 1, e[4]), tr_a(n + 3, 0), down(n + 2, 2, e[2])
                if not last:
                    tr_x(n + 6, 0, i + 2)
                gate_up(n + 5, 2, e[5]), tr_a(n + 4, 1)

            turns = NT // NBUF
            with pe.Fori(0, (turns - 2) // 2) as i2:
                e0, e1 = tile_experts(i2 * 2, 2)
                turn(i2 * 2, e0)
                turn(i2 * 2 + 1, e1)
            for i in range((turns - 2) // 2 * 2, turns - 2):
                turn(i, *tile_experts(i))
            turn(turns - 2, *tile_experts(turns - 2), last=True)
            n, (e,) = NT - NBUF, tile_experts(turns - 1)
            down(n, 0, e[0])
            tr_a(n + 2, 2), down(n + 1, 1, e[1])
            down(n + 2, 2, e[2])


_INS = ["L0_attn_batch", "L0_attn_Wq", "L0_attn_Wk", "L0_attn_Wv", "L0_attn_Wo", "L0_attn_omega", "L0_attn_W1",
        "L0_attn_b1", "L0_attn_W2", "L0_attn_b2", "L0_attn_gamma", "L0_attn_beta", "L0_ffn_shared_gate",
        "L0_ffn_shared_up", "L0_ffn_shared_down", "L0_ffn_gate_w", "L0_ffn_up_w", "L0_ffn_down_w",
        "L0_ffn_router_w", "L0_ffn_routing_bias", "L0_c", "L0_wmod"]


def kernel(**inputs):
    import numpy as _np
    import concourse.bacc as _bacc
    from concourse import mybir as _mybir
    from concourse.bass_utils import run_bass_kernel_spmd as _run

    nc = _bacc.Bacc("TRN2", target_bir_lowering=False, num_devices=1)
    arrays, args = {}, []
    for name in _INS:
        a = _np.ascontiguousarray(inputs[name])
        arrays[f"in_{name}"] = a
        args.append(nc.dram_tensor(f"in_{name}", a.shape, _mybir.dt.from_np(a.dtype), kind="ExternalInput").ap())
    out = nc.dram_tensor("out", inputs["L0_attn_batch"].shape, _mybir.dt.float32, kind="ExternalOutput").ap()
    rows = 8 * (2 * 1024 + 128) + 8 * 128
    xdisp = nc.dram_tensor("xdisp", [rows, 128], _mybir.dt.float32, kind="Internal").ap()
    ydisp = nc.dram_tensor("ydisp", [rows, 128], _mybir.dt.float32, kind="Internal").ap()
    adaln_block(nc, xdisp, ydisp, *args, out)
    r = _run(nc, [arrays], core_ids=[0])
    return r.results[0]["out"]
```
